# Optimizing a Trainium2 kernel written in Bass

```python
import numpy as np
import jax
import jax.numpy as jnp

def _softmax(x, axis=-1):
    return jax.nn.softmax(x, axis=axis)

def _gelu(x):
    return jax.nn.gelu(x, approximate=True)

def _silu(x):
    return jax.nn.silu(x)

def _sigmoid(x):
    return jax.nn.sigmoid(x)

def _layernorm(x, axis=-1, eps=1e-05):
    m = jnp.mean(x, axis=axis, keepdims=True)
    v = jnp.var(x, axis=axis, keepdims=True)
    return (x - m) / jnp.sqrt(v + eps)

def _scatter_add(tgt, idx, src, axis=0):
    return tgt.at[idx].add(src)

def _segment_sum(src, seg, n):
    return jax.ops.segment_sum(src, seg, n)
kernel_name = 'mk_gnn_ffn_d1_gnn_r8_de1b23'

def setup_inputs(seed: int=0):
    np.random.seed(seed)
    _w = jnp.asarray

    def _rec_inputs():
        import jax
        import jax.numpy as jnp
        _gk = jax.random.key(seed)
        x = -0.0003713 + 1 * jax.random.normal(jax.random.fold_in(_gk, 1), (6250, 256), jnp.float32)
        _s = jax.random.randint(jax.random.fold_in(_gk, 2), (50000,), 0, 6250, jnp.int32)
        _d = jax.random.randint(jax.random.fold_in(_gk, 3), (50000,), 0, 6250, jnp.int32)
        _loop = jnp.arange(6250, dtype=jnp.int32)
        src = jnp.concatenate([_s, _d, _loop])
        dst = jnp.concatenate([_d, _s, _loop])
        _o = jnp.argsort(dst, stable=True)
        src = src[_o]
        dst = dst[_o]
        edge_weight = jax.random.uniform(jax.random.fold_in(_gk, 12), (106250,), jnp.float32, 0.0, 0.999998)
        return (x, src, dst, edge_weight)
    x, src, dst, edge_weight = _rec_inputs()

    def _L0_gnn_setup():
        import jax, jax.numpy as jnp
        import numpy as np
        THR_A = 0.1
        THR_W = 0.1
        N, M, F_IN, F_OUT = (6250, 50000, 256, 256)
        key = jax.random.key(seed)
        k1, k2, k3, k4, k5, k6 = jax.random.split(key, 6)
        x = jax.random.normal(k1, (N, F_IN), dtype=jnp.float32)
        edge_index = jax.random.randint(k2, (2, M), 0, N, dtype=jnp.int64)
        edge_weight = jax.random.uniform(k3, (M,), dtype=jnp.float32)
        node_lock = jax.random.randint(k4, (1000,), 0, N, dtype=jnp.int64)
        W = jax.random.normal(k5, (F_OUT, F_IN), dtype=jnp.float32) / np.sqrt(F_IN)
        b = jax.random.normal(k6, (F_OUT,), dtype=jnp.float32) * 0.01
        return {'x': x, 'edge_index': edge_index, 'edge_weight': edge_weight, 'node_lock': node_lock, 'W': W, 'b': b}
    _L0_gnn_all = _L0_gnn_setup()
    _L0_gnn_in = {k: v for k, v in _L0_gnn_all.items() if k in ('node_lock', 'W', 'b')}
    del _L0_gnn_all

    def _L0_ffn_setup():
        import jax, jax.numpy as jnp
        import numpy as np
        E = 8
        K = 2
        D = 256
        H = 512
        DOUT = 256
        EPS = 1e-05
        key = jax.random.key(seed)
        ks = jax.random.split(key, 9)
        s = 0.02
        return {'x': jax.random.normal(ks[0], (4, 1024, D), jnp.float32), 'gamma': 1.0 + 0.05 * jax.random.normal(ks[1], (D,), jnp.float32), 'beta': 0.05 * jax.random.normal(ks[2], (D,), jnp.float32), 'Wr': 0.01 * jax.random.normal(ks[3], (D, E), jnp.float32), 'br': jnp.zeros((E,), jnp.float32), 'W1': s * jax.random.normal(ks[4], (E, D, H), jnp.float32), 'b1': s * jax.random.normal(ks[5], (E, H), jnp.float32), 'W2': s * jax.random.normal(ks[6], (E, H, DOUT), jnp.float32), 'b2': s * jax.random.normal(ks[7], (E, DOUT), jnp.float32)}
    _L0_ffn_all = _L0_ffn_setup()
    _L0_ffn_in = {k: v for k, v in _L0_ffn_all.items() if k in ('gamma', 'beta', 'Wr', 'br', 'W1', 'b1', 'W2', 'b2')}
    del _L0_ffn_all
    return {'x': x, 'src': src, 'dst': dst, 'edge_weight': edge_weight, 'L0_gnn_node_lock': _L0_gnn_in['node_lock'], 'L0_gnn_W': _L0_gnn_in['W'], 'L0_gnn_b': _L0_gnn_in['b'], 'L0_ffn_gamma': _L0_ffn_in['gamma'], 'L0_ffn_beta': _L0_ffn_in['beta'], 'L0_ffn_Wr': _L0_ffn_in['Wr'], 'L0_ffn_br': _L0_ffn_in['br'], 'L0_ffn_W1': _L0_ffn_in['W1'], 'L0_ffn_b1': _L0_ffn_in['b1'], 'L0_ffn_W2': _L0_ffn_in['W2'], 'L0_ffn_b2': _L0_ffn_in['b2']}

def reference(x, src, dst, edge_weight, L0_gnn_node_lock, L0_gnn_W, L0_gnn_b, L0_ffn_gamma, L0_ffn_beta, L0_ffn_Wr, L0_ffn_br, L0_ffn_W1, L0_ffn_b1, L0_ffn_W2, L0_ffn_b2):
    import jax
    import jax.numpy as jnp

    def _L0_gnn_ref(x, edge_index, edge_weight, node_lock, W, b):
        import jax, jax.numpy as jnp
        import numpy as np
        THR_A = 0.1
        THR_W = 0.1
        N, M, F_IN, F_OUT = (6250, 50000, 256, 256)
        n, f_in = x.shape
        norm_node_in = jnp.linalg.norm(x, axis=0)
        norm_all_in = jnp.linalg.norm(norm_node_in) / f_in
        thr_wi = THR_W * norm_all_in / norm_node_in
        W_pruned = jnp.where(jnp.abs(W) < thr_wi[None, :], 0.0, W)
        W_eff = jnp.where(norm_all_in > 1e-08, W_pruned, W)
        h = x @ W_eff.T
        src, dst = (edge_index[0], edge_index[1])
        locked = jnp.zeros((n,), dtype=bool).at[node_lock].set(True)
        lock = locked[dst] | (src == dst)
        msg = edge_weight[:, None] * h[src]
        norm_feat_msg = jnp.linalg.norm(msg, axis=1)
        norm_all_msg = jnp.sum(norm_feat_msg) / msg.shape[0]
        mask0 = (norm_feat_msg < THR_A * norm_all_msg) & ~lock
        msg = jnp.where(mask0[:, None], 0.0, msg)
        out = jax.ops.segment_sum(msg, dst, num_segments=n) + b
        return out

    def _L0_ffn_ref(x, gamma, beta, Wr, br, W1, b1, W2, b2):
        import jax, jax.numpy as jnp
        import numpy as np
        E = 8
        K = 2
        D = 256
        H = 512
        DOUT = 256
        EPS = 1e-05
        mu = jnp.mean(x, axis=-1, keepdims=True)
        var = jnp.mean(jnp.square(x - mu), axis=-1, keepdims=True)
        xn = (x - mu) * jax.lax.rsqrt(var + EPS) * gamma + beta
        logits = jnp.einsum('bsd,de->bse', xn, Wr) + br
        top_vals, top_idx = jax.lax.top_k(logits, K)
        w = jax.nn.softmax(top_vals, axis=-1)
        w_full = jnp.einsum('bsk,bske->bse', w, jax.nn.one_hot(top_idx, E, dtype=w.dtype))
        y = jnp.zeros(x.shape[:-1] + (DOUT,), x.dtype)
        for e in range(E):
            h = jax.nn.gelu(jnp.einsum('bsd,dh->bsh', xn, W1[e]) + b1[e], approximate=False)
            y_e = jnp.einsum('bsh,hd->bsd', h, W2[e]) + b2[e]
            y = y + y_e * w_full[..., e, None]
        return y
    edge_index = jnp.stack([src, dst])
    x = x + _L0_gnn_ref(_layernorm(x, axis=-1), edge_index, edge_weight, L0_gnn_node_lock, L0_gnn_W, L0_gnn_b)
    x = x + _L0_ffn_ref(_layernorm(x, axis=-1)[None], L0_ffn_gamma, L0_ffn_beta, L0_ffn_Wr, L0_ffn_br, L0_ffn_W1, L0_ffn_b1, L0_ffn_W2, L0_ffn_b2)[0]
    return x

_drawn_inputs = setup_inputs


def setup_inputs(seed=0):
    import zlib

    import numpy as np

    out = dict(_drawn_inputs(seed))
    spreads = {'L0_ffn_br': (0.0, 0.376)}
    factors = {'L0_gnn_b': 8.0,
     'L0_ffn_gamma': 8.0,
     'L0_ffn_beta': 8.0,
     'L0_ffn_Wr': 3.778,
     'L0_ffn_W1': 2.728,
     'L0_ffn_b1': 31.573,
     'L0_ffn_b2': 8.0}
    for name, (base, spread) in spreads.items():
        noise = np.random.default_rng([zlib.crc32(name.encode()), seed]).standard_normal(out[name].shape)
        drawn = base * np.exp(spread * noise) if base else spread * noise
        out[name] = jnp.asarray(drawn.astype(out[name].dtype))
    for name, factor in factors.items():
        out[name] = (out[name] * factor).astype(out[name].dtype)
    return out
```

```python
from contextlib import ExitStack

import concourse.bass as bass
from concourse import mybir

ALU = mybir.AluOpType
ACT = mybir.ActivationFunctionType
AX = mybir.AxisListType
F32 = mybir.dt.float32
I32 = mybir.dt.int32

P = 128
GROUP = 7
HALF = 8
BATCH = 8
EPS = 1e-5
BIG = 65536.0


class Chain:

    def __init__(self, engine, sem, base=0):
        self.engine, self.sem, self.base, self.n = engine, sem, base, 0

    def __call__(self, instruction):
        self.n += 1
        instruction.then_inc(self.sem, 1)
        self.engine.wait_ge(self.sem, self.base + self.n)


def gnn_moe_kernel(nc, x, src, dst, edge_weight, node_lock, W, b, gamma, beta, Wr, br, W1, b1, W2, b2, out):
    N, D = x.shape
    E, = src.shape
    NLOCK, = node_lock.shape
    EXPERTS, _, H = W1.shape
    KC = D // P
    HC = H // P
    WINDOWS = -(-N // P)
    GROUPS = WINDOWS // GROUP
    TAIL = N - (WINDOWS - 1) * P
    DUMMY = WINDOWS
    SLOTS_W = WINDOWS + 1
    NOWHERE = SLOTS_W * P - 1
    TILES = -(-E // P)
    ROWGROUPS = -(-TILES // P)
    BATCHES = -(-TILES // BATCH)
    TCOLS = BATCHES * BATCH
    STEPS = 880
    assert STEPS >= TILES + WINDOWS and STEPS % (2 * HALF) == 0
    ITERS = STEPS // (2 * HALF)
    ROUNDS = -(-(TILES * WINDOWS) // STEPS)
    TAB = STEPS + HALF
    FTILES = 2 * WINDOWS + EXPERTS
    SLOT_TILES = FTILES + 2
    LTILES = -(-NLOCK // P)
    HROW = D + 1
    assert WINDOWS % GROUP == 0 and TILES < ROWGROUPS * P and FTILES % 2 == 0

    h_dram = nc.dram_tensor("h_rows", (WINDOWS * P, HROW), F32).ap()
    lock_dram = nc.dram_tensor("lock_row", (WINDOWS, P), F32).ap()
    xs_dram = nc.dram_tensor("slot_inputs", (SLOT_TILES * P, D), F32).ap()
    ys_dram = nc.dram_tensor("slot_outputs", (SLOT_TILES * P, D), F32).ap()

    with ExitStack() as ctx:
        def sb(name, shape, dt=F32):
            return ctx.enter_context(nc.sbuf_tensor(name, shape, dt))

        def sem(name):
            return ctx.enter_context(nc.semaphore(name))

        acc = sb("acc", [P, SLOTS_W, D])
        big = sb("big", [P, 2 * EXPERTS * KC * H])
        scratch = sb("scratch", [P, TCOLS * 4 + SLOTS_W * P + 5 * ROWGROUPS * P])
        ident = sb("ident", [P, P])
        ones = sb("ones", [P, P])
        before = sb("before", [P, P])
        upto = sb("upto", [P, P])
        iota_row = sb("iota_row", [P, TAB])
        pid = sb("pid", [P, 1])
        winlo = sb("winlo", [P, 2])
        thr = sb("thr", [P, 1])
        gate = sb("gate", [P, 4])
        eps_col = sb("eps_col", [P, 1])
        ntab = sb("ntab", [P, 8])
        rounds_i = sb("rounds_i", [P, 2], I32)
        ps = ctx.enter_context(nc.psum_tensor("ps", [P, 8, 512], F32))
        psf = ps[:, :, :].rearrange("p a b -> p (a b)")

        xnT = big[:, 0:KC * WINDOWS * P].rearrange("p (c n) -> p c n", c=KC)
        w1_sb = big[:, 0:EXPERTS * KC * H]
        w2_sb = big[:, EXPERTS * KC * H:]
        rec = scratch[:, 0:TCOLS * 4].rearrange("p (t c) -> p t c", c=4)
        lockrow = scratch[:, TCOLS * 4:TCOLS * 4 + SLOTS_W * P]
        tail_region = scratch[:, TCOLS * 4 + SLOTS_W * P:]

        with ExitStack() as c1:
            def sb1(name, shape, dt=F32):
                return c1.enter_context(nc.sbuf_tensor(name, shape, dt))

            def sem1(name):
                return c1.enter_context(nc.semaphore(name))

            RP = ROWGROUPS * P
            rows_i = tail_region[:, 0:2 * RP].bitcast(I32).rearrange("p (a g e) -> p a g e", a=2, e=P)
            rows_f = tail_region[:, 2 * RP:5 * RP].rearrange("p (a g e) -> p a g e", a=3, e=P)
            lock_i = sb1("lock_i", [8, P], I32)
            lock_f = sb1("lock_f", [8, P])
            spare = big[:, KC * WINDOWS * P:]
            wrow = lockrow[:, 3 * RP:3 * RP + KC * D].rearrange("p (c d) -> p c d", c=KC)
            WT = sb1("WT", [P, KC, D])
            srcI = lockrow[:, 3 * RP + KC * D:3 * RP + KC * D + TCOLS].bitcast(I32)
            acol = sb1("acol", [P, TCOLS])
            bcol = sb1("bcol", [P, TCOLS])
            absw = sb1("absw", [P, TCOLS])
            lockcol = sb1("lockcol", [P, 3, 8])
            lockcol_i = sb1("lockcol_i", [P, 8], I32)
            diag = lockrow[:, 0:2 * RP].rearrange("p (m g e) -> p m g e", m=2, g=ROWGROUPS)
            mnmx = sb1("mnmx", [P, 2, ROWGROUPS])
            cand = lockrow[:, 2 * RP:3 * RP]
            oneB = spare[:, 0:2 * BATCH * P].rearrange("p (s t e) -> p s t e", s=2, t=BATCH)
            oneA = spare[:, 2 * BATCH * P:2 * BATCH * (P + 2 * WINDOWS)].rearrange("p (s m t e) -> p s m t e", s=2, m=2, t=BATCH)
            lockhist = sb1("lockhist", [P, P])
            norms = sb1("norms", [P, WINDOWS])
            small = sb1("small", [P, 16])

            cleared = sem1("cleared")
            consts = sem1("consts")
            src_in, dst_in, w_in = sem1("src_in"), sem1("dst_in"), sem1("w_in")
            lock_in, W_in, x_in = sem1("lock_in"), sem1("W_in"), sem1("x_in")
            rows_float = sem1("rows_float")
            diag_ready = sem1("diag_ready")
            turned = sem1("turned")
            rec_ready = sem1("rec_ready")
            ranges_up = sem1("ranges_up")
            steps_ready = sem1("steps_ready")
            prefix_ready = sem1("prefix_ready")
            v1 = sem1("v1")
            hist_cols = sem1("hist_cols")

            with nc.Block() as block:
                @block.gpsimd
                def _(pool):
                    nc.gpsimd.memset(rows_i[:, 0, ROWGROUPS - 1, :], 0)
                    nc.gpsimd.memset(rows_i[:, 1, ROWGROUPS - 1, :], NOWHERE)
                    nc.gpsimd.memset(rows_f[:, 2, ROWGROUPS - 1, :], 0.0)
                    nc.gpsimd.memset(lock_i[:, :], NOWHERE)
                    nc.gpsimd.memset(lockrow[:, DUMMY * P:], 0.0)
                    nc.gpsimd.memset(acc[:, WINDOWS - 1:SLOTS_W, :], 0.0).then_inc(cleared, 1)
                    nc.gpsimd.memset(ident[:, :], 0.0).then_inc(v1, 1)
                    nc.gpsimd.memset(ones[:, :], 1.0).then_inc(v1, 1)
                    nc.gpsimd.memset(eps_col[:, :], EPS)
                    nc.gpsimd.iota(iota_row[:, :], [[1, TAB]], base=0, channel_multiplier=0,
                                   allow_small_or_imprecise_dtypes=True)
                    nc.gpsimd.iota(pid[:, :], [[1, 1]], base=0, channel_multiplier=1,
                                   allow_small_or_imprecise_dtypes=True)
                    nc.gpsimd.iota(winlo[:, :], [[P, 2]], base=0, channel_multiplier=P,
                                   allow_small_or_imprecise_dtypes=True)
                    pool.wait_ge(v1, 2)
                    nc.gpsimd.affine_select(out=ident[:, :], in_=ident[:, :], compare_op=ALU.not_equal, fill=1.0,
                                            base=0, pattern=[[-1, P]], channel_multiplier=1)
                    nc.gpsimd.affine_select(out=before[:, :], in_=ones[:, :], compare_op=ALU.is_gt, fill=0.0,
                                            base=0, pattern=[[1, P]], channel_multiplier=-1)
                    nc.gpsimd.affine_select(out=upto[:, :], in_=ones[:, :], compare_op=ALU.is_ge, fill=0.0,
                                            base=0, pattern=[[1, P]], channel_multiplier=-1).then_inc(consts, 1)

                @block.sync
                def _(sp):
                    full = (ROWGROUPS - 1) * P * P
                    whole = (TILES - 1) * P
                    rest = TILES - 1 - (ROWGROUPS - 1) * P
                    sp.wait_ge(cleared, 1)
                    for a, (dram, rows, landed) in enumerate(((dst, rows_i[:, 1], dst_in), (src, rows_i[:, 0], src_in),
                                                              (edge_weight, rows_f[:, 2], w_in))):
                        sp.dma_start(rows[:, 0:ROWGROUPS - 1, :],
                                     dram[0:full].rearrange("(g t e) -> t g e", t=P, e=P)).then_inc(landed, 16)
                        sp.dma_start(rows[0:rest, ROWGROUPS - 1, :],
                                     dram[full:whole].rearrange("(t e) -> t e", e=P)).then_inc(landed, 16)
                        sp.dma_start(rows[rest:rest + 1, ROWGROUPS - 1, 0:E - whole],
                                     dram[whole:E].rearrange("(a e) -> a e", a=1)).then_inc(landed, 16)
                    lw = (LTILES - 1) * P
                    sp.dma_start(lock_i[0:LTILES - 1, :],
                                 node_lock[0:lw].rearrange("(t e) -> t e", e=P)).then_inc(lock_in, 16)
                    sp.dma_start(lock_i[LTILES - 1:LTILES, 0:NLOCK - lw],
                                 node_lock[lw:NLOCK].rearrange("(a e) -> a e", a=1)).then_inc(lock_in, 16)
                    sp.dma_start(wrow[:, :, :], W.rearrange("(c o) k -> o c k", o=P)).then_inc(W_in, 16)
                    step = (WINDOWS - 1) // 4
                    for q in range(4):
                        sp.dma_start(acc[:, q * step:(q + 1) * step, :],
                                     x[q * step * P:(q + 1) * step * P, :].rearrange("(w p) d -> p w d", p=P)
                                     ).then_inc(x_in, 16)
                    sp.dma_start(acc[0:TAIL, WINDOWS - 1, :], x[(WINDOWS - 1) * P:N, :]).then_inc(x_in, 16)

                @block.tensor
                def _(pe):
                    pe.wait_ge(consts, 1)
                    for a, ready in ((0, 2), (1, 1), (2, 0)):
                        if a < 2:
                            pe.wait_ge(rows_float, ready)
                        else:
                            pe.wait_ge(w_in, 48)
                        for g in range(ROWGROUPS):
                            last = pe.transpose(psf[:, a * 1024 + g * P:a * 1024 + (g + 1) * P],
                                                rows_f[:, a, g, :], ident[:, :])
                        last.then_inc(turned, 1)
                    pe.wait_ge(rows_float, 3)
                    pe.transpose(ps[:, 6, 0:8], lock_f[:, :], ident[0:8, 0:8]).then_inc(turned, 1)
                    pe.wait_ge(W_in, 16)
                    for k in range(KC):
                        for o in range(KC):
                            last = pe.transpose(ps[:, 7, k * D + o * P:k * D + (o + 1) * P],
                                                wrow[:, o, k * P:(k + 1) * P], ident[:, :])
                    last.then_inc(turned, 1)
                    pe.wait_ge(diag_ready, 1)
                    pe.wait_ge(rec_ready, 2)
                    for m in range(2):
                        for g in range(ROWGROUPS):
                            last = pe.matmul(psf[0:SLOTS_W, m * 1024 + g * P:m * 1024 + (g + 1) * P],
                                             ones[:, 0:SLOTS_W], diag[:, m, g, :], start=True, stop=True)
                    last.then_inc(ranges_up, 1)
                    pe.wait_ge(steps_ready, 1)
                    pe.matmul(ps[0:SLOTS_W, 4, 0:1], before[0:SLOTS_W, 0:SLOTS_W], ntab[0:SLOTS_W, 2:3],
                              start=True, stop=True)
                    pe.matmul(ps[0:SLOTS_W, 4, 1:2], upto[0:SLOTS_W, 0:SLOTS_W], ntab[0:SLOTS_W, 2:3],
                              start=True, stop=True)
                    pe.matmul(ps[:, 4, 2:3], ones[0:SLOTS_W, :], ntab[0:SLOTS_W, 2:3],
                              start=True, stop=True).then_inc(prefix_ready, 1)

                @block.vector
                def _(dve):
                    chain = Chain(dve, hist_cols)
                    dve.wait_ge(dst_in, 48)
                    dve.tensor_copy(rows_f[:, 1], rows_i[:, 1]).then_inc(rows_float, 1)
                    dve.wait_ge(src_in, 48)
                    dve.tensor_copy(rows_f[:, 0], rows_i[:, 0]).then_inc(rows_float, 1)
                    dve.wait_ge(lock_in, 32)
                    dve.tensor_copy(lock_f[:, :], lock_i[:, :]).then_inc(rows_float, 1)
                    dve.wait_ge(rows_float, 3)
                    chain(dve.tensor_reduce(mnmx[:, 0, :], rows_f[:, 1], AX.X, ALU.min))
                    chain(dve.tensor_reduce(mnmx[:, 1, :], rows_f[:, 1], AX.X, ALU.max))
                    dve.wait_ge(consts, 1)
                    for m in range(2):
                        for g in range(ROWGROUPS):
                            last = dve.tensor_scalar(diag[:, m, g, :], ident[:, :], mnmx[:, m, g:g + 1], None, ALU.mult)
                    last.then_inc(diag_ready, 1)
                    dve.wait_ge(turned, 1)
                    dve.tensor_copy(rec[:, :, 0], psf[:, 0:TCOLS]).then_inc(rec_ready, 1)
                    dve.wait_ge(turned, 2)
                    dve.tensor_copy(rec[:, :, 1], psf[:, 1024:1024 + TCOLS]).then_inc(rec_ready, 1)
                    dve.wait_ge(turned, 3)
                    dve.tensor_copy(rec[:, :, 2], psf[:, 2048:2048 + TCOLS]).then_inc(rec_ready, 1)
                    dve.wait_ge(turned, 4)
                    dve.tensor_copy(lockcol[:, 0, :], ps[:, 6, 0:8]).then_inc(rec_ready, 1)
                    dve.wait_ge(turned, 5)
                    dve.tensor_copy(WT[:, :, :], ps[:, 7, :].rearrange("p (c o) -> p c o", c=KC)).then_inc(rec_ready, 1)
                    dve.wait_ge(rec_ready, 5)
                    chain(dve.tensor_copy(srcI[:, :], rec[:, :, 0]))
                    chain(dve.tensor_scalar(srcI[:, :], srcI[:, :], 7, None, ALU.arith_shift_right))
                    chain(dve.tensor_copy(acol[:, :], srcI[:, :]))
                    chain(dve.scalar_tensor_tensor(bcol[:, :], acol[:, :], float(-P), rec[:, :, 0], ALU.mult, ALU.add))
                    chain(dve.scalar_tensor_tensor(absw[:, :], rec[:, :, 2], -1.0, rec[:, :, 2], ALU.mult, ALU.max))
                    chain(dve.tensor_tensor(rec[:, :, 3], rec[:, :, 0], rec[:, :, 1], ALU.is_equal))
                    chain(dve.tensor_copy(lockcol_i[:, :], lockcol[:, 0, :]))
                    chain(dve.tensor_scalar(lockcol_i[:, :], lockcol_i[:, :], 7, None, ALU.arith_shift_right))
                    chain(dve.tensor_copy(lockcol[:, 1, :], lockcol_i[:, :]))
                    chain(dve.scalar_tensor_tensor(lockcol[:, 2, :], lockcol[:, 1, :], float(-P), lockcol[:, 0, :],
                                                   ALU.mult, ALU.add))
                    dve.wait_ge(ranges_up, 1)
                    wn = slice(0, SLOTS_W)
                    chain(dve.tensor_scalar(cand[wn, 0:TILES], psf[wn, 1024:1024 + TILES], winlo[wn, 0:1], BIG,
                                            ALU.is_lt, ALU.mult))
                    chain(dve.tensor_tensor(cand[wn, 0:TILES], cand[wn, 0:TILES], iota_row[wn, 0:TILES], ALU.add))
                    chain(dve.tensor_reduce(ntab[wn, 0:1], cand[wn, 0:TILES], AX.X, ALU.min))
                    chain(dve.tensor_scalar(ntab[wn, 0:1], ntab[wn, 0:1], float(TILES), None, ALU.min))
                    chain(dve.scalar_tensor_tensor(cand[wn, 0:TILES], psf[wn, 0:TILES], winlo[wn, 1:2],
                                                   iota_row[wn, 1:TILES + 1], ALU.is_lt, ALU.mult))
                    chain(dve.tensor_reduce(ntab[wn, 1:2], cand[wn, 0:TILES], AX.X, ALU.max))
                    chain(dve.tensor_tensor(small[wn, 0:1], ntab[wn, 1:2], ntab[wn, 0:1], ALU.subtract))
                    chain(dve.tensor_scalar(small[wn, 1:2], pid[wn, :], float(WINDOWS), None, ALU.is_lt))
                    chain(dve.tensor_scalar(ntab[wn, 2:3], small[wn, 0:1], 0.0, small[wn, 1:2], ALU.max, ALU.mult))
                    dve.sem_inc(steps_ready, 1)
                    dve.wait_ge(prefix_ready, 1)
                    chain(dve.tensor_copy(ntab[wn, 3:5], ps[wn, 4, 0:2]))
                    chain(dve.tensor_tensor(ntab[wn, 5:6], ntab[wn, 0:1], ntab[wn, 3:4], ALU.subtract))
                    chain(dve.tensor_scalar(ntab[wn, 6:7], pid[wn, :], float(-DUMMY), None, ALU.add))
                    chain(dve.tensor_copy(small[:, 2:3], ps[:, 4, 2:3]))
                    chain(dve.tensor_scalar(cand[:, 0:ROUNDS], iota_row[:, 0:ROUNDS], float(STEPS), small[:, 2:3],
                                            ALU.mult, ALU.is_lt))
                    chain(dve.tensor_reduce(small[:, 3:4], cand[:, 0:ROUNDS], AX.X, ALU.add))
                    chain(dve.tensor_scalar(rounds_i[:, 0:1], small[:, 3:4], 1.0, None, ALU.max))

            xn = tail_region[:, 0:GROUP * D].rearrange("p (w d) -> p w d", w=GROUP)
            std = sb1("std", [P, GROUP])
            var_ready, std_ready = sem1("var_ready"), sem1("std_ready")
            sums_ready, norms_ready = sem1("sums_ready"), sem1("norms_ready")
            stats = sb1("stats", [P, GROUP, 6])
            mv = sb1("mv", [P, GROUP, 2])
            rstd = sb1("rstd", [P, GROUP, 1])
            junk = sb1("junk", [P, GROUP * P])
            colsq = sb1("colsq", [P, KC, GROUPS])
            col = sb1("col", [P, 8, KC])
            prune = tail_region[:, 0:2 * KC * D].rearrange("p (m c d) -> p m c d", m=2, c=KC)
            xT = sb1("xT", [P, 2, KC, P])
            hrow = tail_region[:, GROUP * D:GROUP * (D + HROW)].rearrange("p (w d) -> p w d", w=GROUP)
            nsq = sb1("nsq", [P, GROUP])
            xn_ready, xn_turned, xT_saved = sem1("xn_ready"), sem1("xn_turned"), sem1("xT_saved")
            colsum_ready = sem1("colsum_ready")
            v2, v3, v4 = sem1("v2"), sem1("v3"), sem1("v4")
            colsq_ready = sem1("colsq_ready")
            total_ready = sem1("total_ready")
            W_ready = sem1("W_ready")
            B_ready, A_ready, A_eq, hist_done = sem1("B_ready"), sem1("A_ready"), sem1("A_eq"), sem1("hist_done")
            lockB = sem1("lockB")
            lock_up, lock_out, lock_back = sem1("lock_up"), sem1("lock_out"), sem1("lock_back")
            xT_slot, h_up, h_down, h_norm, h_out = (sem1("xT_slot"), sem1("h_up"), sem1("h_down"), sem1("h_norm"),
                                                    sem1("h_out"))
            h_free = sem1("h_free")
            sum_up, thr_up = sem1("sum_up"), sem1("thr_up")
            zero_mm = sb1("zero_mm", [P, P])
            zero_set = sem1("zero_set")

            with nc.Block() as block:
                @block.vector
                def _(dve):
                    chain = Chain(dve, v3)
                    chain(dve.memset(zero_mm[:, :], 0.0))
                    chain(dve.tensor_tensor(oneB[:, 0], iota_row[:, 0:P].unsqueeze(1).to_broadcast([P, BATCH, P]),
                                            lockcol[:, 2, :].unsqueeze(2).to_broadcast([P, BATCH, P]), ALU.is_equal))
                    chain(dve.tensor_tensor(oneA[:, 0, 0],
                                            iota_row[:, 0:WINDOWS].unsqueeze(1).to_broadcast([P, BATCH, WINDOWS]),
                                            lockcol[:, 1, :].unsqueeze(2).to_broadcast([P, BATCH, WINDOWS]),
                                            ALU.is_equal))
                    dve.sem_inc(lockB, 1)
                    dve.wait_ge(lock_up, 1)
                    chain(dve.tensor_scalar(lockhist[0:WINDOWS, :], ps[0:WINDOWS, 6, 0:P], 1.0, None, ALU.min))
                    dve.sem_inc(lock_up, 1)
                    dve.wait_ge(x_in, 80)
                    with dve.Fori(0, GROUPS) as g:
                        c = Chain(dve, v2, g * 3)
                        for j in range(GROUP):
                            last = dve.bn_stats(stats[:, j, :], acc[:, bass.ds(g * GROUP + j, 1), :]
                                                .rearrange("p a d -> p (a d)"))
                        c(last)
                        dve.memset(gate[:, 0:1], 0.0)
                        for j in range(GROUP):
                            last = dve.bn_aggr(mv[:, j, :], stats[:, j, :])
                        c(last)
                        dve.sem_inc(var_ready, 1)
                        dve.wait_ge(std_ready, g + 1)
                        c(dve.reciprocal(rstd[:, :, 0], std[:, :]))
                        for j in range(GROUP):
                            if j == 0:
                                dve.wait_ge(xn_turned, g * GROUP + GROUP)
                            dve.tensor_scalar(xn[:, j, :], acc[:, bass.ds(g * GROUP + j, 1), :]
                                              .rearrange("p a d -> p (a d)"), mv[:, j, 0:1], rstd[:, j, :],
                                              ALU.subtract, ALU.mult).then_inc(xn_ready, 1)
                    chain = Chain(dve, v4)
                    dve.wait_ge(colsq_ready, KC * GROUPS)
                    chain(dve.tensor_reduce(col[:, 0, :], colsq[:, :, :], AX.X, ALU.add))
                    dve.sem_inc(colsum_ready, 1)
                    dve.wait_ge(total_ready, 1)
                    chain(dve.tensor_reduce(col[:, 1, 0:1], ps[:, 7, 0:KC], AX.X, ALU.add))
                    dve.sem_inc(sums_ready, 1)
                    dve.wait_ge(norms_ready, 1)
                    chain(dve.reciprocal(col[:, 3, :], col[:, 2, :]))
                    chain(dve.tensor_scalar(col[:, 1, 0:1], col[:, 6, 1:2], 1.0 / D, None, ALU.mult))
                    chain(dve.tensor_scalar(col[:, 4, 0:1], col[:, 1, 0:1], 0.1, None, ALU.mult))
                    chain(dve.tensor_scalar(col[:, 5, :], col[:, 3, :], col[:, 4, 0:1], None, ALU.mult))
                    chain(dve.tensor_scalar(col[:, 6, 0:1], col[:, 1, 0:1], 1e-8, None, ALU.is_gt))
                    chain(dve.scalar_tensor_tensor(prune[:, 0], WT[:, :, :], -1.0, WT[:, :, :], ALU.mult, ALU.max))
                    for k in range(KC):
                        chain(dve.tensor_scalar(prune[:, 1, k, :], prune[:, 0, k, :], col[:, 5, k:k + 1],
                                                col[:, 6, 0:1], ALU.is_lt, ALU.mult))
                    chain(dve.tensor_tensor(prune[:, 0], prune[:, 1], WT[:, :, :], ALU.mult))
                    chain(dve.tensor_tensor(WT[:, :, :], WT[:, :, :], prune[:, 0], ALU.subtract))
                    dve.sem_inc(W_ready, 1)
                    with dve.Fori(0, BATCHES // 2) as i:
                        for s in range(2):
                            dve.wait_ge(hist_done, i * 2 + s + 1)
                            dve.tensor_tensor(oneB[:, s], iota_row[:, 0:P].unsqueeze(1).to_broadcast([P, BATCH, P]),
                                              bcol[:, bass.ds((i * 2 + s) * BATCH, BATCH)].unsqueeze(2)
                                              .to_broadcast([P, BATCH, P]), ALU.is_equal).then_inc(B_ready, 1)
                            dve.tensor_tensor(oneA[:, s, 0],
                                              iota_row[:, 0:WINDOWS].unsqueeze(1).to_broadcast([P, BATCH, WINDOWS]),
                                              acol[:, bass.ds((i * 2 + s) * BATCH, BATCH)].unsqueeze(2)
                                              .to_broadcast([P, BATCH, WINDOWS]), ALU.is_equal).then_inc(A_eq, 1)
                            dve.wait_ge(A_eq, i * 2 + s + 1)
                            dve.tensor_tensor(oneA[:, s, 1], oneA[:, s, 0],
                                              absw[:, bass.ds((i * 2 + s) * BATCH, BATCH)].unsqueeze(2)
                                              .to_broadcast([P, BATCH, WINDOWS]), ALU.mult).then_inc(A_ready, 1)
                    chain2 = Chain(dve, rows_float, 3)
                    dve.wait_ge(h_down, GROUPS)
                    dve.wait_ge(hist_done, BATCHES + 3)
                    chain2(dve.tensor_tensor(junk[:, 0:WINDOWS], ps[:, 5, 0:WINDOWS], norms[:, :], ALU.mult))
                    chain2(dve.tensor_reduce(col[:, 7, 0:1], junk[:, 0:WINDOWS], AX.X, ALU.add))
                    dve.sem_inc(sum_up, 1)
                    dve.wait_ge(thr_up, 1)
                    chain2(dve.tensor_scalar(thr[:, :], ps[:, 7, 4:5], 1.0 / E, 0.1, ALU.mult, ALU.mult))

                @block.tensor
                def _(pe):
                    pe.sem_inc(xn_turned, GROUP)
                    pe.sem_inc(h_up, 1)
                    pe.sem_inc(hist_done, 2)
                    pe.wait_ge(lockB, 1)
                    for t in range(BATCH):
                        last = pe.matmul(ps[0:WINDOWS, 6, 0:P], oneA[:, 0, 0, t, :], oneB[:, 0, t, :],
                                         start=(t == 0), stop=(t == BATCH - 1))
                    last.then_inc(lock_up, 1)
                    with pe.Fori(0, GROUPS) as g:
                        for j in range(GROUP):
                            pe.wait_ge(xn_ready, g * GROUP + j + 1)
                            if j == 0:
                                pe.wait_ge(xT_saved, g * KC + KC)
                            for k in range(KC):
                                last = pe.transpose(psf[:, k * 1024 + j * P:k * 1024 + (j + 1) * P],
                                                    xn[:, j, k * P:(k + 1) * P], ident[:, :])
                            last.then_inc(xn_turned, 1)
                    pe.wait_ge(colsum_ready, 1)
                    pe.matmul(ps[:, 7, 0:KC], ones[:, :], col[:, 0, :], start=True, stop=True).then_inc(total_ready, 1)
                    pe.matmul(ps[:, 5, 0:WINDOWS], zero_mm[:, :], zero_mm[:, 0:WINDOWS], start=True, stop=False,
                              skip_group_check=True)

                    def histogram(n, s):
                        pe.wait_ge(B_ready, n + 1)
                        pe.wait_ge(A_ready, n + 1)
                        for t in range(BATCH):
                            last = pe.matmul(ps[:, 5, 0:WINDOWS], oneB[:, s, t, :], oneA[:, s, 1, t, :],
                                             start=False, stop=False, skip_group_check=True)
                        last.then_inc(hist_done, 1)

                    pe.wait_ge(W_ready, 1)
                    with pe.Fori(0, GROUPS) as g:
                        for j in range(GROUP):
                            pe.wait_ge(xT_slot, g * GROUP + j + 1)
                            if j >= 2:
                                pe.wait_ge(h_norm, g * GROUP + j + 1)
                            else:
                                pe.wait_ge(h_norm, g * GROUP + 2)
                            for k in range(KC):
                                last = pe.matmul(ps[:, 2 + j % 2, 0:D], xT[:, j % 2, k, :], WT[:, k, :],
                                                 start=(k == 0), stop=(k == KC - 1))
                            last.then_inc(h_up, 1)
                            for s in range(2):
                                histogram(g * (2 * GROUP) + 2 * j + s, s)
                    for n in range(2 * WINDOWS, BATCHES):
                        histogram(n, n % 2)
                    pe.matmul(ps[:, 5, 0:WINDOWS], zero_mm[:, :], zero_mm[:, 0:WINDOWS], start=False, stop=True,
                              skip_group_check=True).then_inc(hist_done, 1)
                    pe.wait_ge(sum_up, 1)
                    pe.matmul(ps[:, 7, 4:5], ones[:, :], col[:, 7, 0:1], start=True, stop=True).then_inc(thr_up, 1)

                @block.scalar
                def _(act):
                    act.sem_inc(xT_saved, KC)
                    act.sem_inc(h_norm, 2)
                    with act.Fori(0, GROUPS) as g:
                        act.wait_ge(var_ready, g + 1)
                        act.activation(std[:, :], mv[:, :, 1], ACT.Sqrt, bias=eps_col[:, :]).then_inc(std_ready, 1)
                        act.wait_ge(xn_turned, (g + 2) * GROUP)
                        for k in range(KC):
                            act.copy(xnT[:, k, bass.ds(g * GROUP * P, GROUP * P)],
                                     psf[:, k * 1024:k * 1024 + GROUP * P])
                            act.activation(junk[:, :], psf[:, k * 1024:k * 1024 + GROUP * P], ACT.Square,
                                           accum_out=colsq[:, k, bass.ds(g, 1)]).then_inc(xT_saved, 1)
                            act.wait_ge(xT_saved, g * KC + k + 1 + KC)
                    act.sem_inc(colsq_ready, KC * GROUPS)
                    act.wait_ge(sums_ready, 1)
                    act.activation(col[:, 2, :], col[:, 0, :], ACT.Sqrt)
                    act.activation(col[:, 6, 1:2], col[:, 1, 0:1], ACT.Sqrt).then_inc(norms_ready, 1)
                    with act.Fori(0, GROUPS) as g:
                        for j in range(GROUP):
                            act.wait_ge(h_up, g * GROUP + max(j - 1, 0) + 1)
                            act.copy(xT[:, j % 2], xnT[:, :, bass.ds((g * GROUP + j) * P, P)]).then_inc(xT_slot, 1)
                            act.wait_ge(h_up, g * GROUP + j + 2)
                            if j == 0:
                                act.wait_ge(h_free, g + 1)
                            act.copy(hrow[:, j, 0:D], ps[:, 2 + j % 2, 0:D])
                            act.activation(junk[:, 0:D], ps[:, 2 + j % 2, 0:D], ACT.Square,
                                           accum_out=nsq[:, j:j + 1]).then_inc(h_norm, 1)
                            act.wait_ge(h_norm, g * GROUP + j + 3)
                        act.activation(norms[:, bass.ds(g * GROUP, GROUP)], nsq[:, :], ACT.Sqrt)
                        act.activation(hrow[:, :, D], nsq[:, :], ACT.Sqrt).then_inc(h_down, 1)

                @block.sync
                def _(sp):
                    sp.wait_ge(lock_up, 2)
                    sp.dma_start(lock_dram, lockhist[0:WINDOWS, :]).then_inc(lock_out, 16)
                    sp.wait_ge(lock_out, 16)
                    sp.dma_start(lockrow[:, 0:WINDOWS * P],
                                 lock_dram.rearrange("(a w) e -> a (w e)", a=1).to_broadcast([P, WINDOWS * P])
                                 ).then_inc(lock_back, 16)
                    sp.sem_inc(h_free, 1)
                    with sp.Fori(0, GROUPS) as g:
                        sp.wait_ge(h_down, g + 1)
                        sp.dma_start(h_dram[bass.ds(g * (GROUP * P), GROUP * P), :]
                                     .rearrange("(w p) d -> p w d", p=P), hrow[:, :, :]).then_inc(h_out, 16)
                        sp.wait_ge(h_out, (g + 1) * 16)
                        sp.sem_inc(h_free, 1)
                    sp.wait_ge(h_out, GROUPS * 16)
                    sp.wait_ge(lock_back, 16)

        with ExitStack() as c2:
            def sb2(name, shape, dt=F32):
                return c2.enter_context(nc.sbuf_tensor(name, shape, dt))

            def sem2(name):
                return c2.enter_context(nc.semaphore(name))

            tile_tab = sb2("tile_tab", [P, TAB], I32)
            win_tab = sb2("win_tab", [P, TAB], I32)
            win_base = sb2("win_base", [P, TAB])
            terms = sb2("terms", [P, 3, TAB])
            bounds = sb2("bounds", [P, 8])
            zeros = sb2("zeros", [P, D])
            recs = sb2("recs", [P, 2, HALF, 4])
            src_idx = sb2("src_idx", [P, 2, HALF], I32)
            coef = sb2("coef", [P, 2, 8, HALF])
            keepw = sb2("keepw", [P, 2, HALF, P])
            S = sb2("S", [P, 4, P])
            G = tail_region[:, 0:2 * HALF * HROW].rearrange("p (s u d) -> p s u d", s=2, u=HALF)
            TH = TAB // 2

            terms_ready, tab_up, tab_ready = sem2("terms_ready"), sem2("tab_up"), sem2("tab_ready")
            tv = sem2("tv")
            recs_ready, idx_ready = sem2("recs_ready"), sem2("idx_ready")
            gathered = [sem2(f"gathered{k}") for k in range(2 * HALF)]
            cv, coef_ready, keep_ready = sem2("cv"), sem2("coef_ready"), sem2("keep_ready")
            S_ready, messages_up, acc_done = sem2("S_ready"), sem2("messages_up"), sem2("acc_done")
            gated = sem2("gated")
            zeros_set, zeroed, weights_in = sem2("zeros_set"), sem2("zeroed"), sem2("weights_in")

            def value(engine, ap, top):
                _, values = nc.values_load_multi_w_load_instructions(
                    ap, engines=[engine.engine], min_val=0, max_val=top,
                    skip_runtime_bounds_check_because="the tables hold tile and window numbers only")
                return values

            with nc.Block() as block:
                @block.sync
                def _(sp):
                    sp.dma_start(w1_sb.rearrange("p (a h) -> p a h", h=H),
                                 W1.rearrange("e (c k) h -> k (e c) h", k=P)).then_inc(weights_in, 16)
                    sp.dma_start(w2_sb.rearrange("p (a d) -> p a d", d=D),
                                 W2.rearrange("e (c k) d -> k (e c) d", k=P)).then_inc(weights_in, 16)
                    sp.wait_ge(zeros_set, 1)
                    for lo in range(0, SLOT_TILES, 27):
                        n = min(27, SLOT_TILES - lo)
                        sp.dma_start(xs_dram[lo * P:(lo + n) * P, :].rearrange("(t p) d -> p t d", p=P),
                                     zeros[:, :].unsqueeze(1).to_broadcast([P, n, D])).then_inc(zeroed, 16)
                    for t in range(FTILES, SLOT_TILES):
                        sp.dma_start(ys_dram[t * P:(t + 1) * P, :], zeros[:, :]).then_inc(zeroed, 16)
                    sp.wait_ge(zeroed, 16 * (-(-SLOT_TILES // 27) + 2))
                    sp.wait_ge(weights_in, 32)

                @block.gpsimd
                def _(pool):
                    pool.sem_inc(gated, 1)
                    nc.gpsimd.memset(zeros[:, :], 0.0).then_inc(zeros_set, 1)
                    pool.wait_ge(zeros_set, 1)
                    rounds = pool.value_load(rounds_i[0:1, 0:1], min_val=1, max_val=ROUNDS)
                    with pool.Fori(0, rounds) as r:
                        with pool.Fori(0, ITERS) as i:
                            for s in range(2):
                                half = r * (2 * ITERS) + i * 2 + s
                                pool.wait_ge(idx_ready, half + 1)
                                pool.wait_ge(messages_up, half * HALF + 4)
                                pool.wait_ge(gated, half + 1)
                                nc.gpsimd.tensor_tensor(gate[:, 0:1], zeros[:, 0:1], zeros[:, 1:2],
                                                        ALU.add).then_inc(gated, 1)
                                for u in range(HALF):
                                    nc.gpsimd.indirect_dma_start(
                                        G[:, s, u, :], None, h_dram,
                                        bass.IndirectOffsetOnAxis(ap=src_idx[:, s, u:u + 1], axis=0)
                                    ).then_inc(gathered[s * HALF + u], 16)

                @block.scalar
                def _(act):
                    def fetch(s, at):
                        tiles = value(act, tile_tab[0:1, bass.ds(at, HALF)], TILES - 1)
                        for u in range(HALF):
                            last = act.copy(recs[:, s, u, :], rec[:, bass.ds(tiles[u], 1), :]
                                            .rearrange("p a c -> p (a c)"))
                        last.then_inc(recs_ready, 1)

                    act.wait_ge(tab_ready, 1)
                    fetch(0, 0)
                    act.wait_ge(recs_ready, 1)
                    act.copy(src_idx[:, 0, :], recs[:, 0, :, 0]).then_inc(idx_ready, 1)
                    rounds = act.value_load(rounds_i[0:1, 0:1], min_val=1, max_val=ROUNDS)
                    with act.Fori(0, rounds) as r:
                        act.wait_ge(tab_ready, r + 1)
                        with act.Fori(0, ITERS) as i:
                            for s in range(2):
                                half = r * (2 * ITERS) + i * 2 + s
                                fetch(1 - s, (i * 2 + s + 1) * HALF)
                                act.wait_ge(recs_ready, half + 2)
                                act.copy(src_idx[:, 1 - s, :], recs[:, 1 - s, :, 0]).then_inc(idx_ready, 1)
                                wins = value(act, win_tab[0:1, bass.ds((i * 2 + s) * HALF, HALF)], DUMMY)
                                act.wait_ge(coef_ready, half + 1)
                                act.wait_ge(S_ready, half * HALF + HALF)
                                for u in range(HALF):
                                    act.activation(keepw[:, s, u, :], lockrow[:, bass.ds(wins[u] * P, P)],
                                                   ACT.Identity, scale=coef[:, s, 5, u:u + 1],
                                                   bias=coef[:, s, 4, u:u + 1]).then_inc(keep_ready, 1)

                @block.tensor
                def _(pe):
                    pe.sem_inc(messages_up, 12)
                    rounds = pe.value_load(rounds_i[0:1, 0:1], min_val=1, max_val=ROUNDS)
                    with pe.Fori(0, rounds) as r:
                        pe.wait_ge(terms_ready, r + 1)
                        for m in range(2):
                            for q in range(2):
                                last = pe.matmul(ps[:, 2 * m + q, 0:TH], ones[0:SLOTS_W, :],
                                                 terms[0:SLOTS_W, 1 + m, q * TH:(q + 1) * TH], start=True, stop=True)
                        last.then_inc(tab_up, 1)
                        with pe.Fori(0, ITERS) as i:
                            for s in range(2):
                                for u in range(HALF):
                                    step = (r * (2 * ITERS) + i * 2 + s) * HALF + u
                                    pe.wait_ge(S_ready, step + 17)
                                    pe.wait_ge(acc_done, step + 1)
                                    pe.matmul(ps[:, 4 + u % 4, 0:D], S[:, u % 4, :], G[:, s, u, 0:D],
                                              start=True, stop=True).then_inc(messages_up, 1)

                @block.vector
                def _(dve):
                    dve.sem_inc(S_ready, 16)
                    dve.sem_inc(acc_done, 4)
                    wn = slice(0, SLOTS_W)
                    c = Chain(dve, tv)
                    c(dve.tensor_copy(bounds[wn, 0:3], ntab[wn, 3:6]))
                    rounds = dve.value_load(rounds_i[0:1, 0:1], min_val=1, max_val=ROUNDS)
                    with dve.Fori(0, rounds) as r:
                        c = Chain(dve, tv, r * 10 + 1)
                        c(dve.tensor_scalar(terms[wn, 0, :], iota_row[wn, :], bounds[wn, 1:2], None, ALU.is_lt))
                        c(dve.scalar_tensor_tensor(terms[wn, 0, :], iota_row[wn, :], bounds[wn, 0:1], terms[wn, 0, :],
                                                   ALU.is_ge, ALU.mult))
                        c(dve.scalar_tensor_tensor(terms[wn, 1, :], iota_row[wn, :], bounds[wn, 2:3], terms[wn, 0, :],
                                                   ALU.add, ALU.mult))
                        c(dve.tensor_scalar(terms[wn, 2, :], terms[wn, 0, :], ntab[wn, 6:7], None, ALU.mult))
                        dve.sem_inc(terms_ready, 1)
                        c(dve.tensor_scalar(bounds[wn, 0:2], bounds[wn, 0:2], float(-STEPS), None, ALU.add))
                        c(dve.tensor_scalar(bounds[wn, 2:3], bounds[wn, 2:3], float(STEPS), None, ALU.add))
                        dve.wait_ge(tab_up, r + 1)
                        halves = lambda t: t.rearrange("p (q n) -> p q n", q=2)
                        c(dve.tensor_copy(halves(tile_tab[:, :]), ps[:, 0:2, 0:TH]))
                        c(dve.tensor_scalar(halves(win_tab[:, :]), ps[:, 2:4, 0:TH], float(DUMMY), None, ALU.add))
                        c(dve.tensor_scalar(halves(win_base[:, :]), ps[:, 2:4, 0:TH], float(DUMMY), float(P),
                                            ALU.add, ALU.mult))
                        c(dve.memset(gate[:, 1:2], 0.0))
                        dve.sem_inc(tab_ready, 1)
                        with dve.Fori(0, ITERS) as i:
                            for s in range(2):
                                half = r * (2 * ITERS) + i * 2 + s
                                wins = value(dve, win_tab[0:1, bass.ds((i * 2 + s) * HALF, HALF)], DUMMY)
                                for u in range(HALF):
                                    dve.wait_ge(gathered[s * HALF + u], (r * ITERS + i) * 16 + 16)
                                c = Chain(dve, cv, half * 4)
                                norm, w, loops = G[:, s, :, D], recs[:, s, :, 2], recs[:, s, :, 3]
                                dve.tensor_tensor(coef[:, s, 6, :], recs[:, s, :, 1],
                                                  win_base[:, bass.ds((i * 2 + s) * HALF, HALF)], ALU.subtract)
                                c(dve.tensor_tensor(coef[:, s, 0, :], norm, w, ALU.mult))
                                c(dve.scalar_tensor_tensor(coef[:, s, 1, :], coef[:, s, 0, :], -1.0, coef[:, s, 0, :],
                                                           ALU.mult, ALU.max))
                                c(dve.scalar_tensor_tensor(coef[:, s, 2, :], coef[:, s, 1, :], thr[:, 0:1], loops,
                                                           ALU.is_ge, ALU.max))
                                c(dve.tensor_tensor(coef[:, s, 4, :], coef[:, s, 2, :], w, ALU.mult))
                                dve.tensor_tensor(coef[:, s, 5, :], w, coef[:, s, 4, :],
                                                  ALU.subtract).then_inc(coef_ready, 1)

                                def add(u):
                                    step = half * HALF + u
                                    dve.wait_ge(messages_up, step + 13)
                                    dve.wait_ge(acc_done, step + 4)
                                    at = acc[:, bass.ds(wins[u], 1), :].rearrange("p a d -> p (a d)")
                                    dve.tensor_tensor(at, at, ps[:, 4 + u % 4, 0:D], ALU.add).then_inc(acc_done, 1)

                                for u in range(HALF):
                                    step = half * HALF + u
                                    dve.wait_ge(keep_ready, step + 1)
                                    dve.wait_ge(messages_up, step + 9)
                                    dve.scalar_tensor_tensor(S[:, u % 4, :], iota_row[:, 0:P], coef[:, s, 6, u:u + 1],
                                                             keepw[:, s, u, :], ALU.is_equal,
                                                             ALU.mult).then_inc(S_ready, 1)
                                    if u >= 2:
                                        add(u - 2)
                                add(HALF - 2)
                                add(HALF - 1)
        xn_all = scratch[:, 0:WINDOWS * D].rearrange("p (w d) -> p w d", w=WINDOWS)
        weight_k = sb("weight_k", [P, 2, WINDOWS])
        pos_k = sb("pos_k", [P, 2, WINDOWS + GROUP], I32)
        tile_expert = sb("tile_expert", [P, FTILES], I32)
        rest3 = scratch[:, WINDOWS * D:]
        gamma_b, beta_b, bias_b = rest3[:, 0:D], rest3[:, D:2 * D], rest3[:, 2 * D:3 * D]
        b1T = sb("b1T", [P, EXPERTS * HC])
        b2_b = sb("b2_b", [P, EXPERTS, D])
        with ExitStack() as c3:
            def sb3(name, shape, dt=F32):
                return c3.enter_context(nc.sbuf_tensor(name, shape, dt))

            def sem3(name):
                return c3.enter_context(nc.semaphore(name))

            Wr_sb = sb3("Wr_sb", [P, KC, EXPERTS])
            br_b = sb3("br_b", [P, EXPERTS])
            b1rows = sb3("b1rows", [EXPERTS * HC, P])
            work3 = sb3("work3", [P, 3 * GROUP * D])
            t1 = work3[:, 0:GROUP * D].rearrange("p (w d) -> p w d", w=GROUP)
            t2 = work3[:, GROUP * D:2 * GROUP * D].rearrange("p (w d) -> p w d", w=GROUP)
            stat = sb3("stat", [P, GROUP, 6])
            mv3 = sb3("mv3", [P, 2, GROUP, 2])
            sd = sb3("sd", [P, 2, GROUP])
            sc = sb3("sc", [P, 2, 2, GROUP])
            xTg = work3[:, 2 * GROUP * D:].rearrange("p (c n) -> p c n", c=KC)
            logits = rest3[:, 3 * D:3 * D + WINDOWS * EXPERTS].rearrange("p (w e) -> p w e", w=WINDOWS)
            r = {n: work3[:, GROUP * D + q * WINDOWS * EXPERTS:GROUP * D + (q + 1) * WINDOWS * EXPERTS]
                 .rearrange("p (w e) -> p w e", w=WINDOWS) for q, n in enumerate(
                     ("eq", "cand", "first", "second", "masked", "both", "scan_a", "scan_b", "pos"))}
            col3 = work3[:, FTILES * EXPERTS:FTILES * EXPERTS + 8 * WINDOWS].rearrange("p (m w) -> p m w", m=8)
            e_tab = sb3("e_tab", [P, 4, EXPERTS])
            e_int = sb3("e_int", [P, EXPERTS], I32)
            te = work3[:, 0:FTILES * EXPERTS].rearrange("p (t e) -> p t e", e=EXPERTS)
            te_f = sb3("te_f", [P, FTILES])
            pos_slot = sb3("pos_slot", [P, 2, GROUP], I32)
            rows_slot = t1

            params_in = sem3("params_in")
            p3 = sem3("p3")
            var3, std3 = sem3("var3"), sem3("std3")
            normed = sem3("normed")
            final3, saved3 = sem3("final3"), sem3("saved3")
            turned3, xT3, routed3, logits3 = sem3("turned3"), sem3("xT3"), sem3("routed3"), sem3("logits3")
            b1_turned = sem3("b1_turned")
            both_ready, counts_up = sem3("both_ready"), sem3("counts_up")
            soft_in, soft_out = sem3("soft_in"), sem3("soft_out")
            r3, normed_go, slots_free, gated3 = sem3("r3"), sem3("normed_go"), sem3("slots_free"), sem3("gated3")

            def row_of(vector, n):
                return vector.rearrange("(a d) -> a d", a=1).to_broadcast([P, n])

            with nc.Block() as block:
                @block.sync
                def _(sp):
                    sp.dma_start(bias_b[:, :], row_of(b, D)).then_inc(params_in, 16)
                    sp.dma_start(gamma_b[:, :], row_of(gamma, D)).then_inc(params_in, 16)
                    sp.dma_start(beta_b[:, :], row_of(beta, D)).then_inc(params_in, 16)
                    sp.dma_start(br_b[:, :], row_of(br, EXPERTS)).then_inc(params_in, 16)
                    sp.dma_start(Wr_sb[:, :, :], Wr.rearrange("(c k) e -> k c e", k=P)).then_inc(params_in, 16)
                    sp.dma_start(b1rows[:, :], b1.rearrange("e (c h) -> (e c) h", h=P)).then_inc(params_in, 16)
                    sp.dma_start(b2_b[:, :, :].rearrange("p e d -> p (e d)"),
                                 b2.rearrange("(a e) d -> a (e d)", a=1).to_broadcast([P, EXPERTS * D])
                                 ).then_inc(params_in, 16)
                    sp.wait_ge(params_in, 7 * 16)

                @block.vector
                def _(dve):
                    dve.wait_ge(params_in, 7 * 16)
                    dve.sem_inc(logits3, 1)
                    with dve.Fori(0, GROUPS) as g:
                        c = Chain(dve, p3, g * 10)
                        at = acc[:, bass.ds(g * GROUP, GROUP), :]
                        c(dve.tensor_tensor(at, at, bias_b[:, :].unsqueeze(1).to_broadcast([P, GROUP, D]), ALU.add))
                        for m in range(2):
                            dve.memset(gate[:, 2:3], 0.0)
                            for j in range(GROUP):
                                row = (acc[:, bass.ds(g * GROUP + j, 1), :].rearrange("p a d -> p (a d)") if m == 0
                                       else t1[:, j, :])
                                last = dve.bn_stats(stat[:, j, :], row)
                            c(last)
                            dve.memset(gate[:, 2:3], 0.0)
                            for j in range(GROUP):
                                last = dve.bn_aggr(mv3[:, m, j, :], stat[:, j, :])
                            c(last)
                            dve.sem_inc(var3, 1)
                            dve.wait_ge(std3, g * 2 + m + 1)
                            c(dve.reciprocal(sc[:, m, 0, :], sd[:, m, :]))
                            c(dve.scalar_tensor_tensor(sc[:, m, 1, :], mv3[:, m, :, 0], -1.0, sc[:, m, 0, :],
                                                       ALU.mult, ALU.mult))
                            dve.sem_inc(normed_go, 1)
                            dve.wait_ge(normed, g * 2 + m + 1)
                        c(dve.tensor_tensor(t2[:, :, :], t2[:, :, :],
                                            gamma_b[:, :].unsqueeze(1).to_broadcast([P, GROUP, D]), ALU.mult))
                        dve.tensor_tensor(t2[:, :, :], t2[:, :, :],
                                          beta_b[:, :].unsqueeze(1).to_broadcast([P, GROUP, D]),
                                          ALU.add).then_inc(final3, 1)
                        dve.wait_ge(routed3, g + 1)
                        dve.tensor_tensor(logits[:, bass.ds(g * GROUP, GROUP), :],
                                          ps[:, 4, 0:GROUP * EXPERTS].rearrange("p (w e) -> p w e", w=GROUP),
                                          br_b[:, :].unsqueeze(1).to_broadcast([P, GROUP, EXPERTS]),
                                          ALU.add).then_inc(logits3, 1)
                    dve.wait_ge(logits3, GROUPS + 1)
                    c = Chain(dve, r3)
                    c(dve.memset(pos_k[:, :, WINDOWS:], 0))
                    e_iota = iota_row[:, 0:EXPERTS].unsqueeze(1).to_broadcast([P, WINDOWS, EXPERTS])
                    over = lambda column: column.unsqueeze(2).to_broadcast([P, WINDOWS, EXPERTS])
                    for scores, top, hot in ((logits[:, :, :], 0, r["first"]), (r["masked"][:, :, :], 1, r["second"])):
                        c(dve.tensor_reduce(col3[:, top, :], scores, AX.X, ALU.max))
                        c(dve.tensor_tensor(r["eq"][:, :, :], scores, over(col3[:, top, :]), ALU.is_ge))
                        c(dve.tensor_scalar(r["cand"][:, :, :], r["eq"][:, :, :], -BIG, BIG, ALU.mult, ALU.add))
                        c(dve.tensor_tensor(r["cand"][:, :, :], r["cand"][:, :, :], e_iota, ALU.add))
                        c(dve.tensor_reduce(col3[:, 2, :], r["cand"][:, :, :], AX.X, ALU.min))
                        c(dve.tensor_tensor(hot[:, :, :], e_iota, over(col3[:, 2, :]), ALU.is_equal))
                        if top == 0:
                            c(dve.scalar_tensor_tensor(r["masked"][:, :, :], hot[:, :, :], -3e38, logits[:, :, :],
                                                       ALU.mult, ALU.add))
                    c(dve.tensor_tensor(col3[:, 3, :], col3[:, 1, :], col3[:, 0, :], ALU.subtract))
                    dve.sem_inc(soft_in, 1)
                    dve.wait_ge(soft_out, 1)
                    c(dve.tensor_scalar(col3[:, 5, :], col3[:, 4, :], 1.0, None, ALU.add))
                    c(dve.reciprocal(weight_k[:, 0, :], col3[:, 5, :]))
                    c(dve.tensor_tensor(weight_k[:, 1, :], col3[:, 4, :], weight_k[:, 0, :], ALU.mult))
                    c(dve.tensor_scalar(col3[:, 6, :], iota_row[:, 0:WINDOWS], float(P), pid[:, :], ALU.mult, ALU.add))
                    c(dve.tensor_scalar(col3[:, 6, :], col3[:, 6, :], float(N), None, ALU.is_lt))
                    c(dve.tensor_tensor(r["both"][:, :, :], r["first"][:, :, :], r["second"][:, :, :], ALU.add))
                    c(dve.tensor_tensor(r["both"][:, :, :], r["both"][:, :, :], over(col3[:, 6, :]), ALU.mult))
                    dve.sem_inc(both_ready, 1)
                    dve.wait_ge(counts_up, 1)
                    flat = WINDOWS * EXPERTS
                    here, there = r["scan_a"], r["scan_b"]
                    c(dve.tensor_copy(here[:, :, :], ps[:, 6, 0:flat].rearrange("p (w e) -> p w e", e=EXPERTS)))
                    shift = 1
                    while shift < WINDOWS:
                        c(dve.tensor_copy(there[:, 0:shift, :], here[:, 0:shift, :]))
                        c(dve.tensor_tensor(there[:, shift:, :], here[:, shift:, :], here[:, 0:WINDOWS - shift, :],
                                            ALU.add))
                        here, there = there, here
                        shift *= 2
                    c(dve.tensor_scalar(e_int[:, :], here[:, WINDOWS - 1, :], float(P - 1), None, ALU.add))
                    c(dve.tensor_scalar(e_int[:, :], e_int[:, :], 7, None, ALU.arith_shift_right))
                    c(dve.tensor_copy(e_tab[:, 0, :], e_int[:, :]))
                    c(dve.memset(e_tab[:, 1, 0:1], 0.0))
                    for e in range(1, EXPERTS):
                        c(dve.tensor_tensor(e_tab[:, 1, e:e + 1], e_tab[:, 1, e - 1:e], e_tab[:, 0, e - 1:e], ALU.add))
                    c(dve.tensor_scalar(e_tab[:, 2, :], e_tab[:, 1, :], float(P), None, ALU.mult))
                    pos = r["pos"]
                    c(dve.tensor_copy(pos[:, :, :], ps[:, 5, 0:flat].rearrange("p (w e) -> p w e", e=EXPERTS)))
                    c(dve.tensor_tensor(pos[:, 1:, :], pos[:, 1:, :], here[:, 0:WINDOWS - 1, :], ALU.add))
                    c(dve.tensor_tensor(pos[:, :, :], pos[:, :, :],
                                        e_tab[:, 2, :].unsqueeze(1).to_broadcast([P, WINDOWS, EXPERTS]), ALU.add))
                    c(dve.tensor_scalar(col3[:, 7, :], col3[:, 6, :], -1.0, 1.0, ALU.mult, ALU.add))
                    c(dve.tensor_scalar(col3[:, 5, 0:1], pid[:, :], float(FTILES * P), None, ALU.add))
                    c(dve.tensor_scalar(col3[:, 7, :], col3[:, 7, :], col3[:, 5, 0:1], None, ALU.mult))
                    for k, hot in enumerate((r["first"], r["second"])):
                        c(dve.tensor_tensor(r["eq"][:, :, :], hot[:, :, :], pos[:, :, :], ALU.mult))
                        c(dve.tensor_reduce(col3[:, 2, :], r["eq"][:, :, :], AX.X, ALU.add))
                        c(dve.tensor_tensor(col3[:, 2, :], col3[:, 2, :], col3[:, 6, :], ALU.mult))
                        if k == 1:
                            c(dve.scalar_tensor_tensor(col3[:, 7, :], col3[:, 6, :], float(-P), col3[:, 7, :],
                                                       ALU.mult, ALU.add))
                            c(dve.tensor_scalar(col3[:, 7, :], col3[:, 7, :], float(P), None, ALU.add))
                        c(dve.tensor_tensor(pos_k[:, k, 0:WINDOWS], col3[:, 2, :], col3[:, 7, :], ALU.add))
                    c(dve.tensor_tensor(te[:, :, 1:],
                                        iota_row[:, 0:FTILES].unsqueeze(2).to_broadcast([P, FTILES, EXPERTS - 1]),
                                        e_tab[:, 1, 1:].unsqueeze(1).to_broadcast([P, FTILES, EXPERTS - 1]), ALU.is_ge))
                    c(dve.tensor_reduce(te_f[:, :], te[:, :, 1:], AX.X, ALU.add))
                    c(dve.tensor_copy(tile_expert[:, :], te_f[:, :]))

                @block.scalar
                def _(act):
                    act.wait_ge(params_in, 7 * 16)
                    act.wait_ge(b1_turned, 1)
                    act.copy(b1T[:, :], ps[:, 7, 0:EXPERTS * HC])
                    with act.Fori(0, GROUPS) as g:
                        for m in range(2):
                            act.wait_ge(var3, g * 2 + m + 1)
                            act.activation(sd[:, m, :], mv3[:, m, :, 1], ACT.Sqrt,
                                           bias=eps_col[:, :]).then_inc(std3, 1)
                            act.wait_ge(normed_go, g * 2 + m + 1)
                            if m == 1:
                                act.wait_ge(saved3, g + 1)
                            for j in range(GROUP):
                                row = (acc[:, bass.ds(g * GROUP + j, 1), :].rearrange("p a d -> p (a d)") if m == 0
                                       else t1[:, j, :])
                                last = act.activation((t1, t2)[m][:, j, :], row, ACT.Identity,
                                                      scale=sc[:, m, 0, j:j + 1], bias=sc[:, m, 1, j:j + 1])
                            last.then_inc(normed, 1)
                        act.wait_ge(final3, g + 1)
                        act.copy(xn_all[:, bass.ds(g * GROUP, GROUP), :], t2[:, :, :])
                        act.wait_ge(turned3, g + 1)
                        for k in range(KC):
                            last = act.copy(xTg[:, k, :], psf[:, k * 1024:k * 1024 + GROUP * P])
                        last.then_inc(xT3, 1)
                        act.wait_ge(xT3, g + 1)
                        act.sem_inc(saved3, 1)
                    act.wait_ge(soft_in, 1)
                    act.activation(col3[:, 4, :], col3[:, 3, :], ACT.Exp).then_inc(soft_out, 1)

                @block.tensor
                def _(pe):
                    pe.sem_inc(saved3, 1)
                    pe.wait_ge(params_in, 7 * 16)
                    pe.transpose(ps[:, 7, 0:EXPERTS * HC], b1rows[:, :],
                                 ident[0:EXPERTS * HC, 0:EXPERTS * HC]).then_inc(b1_turned, 1)
                    with pe.Fori(0, GROUPS) as g:
                        pe.wait_ge(final3, g + 1)
                        for k in range(KC):
                            for j in range(GROUP):
                                last = pe.transpose(psf[:, k * 1024 + j * P:k * 1024 + (j + 1) * P],
                                                    t2[:, j, k * P:(k + 1) * P], ident[:, :])
                        last.then_inc(turned3, 1)
                        pe.wait_ge(xT3, g + 1)
                        pe.wait_ge(logits3, g + 1)
                        for j in range(GROUP):
                            for k in range(KC):
                                last = pe.matmul(ps[:, 4, j * EXPERTS:(j + 1) * EXPERTS],
                                                 xTg[:, k, j * P:(j + 1) * P], Wr_sb[:, k, :],
                                                 start=(k == 0), stop=(k == KC - 1))
                        last.then_inc(routed3, 1)
                    pe.wait_ge(both_ready, 1)
                    both = r["both"][:, :, :].rearrange("p w e -> p (w e)")
                    pe.matmul(ps[:, 5, 0:WINDOWS * EXPERTS], before[:, :], both, start=True, stop=True)
                    pe.matmul(ps[:, 6, 0:WINDOWS * EXPERTS], ones[:, :], both, start=True,
                              stop=True).then_inc(counts_up, 1)

            slot_ready, sent = sem3("slot_ready"), [sem3(f"sent{j}") for j in range(2 * GROUP)]
            with nc.Block() as block:
                @block.scalar
                def _(act):
                    with act.Fori(0, GROUPS) as g:
                        act.wait_ge(slots_free, g + 1)
                        act.copy(rows_slot[:, :, :], xn_all[:, bass.ds(g * GROUP, GROUP), :]).then_inc(slot_ready, 1)

                @block.vector
                def _(dve):
                    dve.sem_inc(slots_free, 1)
                    with dve.Fori(0, GROUPS) as g:
                        dve.tensor_copy(pos_slot[:, :, :],
                                        pos_k[:, :, bass.ds(g * GROUP, GROUP)]).then_inc(slot_ready, 1)
                        for j in range(2 * GROUP):
                            dve.wait_ge(sent[j], (g + 1) * 16)
                        dve.sem_inc(slots_free, 1)

                @block.gpsimd
                def _(pool):
                    pool.sem_inc(gated3, 1)
                    with pool.Fori(0, GROUPS) as g:
                        pool.wait_ge(slot_ready, (g + 1) * 2)
                        pool.wait_ge(gated3, g + 1)
                        nc.gpsimd.tensor_tensor(gate[:, 3:4], ones[:, 0:1], ones[:, 1:2], ALU.add).then_inc(gated3, 1)
                        for j in range(GROUP):
                            for k in range(2):
                                nc.gpsimd.indirect_dma_start(
                                    xs_dram, bass.IndirectOffsetOnAxis(ap=pos_slot[:, k, j:j + 1], axis=0),
                                    rows_slot[:, j, :], None).then_inc(sent[2 * j + k], 16)

        with ExitStack() as c4:
            def sb4(name, shape, dt=F32):
                return c4.enter_context(nc.sbuf_tensor(name, shape, dt))

            def sem4(name):
                return c4.enter_context(nc.semaphore(name))

            xrow = sb4("xrow", [P, 2, D])
            xTt = sb4("xTt", [P, 2, KC, P])
            hid = sb4("hid", [P, 2, H])
            hidT = sb4("hidT", [P, 2, HC, P])
            yrow = sb4("yrow", [P, 2, D])
            x_in4, x_turned4, xT4 = [sem4(f"x_in4_{s}") for s in range(2)], sem4("x_turned4"), sem4("xT4")
            x_free4 = sem4("x_free4")
            hid_up, hid_down, hid_turned, act_done = (sem4("hid_up"), sem4("hid_down"), sem4("hid_turned"),
                                                      sem4("act_done"))
            y_up, y_down, y_out = sem4("y_up"), sem4("y_down"), [sem4(f"y_out{s}") for s in range(2)]
            y_free = sem4("y_free")

            with nc.Block() as block:
                @block.sync
                def _(sp):
                    with sp.Fori(0, FTILES // 2) as i:
                        for s in range(2):
                            sp.wait_ge(x_turned4, i * 2 + s + 1)
                            sp.dma_start(xrow[:, s, :], xs_dram[bass.ds(i * 2 * P + s * P, P), :]
                                         ).then_inc(x_in4[s], 16)

                @block.gpsimd
                def _(pool):
                    pool.sem_inc(y_free, 2)
                    with pool.Fori(0, FTILES // 2) as i:
                        for s in range(2):
                            pool.wait_ge(y_out[s], (i + 1) * 16)
                            pool.sem_inc(y_free, 1)

                @block.scalar
                def _(act):
                    act.sem_inc(act_done, 2)
                    with act.Fori(0, FTILES // 2) as i:
                        experts = value(act, tile_expert[0:1, bass.ds(i * 2, 2)], EXPERTS - 1)
                        for s in range(2):
                            n = i * 2 + s
                            act.wait_ge(hid_turned, n + 1)
                            act.wait_ge(y_up, n + 1)
                            for k in range(HC):
                                last = act.activation(hidT[:, s, k, :], ps[:, 4 + s, k * P:(k + 1) * P], ACT.Gelu,
                                                      bias=b1T[:, bass.ds(experts[s] * HC + k, 1)])
                            last.then_inc(act_done, 1)
                            act.wait_ge(y_down, n + 3)
                            act.dma_start(ys_dram[bass.ds(n * P, P), :], yrow[:, s, :]).then_inc(y_out[s], 16)

                @block.vector
                def _(dve):
                    dve.sem_inc(xT4, 2)
                    dve.sem_inc(hid_down, 2)
                    dve.sem_inc(y_down, 2)
                    with dve.Fori(0, FTILES // 2) as i:
                        experts = value(dve, tile_expert[0:1, bass.ds(i * 2, 2)], EXPERTS - 1)
                        for s in range(2):
                            n = i * 2 + s
                            dve.wait_ge(x_turned4, n + 3)
                            dve.wait_ge(hid_up, n + 1)
                            dve.tensor_copy(xTt[:, s].rearrange("p c n -> p (c n)"),
                                            ps[:, s, 0:KC * P]).then_inc(xT4, 1)
                            dve.wait_ge(hid_up, n + 3)
                            dve.tensor_copy(hid[:, s, :], ps[:, 2 + s, :]).then_inc(hid_down, 1)
                            dve.wait_ge(y_up, n + 3)
                            dve.wait_ge(y_free, n + 1)
                            dve.tensor_tensor(yrow[:, s, :], ps[:, 6 + s, 0:D],
                                              b2_b[:, bass.ds(experts[s], 1), :].rearrange("p a d -> p (a d)"),
                                              ALU.add).then_inc(y_down, 1)

                @block.tensor
                def _(pe):
                    pe.sem_inc(x_turned4, 2)
                    pe.sem_inc(hid_up, 2)
                    pe.sem_inc(y_up, 2)
                    with pe.Fori(0, FTILES // 2) as i:
                        experts = value(pe, tile_expert[0:1, bass.ds(i * 2, 2)], EXPERTS - 1)
                        for s in range(2):
                            n = i * 2 + s
                            pe.wait_ge(x_in4[s], (i + 1) * 16)
                            pe.wait_ge(xT4, n + 1)
                            for k in range(KC):
                                last = pe.transpose(ps[:, s, k * P:(k + 1) * P], xrow[:, s, k * P:(k + 1) * P],
                                                    ident[:, :])
                            last.then_inc(x_turned4, 1)
                            pe.wait_ge(xT4, n + 3)
                            pe.wait_ge(hid_down, n + 1)
                            for k in range(KC):
                                last = pe.matmul(ps[:, 2 + s, :], xTt[:, s, k, :],
                                                 w1_sb[:, bass.ds(experts[s] * (KC * H) + k * H, H)],
                                                 start=(k == 0), stop=(k == KC - 1))
                            last.then_inc(hid_up, 1)
                            pe.wait_ge(hid_down, n + 3)
                            pe.wait_ge(act_done, n + 1)
                            for k in range(HC):
                                last = pe.transpose(ps[:, 4 + s, k * P:(k + 1) * P], hid[:, s, k * P:(k + 1) * P],
                                                    ident[:, :])
                            last.then_inc(hid_turned, 1)
                            pe.wait_ge(act_done, n + 3)
                            pe.wait_ge(y_down, n + 1)
                            for k in range(HC):
                                last = pe.matmul(ps[:, 6 + s, 0:D], hidT[:, s, k, :],
                                                 w2_sb[:, bass.ds(experts[s] * (HC * D) + k * D, D)],
                                                 start=(k == 0), stop=(k == HC - 1))
                            last.then_inc(y_up, 1)

        with ExitStack() as c5:
            def sb5(name, shape, dt=F32):
                return c5.enter_context(nc.sbuf_tensor(name, shape, dt))

            def sem5(name):
                return c5.enter_context(nc.semaphore(name))

            y_got = sb5("y_got", [P, 2, GROUP, D])
            pos_now = sb5("pos_now", [P, 2, GROUP], I32)
            slots5, gated5, added = sem5("slots5"), sem5("gated5"), sem5("added")
            got = [sem5(f"got{j}") for j in range(2 * GROUP)]
            stored = sem5("stored")
            with nc.Block() as block:
                @block.vector
                def _(dve):
                    dve.tensor_copy(pos_now[:, :, :], pos_k[:, :, 0:GROUP]).then_inc(slots5, 1)
                    with dve.Fori(0, GROUPS) as g:
                        for j in range(GROUP):
                            at = acc[:, bass.ds(g * GROUP + j, 1), :].rearrange("p a d -> p (a d)")
                            for k in range(2):
                                dve.wait_ge(got[2 * j + k], (g + 1) * 16)
                                dve.scalar_tensor_tensor(at, y_got[:, k, j, :],
                                                         weight_k[:, k, bass.ds(g * GROUP + j, 1)], at,
                                                         ALU.mult, ALU.add).then_inc(added, 1)
                                dve.wait_ge(added, g * (2 * GROUP) + 2 * j + k + 1)
                        dve.tensor_copy(pos_now[:, :, :],
                                        pos_k[:, :, bass.ds(g * GROUP + GROUP, GROUP)]).then_inc(slots5, 1)

                @block.gpsimd
                def _(pool):
                    pool.sem_inc(gated5, 1)
                    with pool.Fori(0, GROUPS) as g:
                        pool.wait_ge(slots5, g + 1)
                        pool.wait_ge(gated5, g + 1)
                        nc.gpsimd.tensor_tensor(gate[:, 3:4], ones[:, 0:1], ones[:, 1:2], ALU.add).then_inc(gated5, 1)
                        for j in range(GROUP):
                            for k in range(2):
                                nc.gpsimd.indirect_dma_start(
                                    y_got[:, k, j, :], None, ys_dram,
                                    bass.IndirectOffsetOnAxis(ap=pos_now[:, k, j:j + 1], axis=0)
                                ).then_inc(got[2 * j + k], 16)

                @block.sync
                def _(sp):
                    with sp.Fori(0, GROUPS - 1) as g:
                        sp.wait_ge(added, (g + 1) * (2 * GROUP))
                        sp.dma_start(out[bass.ds(g * (GROUP * P), GROUP * P), :].rearrange("(w p) d -> p w d", p=P),
                                     acc[:, bass.ds(g * GROUP, GROUP), :]).then_inc(stored, 16)
                    sp.wait_ge(added, GROUPS * 2 * GROUP)
                    lo = (GROUPS - 1) * GROUP
                    sp.dma_start(out[lo * P:(WINDOWS - 1) * P, :].rearrange("(w p) d -> p w d", p=P),
                                 acc[:, lo:WINDOWS - 1, :]).then_inc(stored, 16)
                    sp.dma_start(out[(WINDOWS - 1) * P:N, :], acc[0:TAIL, WINDOWS - 1, :]).then_inc(stored, 16)
                    sp.wait_ge(stored, (GROUPS + 1) * 16)


_INS = ['x', 'src', 'dst', 'edge_weight', 'L0_gnn_node_lock', 'L0_gnn_W', 'L0_gnn_b', 'L0_ffn_gamma', 'L0_ffn_beta',
        'L0_ffn_Wr', 'L0_ffn_br', 'L0_ffn_W1', 'L0_ffn_b1', 'L0_ffn_W2', 'L0_ffn_b2']


def kernel(**inputs):
    import numpy as _np
    import concourse.bacc as _bacc
    from concourse import mybir as _mybir
    from concourse.bass_utils import run_bass_kernel_spmd as _run

    nc = _bacc.Bacc("TRN2", target_bir_lowering=False, num_devices=1)
    arrays, args = {}, []
    for name in _INS:
        a = _np.ascontiguousarray(inputs[name])
        arrays[f"in_{name}_dram"] = a
        args.append(nc.dram_tensor(f"in_{name}_dram", a.shape, _mybir.dt.from_np(a.dtype), kind="ExternalInput").ap())
    args.append(nc.dram_tensor("out_0_dram", inputs['x'].shape, _mybir.dt.float32, kind="ExternalOutput").ap())
    gnn_moe_kernel(nc, *args)
    r = _run(nc, [arrays], core_ids=[0])
    return r.results[0]["out_0_dram"]
```

```python
from contextlib import ExitStack

import concourse.bass as bass
from concourse import mybir

ALU = mybir.AluOpType
ACT = mybir.ActivationFunctionType
AX = mybir.AxisListType
F32 = mybir.dt.float32
I32 = mybir.dt.int32
BF16 = mybir.dt.bfloat16

P = 128
GROUP = 7
HALF = 8
BATCH = 16
EPS = 1e-5
BIG = 65536.0


class Chain:

    def __init__(self, engine, sem, base=0):
        self.engine, self.sem, self.base, self.n = engine, sem, base, 0

    def __call__(self, instruction):
        self.n += 1
        instruction.then_inc(self.sem, 1)
        self.engine.wait_ge(self.sem, self.base + self.n)


def gnn_moe_kernel(nc, x, src, dst, edge_weight, node_lock, W, b, gamma, beta, Wr, br, W1, b1, W2, b2, out):
    N, D = x.shape
    E, = src.shape
    NLOCK, = node_lock.shape
    EXPERTS, _, H = W1.shape
    KC = D // P
    HC = H // P
    WINDOWS = -(-N // P)
    GROUPS = WINDOWS // GROUP
    TAIL = N - (WINDOWS - 1) * P
    DUMMY = WINDOWS
    SLOTS_W = WINDOWS + 1
    NOWHERE = SLOTS_W * P - 1
    TILES = -(-E // P)
    ROWGROUPS = -(-TILES // P)
    BATCHES = -(-TILES // BATCH)
    TCOLS = BATCHES * BATCH
    STEPS = 880
    assert STEPS >= TILES + WINDOWS and STEPS % (2 * HALF) == 0
    ITERS = STEPS // (2 * HALF)
    ROUNDS = -(-(TILES * WINDOWS) // STEPS)
    TAB = STEPS + 2 * HALF
    FTILES = 2 * WINDOWS + EXPERTS
    SLOT_TILES = FTILES + 2
    LTILES = -(-NLOCK // P)
    HROW = D + 1
    assert BATCHES % 2 == 0 and BATCHES > 6 * GROUPS and LTILES <= 8 and WINDOWS % GROUP == 0 and TILES < ROWGROUPS * P and FTILES % 2 == 0

    h_dram = nc.dram_tensor("h_rows", (WINDOWS * P, HROW), F32).ap()
    lock_dram = nc.dram_tensor("lock_row", (WINDOWS, P), F32).ap()
    xs_dram = nc.dram_tensor("slot_inputs", (SLOT_TILES * P, D), F32).ap()
    ys_dram = nc.dram_tensor("slot_outputs", (SLOT_TILES * P, D), F32).ap()

    with ExitStack() as ctx:
        def sb(name, shape, dt=F32):
            return ctx.enter_context(nc.sbuf_tensor(name, shape, dt))

        def sem(name):
            return ctx.enter_context(nc.semaphore(name))

        acc = sb("acc", [P, SLOTS_W, D])
        big = sb("big", [P, 2 * EXPERTS * KC * H])
        scratch = sb("scratch", [P, TCOLS * 4 + SLOTS_W * P + 5 * ROWGROUPS * P])
        ident = sb("ident", [P, P])
        ones = sb("ones", [P, P])
        before = sb("before", [P, P])
        iota_row = sb("iota_row", [P, TAB])
        pid = sb("pid", [P, 1])
        winlo = sb("winlo", [P, 2])
        thr = sb("thr", [P, 1])
        gate = sb("gate", [P, 4])
        eps_col = sb("eps_col", [P, 1])
        ntab = sb("ntab", [P, 8])
        rounds_i = sb("rounds_i", [P, 2], I32)
        ps = ctx.enter_context(nc.psum_tensor("ps", [P, 8, 512], F32))
        psf = ps[:, :, :].rearrange("p a b -> p (a b)")

        xnT = big[:, 0:KC * WINDOWS * P].rearrange("p (c n) -> p c n", c=KC)
        w1_sb = big[:, 0:EXPERTS * KC * H]
        w2_sb = big[:, EXPERTS * KC * H:]
        rec = scratch[:, 0:TCOLS * 4].rearrange("p (t c) -> p t c", c=4)
        lockrow = scratch[:, TCOLS * 4:TCOLS * 4 + SLOTS_W * P]
        tail_region = scratch[:, TCOLS * 4 + SLOTS_W * P:]

        with ExitStack() as c1:
            def sb1(name, shape, dt=F32):
                return c1.enter_context(nc.sbuf_tensor(name, shape, dt))

            def sem1(name):
                return c1.enter_context(nc.semaphore(name))

            RP = ROWGROUPS * P
            rows_i = tail_region[:, 0:2 * RP].bitcast(I32).rearrange("p (a g e) -> p a g e", a=2, e=P)
            rows_f = tail_region[:, 2 * RP:5 * RP].rearrange("p (a g e) -> p a g e", a=3, e=P)
            lock_i = sb1("lock_i", [8, P], I32)
            lock_f = sb1("lock_f", [8, P])
            spare = big[:, KC * WINDOWS * P:]
            wrow = lockrow[:, 3 * RP:3 * RP + KC * D].rearrange("p (c d) -> p c d", c=KC)
            WT = sb1("WT", [P, KC, D])
            srcI = lockrow[:, 3 * RP + KC * D:3 * RP + KC * D + TCOLS].bitcast(I32)
            absw = lockrow[:, 3 * RP + KC * D + TCOLS:3 * RP + KC * D + 2 * TCOLS]
            acol = sb1("acol", [P, TCOLS], BF16)
            bcol = sb1("bcol", [P, TCOLS], BF16)
            w_parts = sb1("w_parts", [P, 3, TCOLS], BF16)
            lockcol = sb1("lockcol", [P, 3, 8])
            lockcol_i = sb1("lockcol_i", [P, 8], I32)
            diag = lockrow[:, 0:2 * RP].rearrange("p (m g e) -> p m g e", m=2, g=ROWGROUPS)
            mnmx = sb1("mnmx", [P, 2, ROWGROUPS])
            cand = lockrow[:, 2 * RP:3 * RP]
            oneB = spare[:, 0:BATCH * P].bitcast(BF16).rearrange("p (s b t) -> p s b t", s=2, t=BATCH)
            oneA = sb1("oneA", [P, 2, WINDOWS, BATCH], BF16)
            partA = sb1("partA", [P, 2, 3, WINDOWS, BATCH], BF16)
            iota_t = sb1("iota_t", [P, P, BATCH], BF16)
            lockhist = sb1("lockhist", [P, P])
            norms = sb1("norms", [P, WINDOWS])
            small = sb1("small", [P, 16])

            cleared = sem1("cleared")
            consts = sem1("consts")
            src_in, dst_in, w_in = sem1("src_in"), sem1("dst_in"), sem1("w_in")
            lock_in, W_in, x_in = sem1("lock_in"), sem1("W_in"), sem1("x_in")
            rows_float = sem1("rows_float")
            diag_ready = sem1("diag_ready")
            turned = sem1("turned")
            rec_ready = sem1("rec_ready")
            ranges_up = sem1("ranges_up")
            steps_ready = sem1("steps_ready")
            prefix_ready = sem1("prefix_ready")
            v1 = sem1("v1")
            hist_cols = sem1("hist_cols")

            with nc.Block() as block:
                @block.gpsimd
                def _(pool):
                    nc.gpsimd.memset(rows_i[:, 0, ROWGROUPS - 1, :], 0)
                    nc.gpsimd.memset(rows_i[:, 1, ROWGROUPS - 1, :], NOWHERE)
                    nc.gpsimd.memset(rows_f[:, 2, ROWGROUPS - 1, :], 0.0)
                    nc.gpsimd.memset(lock_i[:, :], NOWHERE)
                    nc.gpsimd.memset(lockrow[:, DUMMY * P:], 0.0)
                    nc.gpsimd.memset(acc[:, WINDOWS - 1:SLOTS_W, :], 0.0).then_inc(cleared, 1)
                    nc.gpsimd.memset(ident[:, :], 0.0).then_inc(v1, 1)
                    nc.gpsimd.memset(ones[:, :], 1.0).then_inc(v1, 1)
                    nc.gpsimd.memset(eps_col[:, :], EPS)
                    nc.gpsimd.iota(iota_row[:, :], [[1, TAB]], base=0, channel_multiplier=0,
                                   allow_small_or_imprecise_dtypes=True)
                    nc.gpsimd.iota(pid[:, :], [[1, 1]], base=0, channel_multiplier=1,
                                   allow_small_or_imprecise_dtypes=True)
                    nc.gpsimd.iota(winlo[:, :], [[P, 2]], base=0, channel_multiplier=P,
                                   allow_small_or_imprecise_dtypes=True)
                    pool.wait_ge(v1, 2)
                    nc.gpsimd.affine_select(out=ident[:, :], in_=ident[:, :], compare_op=ALU.not_equal, fill=1.0,
                                            base=0, pattern=[[-1, P]], channel_multiplier=1)
                    nc.gpsimd.affine_select(out=before[:, :], in_=ones[:, :], compare_op=ALU.is_gt, fill=0.0,
                                            base=0, pattern=[[1, P]], channel_multiplier=-1).then_inc(consts, 1)

                @block.sync
                def _(sp):
                    full = (ROWGROUPS - 1) * P * P
                    whole = (TILES - 1) * P
                    rest = TILES - 1 - (ROWGROUPS - 1) * P
                    sp.wait_ge(cleared, 1)
                    for a, (dram, rows, landed) in enumerate(((dst, rows_i[:, 1], dst_in), (src, rows_i[:, 0], src_in),
                                                              (edge_weight, rows_f[:, 2], w_in))):
                        sp.dma_start(rows[:, 0:ROWGROUPS - 1, :],
                                     dram[0:full].rearrange("(g t e) -> t g e", t=P, e=P)).then_inc(landed, 16)
                        sp.dma_start(rows[0:rest, ROWGROUPS - 1, :],
                                     dram[full:whole].rearrange("(t e) -> t e", e=P)).then_inc(landed, 16)
                        sp.dma_start(rows[rest:rest + 1, ROWGROUPS - 1, 0:E - whole],
                                     dram[whole:E].rearrange("(a e) -> a e", a=1)).then_inc(landed, 16)
                    lw = (LTILES - 1) * P
                    sp.dma_start(lock_i[0:LTILES - 1, :],
                                 node_lock[0:lw].rearrange("(t e) -> t e", e=P)).then_inc(lock_in, 16)
                    sp.dma_start(lock_i[LTILES - 1:LTILES, 0:NLOCK - lw],
                                 node_lock[lw:NLOCK].rearrange("(a e) -> a e", a=1)).then_inc(lock_in, 16)
                    sp.dma_start(wrow[:, :, :], W.rearrange("(c o) k -> o c k", o=P)).then_inc(W_in, 16)
                    step = (WINDOWS - 1) // 4
                    for q in range(4):
                        sp.dma_start(acc[:, q * step:(q + 1) * step, :],
                                     x[q * step * P:(q + 1) * step * P, :].rearrange("(w p) d -> p w d", p=P)
                                     ).then_inc(x_in, 16)
                    sp.dma_start(acc[0:TAIL, WINDOWS - 1, :], x[(WINDOWS - 1) * P:N, :]).then_inc(x_in, 16)

                @block.tensor
                def _(pe):
                    pe.wait_ge(consts, 1)
                    for a, ready in ((0, 2), (1, 1), (2, 0)):
                        if a < 2:
                            pe.wait_ge(rows_float, ready)
                        else:
                            pe.wait_ge(w_in, 48)
                        for g in range(ROWGROUPS):
                            last = pe.transpose(psf[:, a * 1024 + g * P:a * 1024 + (g + 1) * P],
                                                rows_f[:, a, g, :], ident[:, :])
                        last.then_inc(turned, 1)
                    pe.wait_ge(rows_float, 3)
                    pe.transpose(ps[:, 6, 0:8], lock_f[:, :], ident[0:8, 0:8]).then_inc(turned, 1)
                    pe.wait_ge(W_in, 16)
                    for k in range(KC):
                        for o in range(KC):
                            last = pe.transpose(ps[:, 7, k * D + o * P:k * D + (o + 1) * P],
                                                wrow[:, o, k * P:(k + 1) * P], ident[:, :])
                    last.then_inc(turned, 1)
                    pe.wait_ge(diag_ready, 1)
                    pe.wait_ge(rec_ready, 2)
                    for m in range(2):
                        for g in range(ROWGROUPS):
                            last = pe.matmul(psf[0:SLOTS_W, m * 1024 + g * P:m * 1024 + (g + 1) * P],
                                             ones[:, 0:SLOTS_W], diag[:, m, g, :], start=True, stop=True)
                    last.then_inc(ranges_up, 1)
                    pe.wait_ge(steps_ready, 1)
                    pe.matmul(ps[0:SLOTS_W, 4, 0:1], before[0:SLOTS_W, 0:SLOTS_W], ntab[0:SLOTS_W, 2:3],
                              start=True, stop=True)
                    pe.matmul(ps[:, 4, 2:3], ones[0:SLOTS_W, :], ntab[0:SLOTS_W, 2:3],
                              start=True, stop=True).then_inc(prefix_ready, 1)

                @block.vector
                def _(dve):
                    chain = Chain(dve, hist_cols)
                    dve.wait_ge(dst_in, 48)
                    dve.tensor_copy(rows_f[:, 1], rows_i[:, 1]).then_inc(rows_float, 1)
                    dve.wait_ge(src_in, 48)
                    dve.tensor_copy(rows_f[:, 0], rows_i[:, 0]).then_inc(rows_float, 1)
                    dve.wait_ge(lock_in, 32)
                    dve.tensor_copy(lock_f[:, :], lock_i[:, :]).then_inc(rows_float, 1)
                    dve.wait_ge(rows_float, 3)
                    chain(dve.tensor_reduce(mnmx[:, 0, :], rows_f[:, 1], AX.X, ALU.min))
                    chain(dve.tensor_reduce(mnmx[:, 1, :], rows_f[:, 1], AX.X, ALU.max))
                    dve.wait_ge(consts, 1)
                    for m in range(2):
                        for g in range(ROWGROUPS):
                            last = dve.tensor_scalar(diag[:, m, g, :], ident[:, :], mnmx[:, m, g:g + 1], None, ALU.mult)
                    last.then_inc(diag_ready, 1)
                    dve.wait_ge(turned, 1)
                    dve.tensor_copy(rec[:, :, 0], psf[:, 0:TCOLS]).then_inc(rec_ready, 1)
                    dve.wait_ge(turned, 2)
                    dve.tensor_copy(rec[:, :, 1], psf[:, 1024:1024 + TCOLS]).then_inc(rec_ready, 1)
                    dve.wait_ge(turned, 3)
                    dve.tensor_copy(rec[:, :, 2], psf[:, 2048:2048 + TCOLS]).then_inc(rec_ready, 1)
                    dve.wait_ge(turned, 4)
                    dve.tensor_copy(lockcol[:, 0, :], ps[:, 6, 0:8]).then_inc(rec_ready, 1)
                    dve.wait_ge(turned, 5)
                    dve.tensor_copy(WT[:, :, :], ps[:, 7, :].rearrange("p (c o) -> p c o", c=KC)).then_inc(rec_ready, 1)
                    dve.wait_ge(rec_ready, 5)
                    chain(dve.tensor_copy(srcI[:, :], rec[:, :, 0]))
                    chain(dve.tensor_scalar(srcI[:, :], srcI[:, :], 7, None, ALU.arith_shift_right))
                    chain(dve.tensor_copy(acol[:, :], srcI[:, :]))
                    chain(dve.scalar_tensor_tensor(bcol[:, :], acol[:, :], float(-P), rec[:, :, 0], ALU.mult, ALU.add))
                    chain(dve.scalar_tensor_tensor(absw[:, :], rec[:, :, 2], -1.0, rec[:, :, 2], ALU.mult, ALU.max))
                    for part in range(3):
                        chain(dve.tensor_copy(w_parts[:, part, :], absw[:, :]))
                        if part < 2:
                            chain(dve.tensor_tensor(absw[:, :], absw[:, :], w_parts[:, part, :], ALU.subtract))
                    chain(dve.tensor_tensor(rec[:, :, 3], rec[:, :, 0], rec[:, :, 1], ALU.is_equal))
                    chain(dve.tensor_copy(lockcol_i[:, :], lockcol[:, 0, :]))
                    chain(dve.tensor_scalar(lockcol_i[:, :], lockcol_i[:, :], 7, None, ALU.arith_shift_right))
                    chain(dve.tensor_copy(lockcol[:, 1, :], lockcol_i[:, :]))
                    chain(dve.scalar_tensor_tensor(lockcol[:, 2, :], lockcol[:, 1, :], float(-P), lockcol[:, 0, :],
                                                   ALU.mult, ALU.add))
                    dve.wait_ge(ranges_up, 1)
                    wn = slice(0, SLOTS_W)
                    chain(dve.tensor_scalar(cand[wn, 0:TILES], psf[wn, 1024:1024 + TILES], winlo[wn, 0:1], BIG,
                                            ALU.is_lt, ALU.mult))
                    chain(dve.tensor_tensor(cand[wn, 0:TILES], cand[wn, 0:TILES], iota_row[wn, 0:TILES], ALU.add))
                    chain(dve.tensor_reduce(ntab[wn, 0:1], cand[wn, 0:TILES], AX.X, ALU.min))
                    chain(dve.tensor_scalar(ntab[wn, 0:1], ntab[wn, 0:1], float(TILES), None, ALU.min))
                    chain(dve.scalar_tensor_tensor(cand[wn, 0:TILES], psf[wn, 0:TILES], winlo[wn, 1:2],
                                                   iota_row[wn, 1:TILES + 1], ALU.is_lt, ALU.mult))
                    chain(dve.tensor_reduce(ntab[wn, 1:2], cand[wn, 0:TILES], AX.X, ALU.max))
                    chain(dve.tensor_tensor(small[wn, 0:1], ntab[wn, 1:2], ntab[wn, 0:1], ALU.subtract))
                    chain(dve.tensor_scalar(small[wn, 1:2], pid[wn, :], float(WINDOWS), None, ALU.is_lt))
                    chain(dve.tensor_scalar(ntab[wn, 2:3], small[wn, 0:1], 0.0, small[wn, 1:2], ALU.max, ALU.mult))
                    dve.sem_inc(steps_ready, 1)
                    dve.wait_ge(prefix_ready, 1)
                    chain(dve.tensor_copy(ntab[wn, 3:4], ps[wn, 4, 0:1]))
                    chain(dve.tensor_tensor(ntab[wn, 4:5], ntab[wn, 3:4], ntab[wn, 2:3], ALU.add))
                    chain(dve.tensor_tensor(ntab[wn, 5:6], ntab[wn, 0:1], ntab[wn, 3:4], ALU.subtract))
                    chain(dve.tensor_scalar(ntab[wn, 6:7], pid[wn, :], float(-DUMMY), None, ALU.add))
                    chain(dve.tensor_copy(small[:, 2:3], ps[:, 4, 2:3]))
                    chain(dve.tensor_scalar(cand[:, 0:ROUNDS], iota_row[:, 0:ROUNDS], float(STEPS), small[:, 2:3],
                                            ALU.mult, ALU.is_lt))
                    chain(dve.tensor_reduce(small[:, 3:4], cand[:, 0:ROUNDS], AX.X, ALU.add))
                    chain(dve.tensor_scalar(rounds_i[:, 0:1], small[:, 3:4], 1.0, None, ALU.max))

            xn = tail_region[:, 0:GROUP * D].rearrange("p (w d) -> p w d", w=GROUP)
            std = sb1("std", [P, GROUP])
            var_ready, std_ready = sem1("var_ready"), sem1("std_ready")
            sums_ready, norms_ready = sem1("sums_ready"), sem1("norms_ready")
            stats = sb1("stats", [P, GROUP, 6])
            mv = sb1("mv", [P, GROUP, 2])
            rstd = sb1("rstd", [P, GROUP, 1])
            junk = sb1("junk", [P, D])
            junk_rows = lockrow[:, 0:GROUP * P]
            colsq = sb1("colsq", [P, KC, GROUPS])
            col = sb1("col", [P, 8, KC])
            prune = tail_region[:, 0:2 * KC * D].rearrange("p (m c d) -> p m c d", m=2, c=KC)
            xT = sb1("xT", [P, 2, KC, P])
            hrow = tail_region[:, GROUP * D:GROUP * (D + HROW)].rearrange("p (w d) -> p w d", w=GROUP)
            nsq = sb1("nsq", [P, GROUP])
            xn_ready, xn_turned, xT_saved = sem1("xn_ready"), sem1("xn_turned"), sem1("xT_saved")
            colsum_ready = sem1("colsum_ready")
            v2, v3, v4 = sem1("v2"), sem1("v3"), sem1("v4")
            colsq_ready = sem1("colsq_ready")
            total_ready = sem1("total_ready")
            W_ready = sem1("W_ready")
            one_hots_ready, A_eq, hist_done = sem1("one_hots_ready"), sem1("A_eq"), sem1("hist_done")
            iota_ready = sem1("iota_ready")
            lockB = sem1("lockB")
            lock_up, lock_out, lock_back = sem1("lock_up"), sem1("lock_out"), sem1("lock_back")
            xT_slot, h_up, h_down, h_norm, h_out = (sem1("xT_slot"), sem1("h_up"), sem1("h_down"), sem1("h_norm"),
                                                    sem1("h_out"))
            h_free = sem1("h_free")
            sum_up, thr_up = sem1("sum_up"), sem1("thr_up")
            zero_mm = sb1("zero_mm", [P, 3 * WINDOWS], BF16)
            zero_set = sem1("zero_set")

            with nc.Block() as block:
                @block.vector
                def _(dve):
                    chain = Chain(dve, v3)
                    chain(dve.memset(zero_mm[:, :], 0.0))
                    chain(dve.tensor_tensor(oneB[:, 0, :, 0:8], iota_row[:, 0:P].unsqueeze(2).to_broadcast([P, P, 8]),
                                            lockcol[:, 2, :].unsqueeze(1).to_broadcast([P, P, 8]), ALU.is_equal))
                    chain(dve.tensor_tensor(oneA[:, 0, :, 0:8],
                                            iota_row[:, 0:WINDOWS].unsqueeze(2).to_broadcast([P, WINDOWS, 8]),
                                            lockcol[:, 1, :].unsqueeze(1).to_broadcast([P, WINDOWS, 8]),
                                            ALU.is_equal))
                    dve.sem_inc(lockB, 1)
                    dve.wait_ge(lock_up, 1)
                    chain(dve.tensor_scalar(lockhist[0:WINDOWS, :], ps[0:WINDOWS, 6, 0:P], 1.0, None, ALU.min))
                    dve.sem_inc(lock_up, 1)

                    def one_hots(at, s, n):
                        across = lambda ap, m: ap.unsqueeze(1).to_broadcast([P, m, BATCH])
                        dve.wait_ge(hist_done, n + 1)
                        dve.tensor_tensor(oneB[:, s], iota_t[:, :, :], across(bcol[:, bass.ds(at, BATCH)], P),
                                          ALU.is_equal)
                        dve.tensor_tensor(oneA[:, s], iota_t[:, 0:WINDOWS, :],
                                          across(acol[:, bass.ds(at, BATCH)], WINDOWS),
                                          ALU.is_equal).then_inc(A_eq, 1)
                        dve.wait_ge(A_eq, n + 1)
                        dve.tensor_tensor(partA[:, s], oneA[:, s].unsqueeze(1).to_broadcast([P, 3, WINDOWS, BATCH]),
                                          w_parts[:, :, bass.ds(at, BATCH)].unsqueeze(2)
                                          .to_broadcast([P, 3, WINDOWS, BATCH]), ALU.mult).then_inc(one_hots_ready, 1)

                    dve.wait_ge(iota_ready, 1)
                    dve.wait_ge(x_in, 80)
                    with dve.Fori(0, GROUPS) as g:
                        c = Chain(dve, v2, g * 3)
                        for j in range(GROUP):
                            last = dve.bn_stats(stats[:, j, :], acc[:, bass.ds(g * GROUP + j, 1), :]
                                                .rearrange("p a d -> p (a d)"))
                        c(last)
                        dve.memset(gate[:, 0:1], 0.0)
                        for j in range(GROUP):
                            last = dve.bn_aggr(mv[:, j, :], stats[:, j, :])
                        c(last)
                        dve.sem_inc(var_ready, 1)
                        one_hots(g * (2 * BATCH), 0, g * 2)
                        dve.wait_ge(std_ready, g + 1)
                        c(dve.reciprocal(rstd[:, :, 0], std[:, :]))
                        for j in range(GROUP):
                            if j == 0:
                                dve.wait_ge(xn_turned, g * GROUP + GROUP)
                            dve.tensor_scalar(xn[:, j, :], acc[:, bass.ds(g * GROUP + j, 1), :]
                                              .rearrange("p a d -> p (a d)"), mv[:, j, 0:1], rstd[:, j, :],
                                              ALU.subtract, ALU.mult).then_inc(xn_ready, 1)
                        one_hots(g * (2 * BATCH) + BATCH, 1, g * 2 + 1)
                    chain = Chain(dve, v4)
                    dve.wait_ge(colsq_ready, KC * GROUPS)
                    chain(dve.tensor_reduce(col[:, 0, :], colsq[:, :, :], AX.X, ALU.add))
                    dve.sem_inc(colsum_ready, 1)
                    dve.wait_ge(total_ready, 1)
                    chain(dve.tensor_reduce(col[:, 1, 0:1], ps[:, 7, 0:KC], AX.X, ALU.add))
                    dve.sem_inc(sums_ready, 1)
                    dve.wait_ge(norms_ready, 1)
                    chain(dve.reciprocal(col[:, 3, :], col[:, 2, :]))
                    chain(dve.tensor_scalar(col[:, 1, 0:1], col[:, 6, 1:2], 1.0 / D, None, ALU.mult))
                    chain(dve.tensor_scalar(col[:, 4, 0:1], col[:, 1, 0:1], 0.1, None, ALU.mult))
                    chain(dve.tensor_scalar(col[:, 5, :], col[:, 3, :], col[:, 4, 0:1], None, ALU.mult))
                    chain(dve.tensor_scalar(col[:, 6, 0:1], col[:, 1, 0:1], 1e-8, None, ALU.is_gt))
                    chain(dve.scalar_tensor_tensor(prune[:, 0], WT[:, :, :], -1.0, WT[:, :, :], ALU.mult, ALU.max))
                    for k in range(KC):
                        chain(dve.tensor_scalar(prune[:, 1, k, :], prune[:, 0, k, :], col[:, 5, k:k + 1],
                                                col[:, 6, 0:1], ALU.is_lt, ALU.mult))
                    chain(dve.tensor_tensor(prune[:, 0], prune[:, 1], WT[:, :, :], ALU.mult))
                    chain(dve.tensor_tensor(WT[:, :, :], WT[:, :, :], prune[:, 0], ALU.subtract))
                    dve.sem_inc(W_ready, 1)
                    with dve.Fori(0, (BATCHES - 2 * GROUPS) // 2) as i:
                        for s in range(2):
                            one_hots((i * 2 + (s + 2 * GROUPS)) * BATCH, s, i * 2 + (s + 2 * GROUPS))
                    chain2 = Chain(dve, rows_float, 3)
                    dve.wait_ge(h_down, GROUPS)
                    dve.wait_ge(hist_done, BATCHES + 3)
                    chain2(dve.tensor_tensor(junk[:, 0:3 * WINDOWS].rearrange("p (a w) -> p a w", a=3),
                                             ps[:, 5, 0:3 * WINDOWS].rearrange("p (a w) -> p a w", a=3),
                                             norms[:, :].unsqueeze(1).to_broadcast([P, 3, WINDOWS]), ALU.mult))
                    chain2(dve.tensor_reduce(col[:, 7, 0:1], junk[:, 0:3 * WINDOWS], AX.X, ALU.add))
                    dve.sem_inc(sum_up, 1)
                    dve.wait_ge(thr_up, 1)
                    chain2(dve.tensor_scalar(thr[:, :], ps[:, 7, 4:5], 1.0 / E, 0.1, ALU.mult, ALU.mult))

                @block.tensor
                def _(pe):
                    pe.sem_inc(xn_turned, GROUP)
                    pe.sem_inc(h_up, 1)
                    pe.sem_inc(hist_done, 2)
                    pe.wait_ge(lockB, 1)
                    for t in range(8):
                        last = pe.matmul(ps[0:WINDOWS, 6, 0:P], oneA[:, 0, :, t], oneB[:, 0, :, t],
                                         start=(t == 0), stop=(t == 7))
                    last.then_inc(lock_up, 1)
                    pe.matmul(ps[:, 5, 0:3 * WINDOWS], zero_mm[:, 0:P], zero_mm[:, :], start=True,
                              stop=False, skip_group_check=True)

                    def histogram(n, s):
                        pe.wait_ge(one_hots_ready, n + 1)
                        for t in range(BATCH):
                            last = pe.matmul(ps[:, 5, 0:3 * WINDOWS], oneB[:, s, :, t],
                                             partA[:, s, :, :, t].rearrange("p a w -> p (a w)"),
                                             start=False, stop=False, skip_group_check=True)
                        last.then_inc(hist_done, 1)

                    with pe.Fori(0, GROUPS) as g:
                        histogram(g * 2, 0)
                        for j in range(GROUP):
                            pe.wait_ge(xn_ready, g * GROUP + j + 1)
                            if j == 0:
                                pe.wait_ge(xT_saved, g * KC + KC)
                            for k in range(KC):
                                last = pe.transpose(psf[:, k * 1024 + j * P:k * 1024 + (j + 1) * P],
                                                    xn[:, j, k * P:(k + 1) * P], ident[:, :])
                            last.then_inc(xn_turned, 1)
                        histogram(g * 2 + 1, 1)
                    pe.wait_ge(colsum_ready, 1)
                    pe.matmul(ps[:, 7, 0:KC], ones[:, :], col[:, 0, :], start=True, stop=True).then_inc(total_ready, 1)
                    pe.wait_ge(W_ready, 1)
                    with pe.Fori(0, GROUPS) as g:
                        for j in range(GROUP):
                            pe.wait_ge(xT_slot, g * GROUP + j + 1)
                            if j >= 2:
                                pe.wait_ge(h_norm, g * GROUP + j + 1)
                            else:
                                pe.wait_ge(h_norm, g * GROUP + 2)
                            for k in range(KC):
                                last = pe.matmul(ps[:, 2 + j % 2, 0:D], xT[:, j % 2, k, :], WT[:, k, :],
                                                 start=(k == 0), stop=(k == KC - 1))
                            last.then_inc(h_up, 1)
                            if j in (1, 3, 5, 6):
                                at = (1, 3, 5, 6).index(j)
                                histogram(g * 4 + (2 * GROUPS + at), at % 2)
                    with pe.Fori(0, (BATCHES - 6 * GROUPS) // 2) as i:
                        for s in range(2):
                            histogram(i * 2 + (6 * GROUPS + s), s)
                    pe.matmul(ps[:, 5, 0:3 * WINDOWS], zero_mm[:, 0:P], zero_mm[:, :], start=False,
                              stop=True, skip_group_check=True).then_inc(hist_done, 1)
                    pe.wait_ge(sum_up, 1)
                    pe.matmul(ps[:, 7, 4:5], ones[:, :], col[:, 7, 0:1], start=True, stop=True).then_inc(thr_up, 1)

                @block.scalar
                def _(act):
                    act.copy(iota_t[:, :, :], iota_row[:, 0:P].unsqueeze(2).to_broadcast([P, P, BATCH])
                             ).then_inc(iota_ready, 1)
                    act.sem_inc(xT_saved, KC)
                    act.sem_inc(h_norm, 2)
                    with act.Fori(0, GROUPS) as g:
                        act.wait_ge(var_ready, g + 1)
                        act.activation(std[:, :], mv[:, :, 1], ACT.Sqrt, bias=eps_col[:, :]).then_inc(std_ready, 1)
                        act.wait_ge(xn_turned, (g + 2) * GROUP)
                        for k in range(KC):
                            act.copy(xnT[:, k, bass.ds(g * GROUP * P, GROUP * P)],
                                     psf[:, k * 1024:k * 1024 + GROUP * P])
                            act.activation(junk_rows[:, :], psf[:, k * 1024:k * 1024 + GROUP * P], ACT.Square,
                                           accum_out=colsq[:, k, bass.ds(g, 1)]).then_inc(xT_saved, 1)
                            act.wait_ge(xT_saved, g * KC + k + 1 + KC)
                    act.sem_inc(colsq_ready, KC * GROUPS)
                    act.wait_ge(sums_ready, 1)
                    act.activation(col[:, 2, :], col[:, 0, :], ACT.Sqrt)
                    act.activation(col[:, 6, 1:2], col[:, 1, 0:1], ACT.Sqrt).then_inc(norms_ready, 1)
                    with act.Fori(0, GROUPS) as g:
                        for j in range(GROUP):
                            act.wait_ge(h_up, g * GROUP + max(j - 1, 0) + 1)
                            act.copy(xT[:, j % 2], xnT[:, :, bass.ds((g * GROUP + j) * P, P)]).then_inc(xT_slot, 1)
                            act.wait_ge(h_up, g * GROUP + j + 2)
                            if j == 0:
                                act.wait_ge(h_free, g + 1)
                            act.copy(hrow[:, j, 0:D], ps[:, 2 + j % 2, 0:D])
                            act.activation(junk[:, 0:D], ps[:, 2 + j % 2, 0:D], ACT.Square,
                                           accum_out=nsq[:, j:j + 1]).then_inc(h_norm, 1)
                            act.wait_ge(h_norm, g * GROUP + j + 3)
                        act.activation(norms[:, bass.ds(g * GROUP, GROUP)], nsq[:, :], ACT.Sqrt)
                        act.activation(hrow[:, :, D], nsq[:, :], ACT.Sqrt).then_inc(h_down, 1)

                @block.sync
                def _(sp):
                    sp.wait_ge(lock_up, 2)
                    sp.dma_start(lock_dram, lockhist[0:WINDOWS, :]).then_inc(lock_out, 16)
                    sp.wait_ge(lock_out, 16)
                    sp.wait_ge(W_ready, 1)
                    sp.dma_start(lockrow[:, 0:WINDOWS * P],
                                 lock_dram.rearrange("(a w) e -> a (w e)", a=1).to_broadcast([P, WINDOWS * P])
                                 ).then_inc(lock_back, 16)
                    sp.sem_inc(h_free, 1)
                    with sp.Fori(0, GROUPS) as g:
                        sp.wait_ge(h_down, g + 1)
                        sp.dma_start(h_dram[bass.ds(g * (GROUP * P), GROUP * P), :]
                                     .rearrange("(w p) d -> p w d", p=P), hrow[:, :, :]).then_inc(h_out, 16)
                        sp.wait_ge(h_out, (g + 1) * 16)
                        sp.sem_inc(h_free, 1)
                    sp.wait_ge(h_out, GROUPS * 16)
                    sp.wait_ge(lock_back, 16)

        with ExitStack() as c2:
            def sb2(name, shape, dt=F32):
                return c2.enter_context(nc.sbuf_tensor(name, shape, dt))

            def sem2(name):
                return c2.enter_context(nc.semaphore(name))

            tile_tab = sb2("tile_tab", [P, TAB], I32)
            win_tab = sb2("win_tab", [P, TAB], I32)
            win_base = sb2("win_base", [P, TAB])
            terms = sb2("terms", [P, 3, TAB])
            bounds = sb2("bounds", [P, 8])
            zeros = sb2("zeros", [P, D])
            recs = sb2("recs", [P, 2, HALF, 4])
            src_idx = sb2("src_idx", [P, 2, HALF], I32)
            coef = sb2("coef", [P, 2, 8, HALF])
            keepw = sb2("keepw", [P, 2, HALF, P])
            S = sb2("S", [P, 4, P])
            G = tail_region[:, 0:2 * HALF * HROW].rearrange("p (s u d) -> p s u d", s=2, u=HALF)
            TH = TAB // 2

            terms_ready, tab_up, tab_ready = sem2("terms_ready"), sem2("tab_up"), sem2("tab_ready")
            tv = sem2("tv")
            recs_ready, idx_ready = sem2("recs_ready"), sem2("idx_ready")
            gathered = [sem2(f"gathered{k}") for k in range(2 * HALF)]
            cv, coef_ready, keep_ready = sem2("cv"), sem2("coef_ready"), sem2("keep_ready")
            S_ready, messages_up, acc_done = sem2("S_ready"), sem2("messages_up"), sem2("acc_done")
            gated, half_in = sem2("gated"), sem2("half_in")
            zeros_set, zeroed, weights_in = sem2("zeros_set"), sem2("zeroed"), sem2("weights_in")

            def value(engine, ap, top):
                _, values = nc.values_load_multi_w_load_instructions(
                    ap, engines=[engine.engine], min_val=0, max_val=top,
                    skip_runtime_bounds_check_because="the tables hold tile and window numbers only")
                return values

            with nc.Block() as block:
                @block.sync
                def _(sp):
                    sp.dma_start(w1_sb.rearrange("p (a h) -> p a h", h=H),
                                 W1.rearrange("e (c k) h -> k (e c) h", k=P)).then_inc(weights_in, 16)
                    sp.dma_start(w2_sb.rearrange("p (a d) -> p a d", d=D),
                                 W2.rearrange("e (c k) d -> k (e c) d", k=P)).then_inc(weights_in, 16)
                    sp.wait_ge(zeros_set, 1)
                    for lo in range(0, SLOT_TILES, 27):
                        n = min(27, SLOT_TILES - lo)
                        sp.dma_start(xs_dram[lo * P:(lo + n) * P, :].rearrange("(t p) d -> p t d", p=P),
                                     zeros[:, :].unsqueeze(1).to_broadcast([P, n, D])).then_inc(zeroed, 16)
                    for t in range(FTILES, SLOT_TILES):
                        sp.dma_start(ys_dram[t * P:(t + 1) * P, :], zeros[:, :]).then_inc(zeroed, 16)
                    sp.wait_ge(zeroed, 16 * (-(-SLOT_TILES // 27) + 2))
                    sp.wait_ge(weights_in, 32)
                    rounds = sp.value_load(rounds_i[0:1, 0:1], min_val=1, max_val=ROUNDS)
                    with sp.Fori(0, rounds) as r:
                        with sp.Fori(0, ITERS) as i:
                            for s in range(2):
                                for u in range(HALF):
                                    sp.wait_ge(gathered[s * HALF + u], (r * ITERS + i) * 16 + 16)
                                sp.sem_inc(half_in, 1)
                    sp.sem_inc(half_in, 1)

                @block.gpsimd
                def _(pool):
                    pool.sem_inc(gated, 1)
                    nc.gpsimd.memset(zeros[:, :], 0.0).then_inc(zeros_set, 1)
                    pool.wait_ge(zeros_set, 1)
                    rounds = pool.value_load(rounds_i[0:1, 0:1], min_val=1, max_val=ROUNDS)
                    with pool.Fori(0, rounds) as r:
                        with pool.Fori(0, ITERS) as i:
                            for s in range(2):
                                half = r * (2 * ITERS) + i * 2 + s
                                pool.wait_ge(idx_ready, half + 1)
                                for quad in range(2):
                                    pool.wait_ge(messages_up, half * HALF + (quad + 1) * (HALF // 2))
                                    pool.wait_ge(gated, half * 2 + (quad + 1))
                                    nc.gpsimd.tensor_tensor(gate[:, 0:1], zeros[:, 0:1], zeros[:, 1:2],
                                                            ALU.add).then_inc(gated, 1)
                                    for u in range(quad * (HALF // 2), (quad + 1) * (HALF // 2)):
                                        nc.gpsimd.indirect_dma_start(
                                            G[:, s, u, :], None, h_dram,
                                            bass.IndirectOffsetOnAxis(ap=src_idx[:, s, u:u + 1], axis=0)
                                        ).then_inc(gathered[s * HALF + u], 16)

                @block.scalar
                def _(act):
                    def fetch(s, tiles, half):
                        for u in range(HALF):
                            last = act.copy(recs[:, s, u, :], rec[:, bass.ds(tiles[u], 1), :]
                                            .rearrange("p a c -> p (a c)"))
                        last.then_inc(recs_ready, 1)
                        act.wait_ge(recs_ready, half + 1)
                        act.copy(src_idx[:, s, :], recs[:, s, :, 0]).then_inc(idx_ready, 1)

                    def tiles_at(at):
                        return value(act, tile_tab[0:1, bass.ds(at, HALF)], TILES - 1)

                    act.wait_ge(tab_ready, 1)
                    for s in range(2):
                        fetch(s, tiles_at(s * HALF), s)
                    rounds = act.value_load(rounds_i[0:1, 0:1], min_val=1, max_val=ROUNDS)
                    with act.Fori(0, rounds) as r:
                        act.wait_ge(tab_ready, r + 1)
                        with act.Fori(0, ITERS) as i:
                            for s in range(2):
                                half = r * (2 * ITERS) + i * 2 + s
                                tiles = tiles_at((i * 2 + s + 2) * HALF)
                                wins = value(act, win_tab[0:1, bass.ds((i * 2 + s) * HALF, HALF)], DUMMY)
                                act.wait_ge(coef_ready, half + 1)
                                act.wait_ge(S_ready, half * HALF + HALF)
                                for u in range(HALF):
                                    if u == HALF // 2:
                                        fetch(s, tiles, half + 2)
                                    act.activation(keepw[:, s, u, :], lockrow[:, bass.ds(wins[u] * P, P)],
                                                   ACT.Identity, scale=coef[:, s, 5, u:u + 1],
                                                   bias=coef[:, s, 4, u:u + 1]).then_inc(keep_ready, 1)

                @block.tensor
                def _(pe):
                    pe.sem_inc(messages_up, 16)
                    rounds = pe.value_load(rounds_i[0:1, 0:1], min_val=1, max_val=ROUNDS)

                    def tables_up(r):
                        pe.wait_ge(terms_ready, r + 1)
                        for m in range(2):
                            for q in range(2):
                                last = pe.matmul(ps[:, 2 * m + q, 0:TH], ones[0:SLOTS_W, :],
                                                 terms[0:SLOTS_W, 1 + m, q * TH:(q + 1) * TH], start=True, stop=True)
                        last.then_inc(tab_up, 1)

                    tables_up(0)
                    with pe.Fori(0, rounds) as r:
                        with pe.Fori(0, ITERS) as i:
                            for s in range(2):
                                for u in range(HALF):
                                    step = (r * (2 * ITERS) + i * 2 + s) * HALF + u
                                    pe.wait_ge(S_ready, step + 17)
                                    pe.wait_ge(acc_done, step + 1)
                                    pe.matmul(ps[:, 4 + u % 4, 0:D], S[:, u % 4, :], G[:, s, u, 0:D],
                                              start=True, stop=True).then_inc(messages_up, 1)
                        tables_up(r + 1)

                @block.vector
                def _(dve):
                    dve.sem_inc(S_ready, 16)
                    dve.sem_inc(acc_done, 4)
                    wn = slice(0, SLOTS_W)

                    def coefs(s, at, half):
                        dve.wait_ge(half_in, half + 1)
                        c = Chain(dve, cv, half * 4)
                        norm, w, loops = G[:, s, :, D], recs[:, s, :, 2], recs[:, s, :, 3]
                        dve.tensor_tensor(coef[:, s, 6, :], recs[:, s, :, 1], win_base[:, bass.ds(at, HALF)],
                                          ALU.subtract)
                        c(dve.tensor_tensor(coef[:, s, 0, :], norm, w, ALU.mult))
                        c(dve.scalar_tensor_tensor(coef[:, s, 1, :], coef[:, s, 0, :], -1.0, coef[:, s, 0, :],
                                                   ALU.mult, ALU.max))
                        c(dve.scalar_tensor_tensor(coef[:, s, 2, :], coef[:, s, 1, :], thr[:, 0:1], loops,
                                                   ALU.is_ge, ALU.max))
                        c(dve.tensor_tensor(coef[:, s, 4, :], coef[:, s, 2, :], w, ALU.mult))
                        dve.tensor_tensor(coef[:, s, 5, :], w, coef[:, s, 4, :], ALU.subtract).then_inc(coef_ready, 1)

                    def make_tables(r):
                        c = Chain(dve, tv, r * 10 + 1)
                        c(dve.tensor_scalar(terms[wn, 0, :], iota_row[wn, :], bounds[wn, 1:2], None, ALU.is_lt))
                        c(dve.scalar_tensor_tensor(terms[wn, 0, :], iota_row[wn, :], bounds[wn, 0:1], terms[wn, 0, :],
                                                   ALU.is_ge, ALU.mult))
                        c(dve.scalar_tensor_tensor(terms[wn, 1, :], iota_row[wn, :], bounds[wn, 2:3], terms[wn, 0, :],
                                                   ALU.add, ALU.mult))
                        c(dve.tensor_scalar(terms[wn, 2, :], terms[wn, 0, :], ntab[wn, 6:7], None, ALU.mult))
                        dve.sem_inc(terms_ready, 1)
                        c(dve.tensor_scalar(bounds[wn, 0:2], bounds[wn, 0:2], float(-STEPS), None, ALU.add))
                        c(dve.tensor_scalar(bounds[wn, 2:3], bounds[wn, 2:3], float(STEPS), None, ALU.add))
                        dve.wait_ge(tab_up, r + 1)
                        halves = lambda t: t.rearrange("p (q n) -> p q n", q=2)
                        c(dve.tensor_copy(halves(tile_tab[:, :]), ps[:, 0:2, 0:TH]))
                        c(dve.tensor_scalar(halves(win_tab[:, :]), ps[:, 2:4, 0:TH], float(DUMMY), None, ALU.add))
                        c(dve.tensor_scalar(halves(win_base[:, :]), ps[:, 2:4, 0:TH], float(DUMMY), float(P),
                                            ALU.add, ALU.mult))
                        c(dve.memset(gate[:, 1:2], 0.0))
                        dve.sem_inc(tab_ready, 1)
                    c = Chain(dve, tv)
                    c(dve.tensor_copy(bounds[wn, 0:3], ntab[wn, 3:6]))
                    rounds = dve.value_load(rounds_i[0:1, 0:1], min_val=1, max_val=ROUNDS)
                    make_tables(0)
                    coefs(0, 0, 0)
                    with dve.Fori(0, rounds) as r:
                        with dve.Fori(0, ITERS) as i:
                            for s in range(2):
                                half = r * (2 * ITERS) + i * 2 + s
                                wins = value(dve, win_tab[0:1, bass.ds((i * 2 + s) * HALF, HALF)], DUMMY)

                                def add(u):
                                    step = half * HALF + u
                                    dve.wait_ge(messages_up, step + 17)
                                    dve.wait_ge(acc_done, step + 4)
                                    at = acc[:, bass.ds(wins[u], 1), :].rearrange("p a d -> p (a d)")
                                    dve.tensor_tensor(at, at, ps[:, 4 + u % 4, 0:D], ALU.add).then_inc(acc_done, 1)

                                for u in range(HALF):
                                    step = half * HALF + u
                                    dve.wait_ge(keep_ready, step + 1)
                                    dve.wait_ge(messages_up, step + 13)
                                    dve.scalar_tensor_tensor(S[:, u % 4, :], iota_row[:, 0:P], coef[:, s, 6, u:u + 1],
                                                             keepw[:, s, u, :], ALU.is_equal,
                                                             ALU.mult).then_inc(S_ready, 1)
                                    if u >= 2:
                                        add(u - 2)
                                coefs(1 - s, (i * 2 + s + 1) * HALF, half + 1)
                                add(HALF - 2)
                                add(HALF - 1)
                        make_tables(r + 1)
        xn_all = scratch[:, 0:WINDOWS * D].rearrange("p (w d) -> p w d", w=WINDOWS)
        weight_k = sb("weight_k", [P, 2, WINDOWS])
        pos_k = sb("pos_k", [P, 2, WINDOWS + GROUP], I32)
        tile_expert = sb("tile_expert", [P, FTILES], I32)
        rest3 = scratch[:, WINDOWS * D:]
        gamma_b, beta_b, bias_b = rest3[:, 0:D], rest3[:, D:2 * D], rest3[:, 2 * D:3 * D]
        b1T = sb("b1T", [P, EXPERTS * HC])
        b2_b = sb("b2_b", [P, EXPERTS, D])
        with ExitStack() as c3:
            def sb3(name, shape, dt=F32):
                return c3.enter_context(nc.sbuf_tensor(name, shape, dt))

            def sem3(name):
                return c3.enter_context(nc.semaphore(name))

            Wr_sb = sb3("Wr_sb", [P, KC, EXPERTS])
            br_b = sb3("br_b", [P, EXPERTS])
            b1rows = sb3("b1rows", [EXPERTS * HC, P])
            work3 = sb3("work3", [P, 3 * GROUP * D])
            t1 = work3[:, 0:GROUP * D].rearrange("p (w d) -> p w d", w=GROUP)
            t2 = work3[:, GROUP * D:2 * GROUP * D].rearrange("p (w d) -> p w d", w=GROUP)
            stat = sb3("stat", [P, GROUP, 6])
            mv3 = sb3("mv3", [P, 2, GROUP, 2])
            sd = sb3("sd", [P, 2, GROUP])
            sc = sb3("sc", [P, 2, 2, GROUP])
            xTg = work3[:, 2 * GROUP * D:].rearrange("p (c n) -> p c n", c=KC)
            logits = rest3[:, 3 * D:3 * D + WINDOWS * EXPERTS].rearrange("p (w e) -> p w e", w=WINDOWS)
            r = {n: work3[:, GROUP * D + q * WINDOWS * EXPERTS:GROUP * D + (q + 1) * WINDOWS * EXPERTS]
                 .rearrange("p (w e) -> p w e", w=WINDOWS) for q, n in enumerate(
                     ("eq", "cand", "first", "second", "masked", "both", "scan_a", "scan_b", "pos"))}
            col3 = work3[:, FTILES * EXPERTS:FTILES * EXPERTS + 8 * WINDOWS].rearrange("p (m w) -> p m w", m=8)
            e_tab = sb3("e_tab", [P, 4, EXPERTS])
            e_int = sb3("e_int", [P, EXPERTS], I32)
            te = work3[:, 0:FTILES * EXPERTS].rearrange("p (t e) -> p t e", e=EXPERTS)
            te_f = sb3("te_f", [P, FTILES])
            pos_slot = sb3("pos_slot", [P, 2, GROUP], I32)
            rows_slot = t1

            params_in = sem3("params_in")
            p3 = sem3("p3")
            var3, std3 = sem3("var3"), sem3("std3")
            normed = sem3("normed")
            final3, saved3 = sem3("final3"), sem3("saved3")
            turned3, xT3, routed3, logits3 = sem3("turned3"), sem3("xT3"), sem3("routed3"), sem3("logits3")
            b1_turned = sem3("b1_turned")
            both_ready, counts_up = sem3("both_ready"), sem3("counts_up")
            soft_in, soft_out = sem3("soft_in"), sem3("soft_out")
            r3, normed_go, slots_free, gated3 = sem3("r3"), sem3("normed_go"), sem3("slots_free"), sem3("gated3")

            def row_of(vector, n):
                return vector.rearrange("(a d) -> a d", a=1).to_broadcast([P, n])

            with nc.Block() as block:
                @block.sync
                def _(sp):
                    sp.dma_start(bias_b[:, :], row_of(b, D)).then_inc(params_in, 16)
                    sp.dma_start(gamma_b[:, :], row_of(gamma, D)).then_inc(params_in, 16)
                    sp.dma_start(beta_b[:, :], row_of(beta, D)).then_inc(params_in, 16)
                    sp.dma_start(br_b[:, :], row_of(br, EXPERTS)).then_inc(params_in, 16)
                    sp.dma_start(Wr_sb[:, :, :], Wr.rearrange("(c k) e -> k c e", k=P)).then_inc(params_in, 16)
                    sp.dma_start(b1rows[:, :], b1.rearrange("e (c h) -> (e c) h", h=P)).then_inc(params_in, 16)
                    sp.dma_start(b2_b[:, :, :].rearrange("p e d -> p (e d)"),
                                 b2.rearrange("(a e) d -> a (e d)", a=1).to_broadcast([P, EXPERTS * D])
                                 ).then_inc(params_in, 16)
                    sp.wait_ge(params_in, 7 * 16)

                @block.vector
                def _(dve):
                    dve.wait_ge(params_in, 7 * 16)
                    dve.sem_inc(logits3, 1)
                    with dve.Fori(0, GROUPS) as g:
                        c = Chain(dve, p3, g * 10)
                        at = acc[:, bass.ds(g * GROUP, GROUP), :]
                        c(dve.tensor_tensor(at, at, bias_b[:, :].unsqueeze(1).to_broadcast([P, GROUP, D]), ALU.add))
                        for m in range(2):
                            dve.memset(gate[:, 2:3], 0.0)
                            for j in range(GROUP):
                                row = (acc[:, bass.ds(g * GROUP + j, 1), :].rearrange("p a d -> p (a d)") if m == 0
                                       else t1[:, j, :])
                                last = dve.bn_stats(stat[:, j, :], row)
                            c(last)
                            dve.memset(gate[:, 2:3], 0.0)
                            for j in range(GROUP):
                                last = dve.bn_aggr(mv3[:, m, j, :], stat[:, j, :])
                            c(last)
                            dve.sem_inc(var3, 1)
                            dve.wait_ge(std3, g * 2 + m + 1)
                            c(dve.reciprocal(sc[:, m, 0, :], sd[:, m, :]))
                            c(dve.scalar_tensor_tensor(sc[:, m, 1, :], mv3[:, m, :, 0], -1.0, sc[:, m, 0, :],
                                                       ALU.mult, ALU.mult))
                            dve.sem_inc(normed_go, 1)
                            dve.wait_ge(normed, g * 2 + m + 1)
                        c(dve.tensor_tensor(t2[:, :, :], t2[:, :, :],
                                            gamma_b[:, :].unsqueeze(1).to_broadcast([P, GROUP, D]), ALU.mult))
                        dve.tensor_tensor(t2[:, :, :], t2[:, :, :],
                                          beta_b[:, :].unsqueeze(1).to_broadcast([P, GROUP, D]),
                                          ALU.add).then_inc(final3, 1)
                        dve.wait_ge(routed3, g + 1)
                        dve.tensor_tensor(logits[:, bass.ds(g * GROUP, GROUP), :],
                                          ps[:, 4, 0:GROUP * EXPERTS].rearrange("p (w e) -> p w e", w=GROUP),
                                          br_b[:, :].unsqueeze(1).to_broadcast([P, GROUP, EXPERTS]),
                                          ALU.add).then_inc(logits3, 1)
                    dve.wait_ge(logits3, GROUPS + 1)
                    c = Chain(dve, r3)
                    c(dve.memset(pos_k[:, :, WINDOWS:], 0))
                    e_iota = iota_row[:, 0:EXPERTS].unsqueeze(1).to_broadcast([P, WINDOWS, EXPERTS])
                    over = lambda column: column.unsqueeze(2).to_broadcast([P, WINDOWS, EXPERTS])
                    for scores, top, hot in ((logits[:, :, :], 0, r["first"]), (r["masked"][:, :, :], 1, r["second"])):
                        c(dve.tensor_reduce(col3[:, top, :], scores, AX.X, ALU.max))
                        c(dve.tensor_tensor(r["eq"][:, :, :], scores, over(col3[:, top, :]), ALU.is_ge))
                        c(dve.tensor_scalar(r["cand"][:, :, :], r["eq"][:, :, :], -BIG, BIG, ALU.mult, ALU.add))
                        c(dve.tensor_tensor(r["cand"][:, :, :], r["cand"][:, :, :], e_iota, ALU.add))
                        c(dve.tensor_reduce(col3[:, 2, :], r["cand"][:, :, :], AX.X, ALU.min))
                        c(dve.tensor_tensor(hot[:, :, :], e_iota, over(col3[:, 2, :]), ALU.is_equal))
                        if top == 0:
                            c(dve.scalar_tensor_tensor(r["masked"][:, :, :], hot[:, :, :], -3e38, logits[:, :, :],
                                                       ALU.mult, ALU.add))
                    c(dve.tensor_tensor(col3[:, 3, :], col3[:, 1, :], col3[:, 0, :], ALU.subtract))
                    dve.sem_inc(soft_in, 1)
                    dve.wait_ge(soft_out, 1)
                    c(dve.tensor_scalar(col3[:, 5, :], col3[:, 4, :], 1.0, None, ALU.add))
                    c(dve.reciprocal(weight_k[:, 0, :], col3[:, 5, :]))
                    c(dve.tensor_tensor(weight_k[:, 1, :], col3[:, 4, :], weight_k[:, 0, :], ALU.mult))
                    c(dve.tensor_scalar(col3[:, 6, :], iota_row[:, 0:WINDOWS], float(P), pid[:, :], ALU.mult, ALU.add))
                    c(dve.tensor_scalar(col3[:, 6, :], col3[:, 6, :], float(N), None, ALU.is_lt))
                    c(dve.tensor_tensor(r["both"][:, :, :], r["first"][:, :, :], r["second"][:, :, :], ALU.add))
                    c(dve.tensor_tensor(r["both"][:, :, :], r["both"][:, :, :], over(col3[:, 6, :]), ALU.mult))
                    dve.sem_inc(both_ready, 1)
                    dve.wait_ge(counts_up, 1)
                    flat = WINDOWS * EXPERTS
                    here, there = r["scan_a"], r["scan_b"]
                    c(dve.tensor_copy(here[:, :, :], ps[:, 6, 0:flat].rearrange("p (w e) -> p w e", e=EXPERTS)))
                    shift = 1
                    while shift < WINDOWS:
                        c(dve.tensor_copy(there[:, 0:shift, :], here[:, 0:shift, :]))
                        c(dve.tensor_tensor(there[:, shift:, :], here[:, shift:, :], here[:, 0:WINDOWS - shift, :],
                                            ALU.add))
                        here, there = there, here
                        shift *= 2
                    c(dve.tensor_scalar(e_int[:, :], here[:, WINDOWS - 1, :], float(P - 1), None, ALU.add))
                    c(dve.tensor_scalar(e_int[:, :], e_int[:, :], 7, None, ALU.arith_shift_right))
                    c(dve.tensor_copy(e_tab[:, 0, :], e_int[:, :]))
                    c(dve.memset(e_tab[:, 1, 0:1], 0.0))
                    for e in range(1, EXPERTS):
                        c(dve.tensor_tensor(e_tab[:, 1, e:e + 1], e_tab[:, 1, e - 1:e], e_tab[:, 0, e - 1:e], ALU.add))
                    c(dve.tensor_scalar(e_tab[:, 2, :], e_tab[:, 1, :], float(P), None, ALU.mult))
                    pos = r["pos"]
                    c(dve.tensor_copy(pos[:, :, :], ps[:, 5, 0:flat].rearrange("p (w e) -> p w e", e=EXPERTS)))
                    c(dve.tensor_tensor(pos[:, 1:, :], pos[:, 1:, :], here[:, 0:WINDOWS - 1, :], ALU.add))
                    c(dve.tensor_tensor(pos[:, :, :], pos[:, :, :],
                                        e_tab[:, 2, :].unsqueeze(1).to_broadcast([P, WINDOWS, EXPERTS]), ALU.add))
                    c(dve.tensor_scalar(col3[:, 7, :], col3[:, 6, :], -1.0, 1.0, ALU.mult, ALU.add))
                    c(dve.tensor_scalar(col3[:, 5, 0:1], pid[:, :], float(FTILES * P), None, ALU.add))
                    c(dve.tensor_scalar(col3[:, 7, :], col3[:, 7, :], col3[:, 5, 0:1], None, ALU.mult))
                    for k, hot in enumerate((r["first"], r["second"])):
                        c(dve.tensor_tensor(r["eq"][:, :, :], hot[:, :, :], pos[:, :, :], ALU.mult))
                        c(dve.tensor_reduce(col3[:, 2, :], r["eq"][:, :, :], AX.X, ALU.add))
                        c(dve.tensor_tensor(col3[:, 2, :], col3[:, 2, :], col3[:, 6, :], ALU.mult))
                        if k == 1:
                            c(dve.scalar_tensor_tensor(col3[:, 7, :], col3[:, 6, :], float(-P), col3[:, 7, :],
                                                       ALU.mult, ALU.add))
                            c(dve.tensor_scalar(col3[:, 7, :], col3[:, 7, :], float(P), None, ALU.add))
                        c(dve.tensor_tensor(pos_k[:, k, 0:WINDOWS], col3[:, 2, :], col3[:, 7, :], ALU.add))
                    c(dve.tensor_tensor(te[:, :, 1:],
                                        iota_row[:, 0:FTILES].unsqueeze(2).to_broadcast([P, FTILES, EXPERTS - 1]),
                                        e_tab[:, 1, 1:].unsqueeze(1).to_broadcast([P, FTILES, EXPERTS - 1]), ALU.is_ge))
                    c(dve.tensor_reduce(te_f[:, :], te[:, :, 1:], AX.X, ALU.add))
                    c(dve.tensor_copy(tile_expert[:, :], te_f[:, :]))

                @block.scalar
                def _(act):
                    act.wait_ge(params_in, 7 * 16)
                    act.wait_ge(b1_turned, 1)
                    act.copy(b1T[:, :], ps[:, 7, 0:EXPERTS * HC])
                    with act.Fori(0, GROUPS) as g:
                        for m in range(2):
                            act.wait_ge(var3, g * 2 + m + 1)
                            act.activation(sd[:, m, :], mv3[:, m, :, 1], ACT.Sqrt,
                                           bias=eps_col[:, :]).then_inc(std3, 1)
                            act.wait_ge(normed_go, g * 2 + m + 1)
                            if m == 1:
                                act.wait_ge(saved3, g + 1)
                            for j in range(GROUP):
                                row = (acc[:, bass.ds(g * GROUP + j, 1), :].rearrange("p a d -> p (a d)") if m == 0
                                       else t1[:, j, :])
                                last = act.activation((t1, t2)[m][:, j, :], row, ACT.Identity,
                                                      scale=sc[:, m, 0, j:j + 1], bias=sc[:, m, 1, j:j + 1])
                            last.then_inc(normed, 1)
                        act.wait_ge(final3, g + 1)
                        act.copy(xn_all[:, bass.ds(g * GROUP, GROUP), :], t2[:, :, :])
                        act.wait_ge(turned3, g + 1)
                        for k in range(KC):
                            last = act.copy(xTg[:, k, :], psf[:, k * 1024:k * 1024 + GROUP * P])
                        last.then_inc(xT3, 1)
                        act.wait_ge(xT3, g + 1)
                        act.sem_inc(saved3, 1)
                    act.wait_ge(soft_in, 1)
                    act.activation(col3[:, 4, :], col3[:, 3, :], ACT.Exp).then_inc(soft_out, 1)

                @block.tensor
                def _(pe):
                    pe.sem_inc(saved3, 1)
                    pe.wait_ge(params_in, 7 * 16)
                    pe.transpose(ps[:, 7, 0:EXPERTS * HC], b1rows[:, :],
                                 ident[0:EXPERTS * HC, 0:EXPERTS * HC]).then_inc(b1_turned, 1)
                    with pe.Fori(0, GROUPS) as g:
                        pe.wait_ge(final3, g + 1)
                        for k in range(KC):
                            for j in range(GROUP):
                                last = pe.transpose(psf[:, k * 1024 + j * P:k * 1024 + (j + 1) * P],
                                                    t2[:, j, k * P:(k + 1) * P], ident[:, :])
                        last.then_inc(turned3, 1)
                        pe.wait_ge(xT3, g + 1)
                        pe.wait_ge(logits3, g + 1)
                        for j in range(GROUP):
                            for k in range(KC):
                                last = pe.matmul(ps[:, 4, j * EXPERTS:(j + 1) * EXPERTS],
                                                 xTg[:, k, j * P:(j + 1) * P], Wr_sb[:, k, :],
                                                 start=(k == 0), stop=(k == KC - 1))
                        last.then_inc(routed3, 1)
                    pe.wait_ge(both_ready, 1)
                    both = r["both"][:, :, :].rearrange("p w e -> p (w e)")
                    pe.matmul(ps[:, 5, 0:WINDOWS * EXPERTS], before[:, :], both, start=True, stop=True)
                    pe.matmul(ps[:, 6, 0:WINDOWS * EXPERTS], ones[:, :], both, start=True,
                              stop=True).then_inc(counts_up, 1)

            slot_ready, sent = sem3("slot_ready"), [sem3(f"sent{j}") for j in range(2 * GROUP)]
            with nc.Block() as block:
                @block.scalar
                def _(act):
                    with act.Fori(0, GROUPS) as g:
                        act.wait_ge(slots_free, g + 1)
                        act.copy(rows_slot[:, :, :], xn_all[:, bass.ds(g * GROUP, GROUP), :]).then_inc(slot_ready, 1)

                @block.vector
                def _(dve):
                    dve.sem_inc(slots_free, 1)
                    with dve.Fori(0, GROUPS) as g:
                        dve.tensor_copy(pos_slot[:, :, :],
                                        pos_k[:, :, bass.ds(g * GROUP, GROUP)]).then_inc(slot_ready, 1)
                        for j in range(2 * GROUP):
                            dve.wait_ge(sent[j], (g + 1) * 16)
                        dve.sem_inc(slots_free, 1)

                @block.gpsimd
                def _(pool):
                    pool.sem_inc(gated3, 1)
                    with pool.Fori(0, GROUPS) as g:
                        pool.wait_ge(slot_ready, (g + 1) * 2)
                        pool.wait_ge(gated3, g + 1)
                        nc.gpsimd.tensor_tensor(gate[:, 3:4], ones[:, 0:1], ones[:, 1:2], ALU.add).then_inc(gated3, 1)
                        for j in range(GROUP):
                            for k in range(2):
                                nc.gpsimd.indirect_dma_start(
                                    xs_dram, bass.IndirectOffsetOnAxis(ap=pos_slot[:, k, j:j + 1], axis=0),
                                    rows_slot[:, j, :], None).then_inc(sent[2 * j + k], 16)

        with ExitStack() as c4:
            def sb4(name, shape, dt=F32):
                return c4.enter_context(nc.sbuf_tensor(name, shape, dt))

            def sem4(name):
                return c4.enter_context(nc.semaphore(name))

            XS = 3
            UNROLL = 6
            assert (FTILES - 4) % UNROLL == 0 and UNROLL % XS == 0 and UNROLL % 2 == 0
            xrow = sb4("xrow", [P, XS, D])
            xTt = sb4("xTt", [P, 2, KC, P])
            hid = sb4("hid", [P, 2, H])
            hidT = sb4("hidT", [P, 2, HC, P])
            yrow = sb4("yrow", [P, 2, D])
            x_in4, x_turned4, xT4 = [sem4(f"x_in4_{s}") for s in range(XS)], sem4("x_turned4"), sem4("xT4")
            hid_up, hid_down, hid_turned, act_done = (sem4("hid_up"), sem4("hid_down"), sem4("hid_turned"),
                                                      sem4("act_done"))
            y_up, y_down, y_out = sem4("y_up"), sem4("y_down"), [sem4(f"y_out{s}") for s in range(2)]
            y_free = sem4("y_free")

            def tiles(engine, stages, of_experts=True):
                behind_most = 3
                per_slot = UNROLL // XS

                def load_experts(first, count):
                    return (value(engine, tile_expert[0:1, bass.ds(first, count)], EXPERTS - 1) if of_experts
                            else [None] * count)

                experts = load_experts(0, 4)
                for front in range(behind_most):
                    for behind, stage in stages:
                        n = front - behind
                        if n >= 0:
                            stage(n, n % UNROLL, n // XS + 1, experts[n])
                with engine.Fori(0, (FTILES - 4) // UNROLL) as i:
                    experts = load_experts(i * UNROLL, UNROLL + 3)
                    for u in range(UNROLL):
                        for behind, stage in stages:
                            v = u + behind_most - behind
                            stage(i * UNROLL + v, v % UNROLL, i * per_slot + v // XS + 1, experts[v])
                experts = load_experts(FTILES - 4, 4)
                for front in range(FTILES - 1, FTILES + behind_most):
                    for behind, stage in stages:
                        n = front - behind
                        if n < FTILES:
                            stage(n, n % UNROLL, n // XS + 1, experts[n - (FTILES - 4)])

            with nc.Block() as block:
                @block.sync
                def _(sp):
                    def load(n, u, use, _):
                        sp.wait_ge(x_turned4, n + 1)
                        sp.dma_start(xrow[:, u % XS, :], xs_dram[bass.ds(n * P, P), :]).then_inc(x_in4[u % XS], 16)

                    tiles(sp, [(0, load)], of_experts=False)

                @block.gpsimd
                def _(pool):
                    pool.sem_inc(y_free, 2)
                    with pool.Fori(0, FTILES // 2) as i:
                        for s in range(2):
                            pool.wait_ge(y_out[s], (i + 1) * 16)
                            pool.sem_inc(y_free, 1)

                @block.scalar
                def _(act):
                    act.sem_inc(act_done, 2)

                    def gelu(n, u, use, expert):
                        s = u % 2
                        act.wait_ge(hid_turned, n + 1)
                        act.wait_ge(y_up, n + 1)
                        for k in range(HC):
                            last = act.activation(hidT[:, s, k, :], ps[:, 4 + s, k * P:(k + 1) * P], ACT.Gelu,
                                                  bias=b1T[:, bass.ds(expert * HC + k, 1)])
                        last.then_inc(act_done, 1)

                    def store(n, u, use, _):
                        act.wait_ge(y_down, n + 3)
                        act.dma_start(ys_dram[bass.ds(n * P, P), :], yrow[:, u % 2, :]).then_inc(y_out[u % 2], 16)

                    tiles(act, [(2, gelu), (3, store)])

                @block.vector
                def _(dve):
                    dve.sem_inc(xT4, 2)
                    dve.sem_inc(hid_down, 2)
                    dve.sem_inc(y_down, 2)

                    def keep_rows(n, u, use, _):
                        dve.wait_ge(x_turned4, n + XS + 1)
                        dve.wait_ge(hid_up, n + 1)
                        dve.tensor_copy(xTt[:, u % 2].rearrange("p c n -> p (c n)"),
                                        ps[:, u % 2, 0:KC * P]).then_inc(xT4, 1)

                    def keep_hidden(n, u, use, _):
                        dve.wait_ge(hid_up, n + 3)
                        dve.tensor_copy(hid[:, u % 2, :], ps[:, 2 + u % 2, :]).then_inc(hid_down, 1)

                    def finish(n, u, use, expert):
                        dve.wait_ge(y_up, n + 3)
                        dve.wait_ge(y_free, n + 1)
                        dve.tensor_tensor(yrow[:, u % 2, :], ps[:, 6 + u % 2, 0:D],
                                          b2_b[:, bass.ds(expert, 1), :].rearrange("p a d -> p (a d)"),
                                          ALU.add).then_inc(y_down, 1)

                    tiles(dve, [(0, keep_rows), (1, keep_hidden), (3, finish)])

                @block.tensor
                def _(pe):
                    pe.sem_inc(x_turned4, XS)
                    pe.sem_inc(hid_up, 2)
                    pe.sem_inc(y_up, 2)

                    def turn_rows(n, u, use, _):
                        pe.wait_ge(x_in4[u % XS], use * 16)
                        pe.wait_ge(xT4, n + 1)
                        for k in range(KC):
                            last = pe.transpose(ps[:, u % 2, k * P:(k + 1) * P], xrow[:, u % XS, k * P:(k + 1) * P],
                                                ident[:, :])
                        last.then_inc(x_turned4, 1)

                    def into_hidden(n, u, use, expert):
                        pe.wait_ge(xT4, n + 3)
                        pe.wait_ge(hid_down, n + 1)
                        for k in range(KC):
                            last = pe.matmul(ps[:, 2 + u % 2, :], xTt[:, u % 2, k, :],
                                             w1_sb[:, bass.ds(expert * (KC * H) + k * H, H)],
                                             start=(k == 0), stop=(k == KC - 1))
                        last.then_inc(hid_up, 1)

                    def turn_hidden(n, u, use, _):
                        pe.wait_ge(hid_down, n + 3)
                        pe.wait_ge(act_done, n + 1)
                        for k in range(HC):
                            last = pe.transpose(ps[:, 4 + u % 2, k * P:(k + 1) * P],
                                                hid[:, u % 2, k * P:(k + 1) * P], ident[:, :])
                        last.then_inc(hid_turned, 1)

                    def out_of_hidden(n, u, use, expert):
                        pe.wait_ge(act_done, n + 3)
                        pe.wait_ge(y_down, n + 1)
                        for k in range(HC):
                            last = pe.matmul(ps[:, 6 + u % 2, 0:D], hidT[:, u % 2, k, :],
                                             w2_sb[:, bass.ds(expert * (HC * D) + k * D, D)],
                                             start=(k == 0), stop=(k == HC - 1))
                        last.then_inc(y_up, 1)

                    tiles(pe, [(0, turn_rows), (1, into_hidden), (2, turn_hidden), (3, out_of_hidden)])

        with ExitStack() as c5:
            def sb5(name, shape, dt=F32):
                return c5.enter_context(nc.sbuf_tensor(name, shape, dt))

            def sem5(name):
                return c5.enter_context(nc.semaphore(name))

            y_got = sb5("y_got", [P, 2, GROUP, D])
            pos_now = sb5("pos_now", [P, 2, GROUP], I32)
            slots5, gated5, added = sem5("slots5"), sem5("gated5"), sem5("added")
            got = [sem5(f"got{j}") for j in range(2 * GROUP)]
            stored = sem5("stored")
            with nc.Block() as block:
                @block.vector
                def _(dve):
                    dve.tensor_copy(pos_now[:, :, :], pos_k[:, :, 0:GROUP]).then_inc(slots5, 1)
                    with dve.Fori(0, GROUPS) as g:
                        for j in range(GROUP):
                            at = acc[:, bass.ds(g * GROUP + j, 1), :].rearrange("p a d -> p (a d)")
                            for k in range(2):
                                dve.wait_ge(got[2 * j + k], (g + 1) * 16)
                                dve.scalar_tensor_tensor(at, y_got[:, k, j, :],
                                                         weight_k[:, k, bass.ds(g * GROUP + j, 1)], at,
                                                         ALU.mult, ALU.add).then_inc(added, 1)
                                dve.wait_ge(added, g * (2 * GROUP) + 2 * j + k + 1)
                        dve.tensor_copy(pos_now[:, :, :],
                                        pos_k[:, :, bass.ds(g * GROUP + GROUP, GROUP)]).then_inc(slots5, 1)

                @block.gpsimd
                def _(pool):
                    pool.sem_inc(gated5, 1)
                    with pool.Fori(0, GROUPS) as g:
                        pool.wait_ge(slots5, g + 1)
                        pool.wait_ge(gated5, g + 1)
                        nc.gpsimd.tensor_tensor(gate[:, 3:4], ones[:, 0:1], ones[:, 1:2], ALU.add).then_inc(gated5, 1)
                        for j in range(GROUP):
                            for k in range(2):
                                nc.gpsimd.indirect_dma_start(
                                    y_got[:, k, j, :], None, ys_dram,
                                    bass.IndirectOffsetOnAxis(ap=pos_now[:, k, j:j + 1], axis=0)
                                ).then_inc(got[2 * j + k], 16)

                @block.sync
                def _(sp):
                    with sp.Fori(0, GROUPS - 1) as g:
                        sp.wait_ge(added, (g + 1) * (2 * GROUP))
                        sp.dma_start(out[bass.ds(g * (GROUP * P), GROUP * P), :].rearrange("(w p) d -> p w d", p=P),
                                     acc[:, bass.ds(g * GROUP, GROUP), :]).then_inc(stored, 16)
                    sp.wait_ge(added, GROUPS * 2 * GROUP)
                    lo = (GROUPS - 1) * GROUP
                    sp.dma_start(out[lo * P:(WINDOWS - 1) * P, :].rearrange("(w p) d -> p w d", p=P),
                                 acc[:, lo:WINDOWS - 1, :]).then_inc(stored, 16)
                    sp.dma_start(out[(WINDOWS - 1) * P:N, :], acc[0:TAIL, WINDOWS - 1, :]).then_inc(stored, 16)
                    sp.wait_ge(stored, (GROUPS + 1) * 16)


_INS = ['x', 'src', 'dst', 'edge_weight', 'L0_gnn_node_lock', 'L0_gnn_W', 'L0_gnn_b', 'L0_ffn_gamma', 'L0_ffn_beta',
        'L0_ffn_Wr', 'L0_ffn_br', 'L0_ffn_W1', 'L0_ffn_b1', 'L0_ffn_W2', 'L0_ffn_b2']


def kernel(**inputs):
    import numpy as _np
    import concourse.bacc as _bacc
    from concourse import mybir as _mybir
    from concourse.bass_utils import run_bass_kernel_spmd as _run

    nc = _bacc.Bacc("TRN2", target_bir_lowering=False, num_devices=1)
    arrays, args = {}, []
    for name in _INS:
        a = _np.ascontiguousarray(inputs[name])
        arrays[f"in_{name}_dram"] = a
        args.append(nc.dram_tensor(f"in_{name}_dram", a.shape, _mybir.dt.from_np(a.dtype), kind="ExternalInput").ap())
    args.append(nc.dram_tensor("out_0_dram", inputs['x'].shape, _mybir.dt.float32, kind="ExternalOutput").ap())
    gnn_moe_kernel(nc, *args)
    r = _run(nc, [arrays], core_ids=[0])
    return r.results[0]["out_0_dram"]
```

```python
from contextlib import ExitStack

import concourse.bass as bass
from concourse import mybir

ALU = mybir.AluOpType
ACT = mybir.ActivationFunctionType
AX = mybir.AxisListType
F32 = mybir.dt.float32
I32 = mybir.dt.int32
BF16 = mybir.dt.bfloat16

P = 128
GROUP = 7
PACK = 8
PACKS = 5
AHEAD = 3
BATCH = 16
EPS = 1e-5
BIG = 65536.0


class Chain:

    def __init__(self, engine, sem, base=0):
        self.engine, self.sem, self.base, self.n = engine, sem, base, 0

    def __call__(self, instruction):
        self.n += 1
        instruction.then_inc(self.sem, 1)
        self.engine.wait_ge(self.sem, self.base + self.n)


def gnn_moe_kernel(nc, x, src, dst, edge_weight, node_lock, W, b, gamma, beta, Wr, br, W1, b1, W2, b2, out):
    N, D = x.shape
    E, = src.shape
    NLOCK, = node_lock.shape
    EXPERTS, _, H = W1.shape
    KC = D // P
    HC = H // P
    WINDOWS = -(-N // P)
    GROUPS = WINDOWS // GROUP
    TAIL = N - (WINDOWS - 1) * P
    DUMMY = WINDOWS
    SLOTS_W = WINDOWS + 1
    NOWHERE = SLOTS_W * P - 1
    TILES = -(-E // P)
    ROWGROUPS = -(-TILES // P)
    BATCHES = -(-TILES // BATCH)
    TCOLS = BATCHES * BATCH
    STEPS = 880
    assert STEPS >= TILES + WINDOWS and STEPS % (PACKS * PACK) == 0
    ITERS = STEPS // (PACKS * PACK)
    ROUNDS = -(-(TILES * WINDOWS) // STEPS)
    TAB = STEPS + AHEAD * PACK
    FTILES = 2 * WINDOWS + EXPERTS
    REGION = (WINDOWS + 1) * P
    IDLE = EXPERTS * REGION
    SPARE = IDLE + EXPERTS * P
    SLOT_ROWS = SPARE + 2 * P
    LTILES = -(-NLOCK // P)
    HROW = D + 1
    assert BATCHES % 2 == 0 and BATCHES > 6 * GROUPS + 2 and WINDOWS % GROUP == 0 and FTILES % 2 == 0
    assert LTILES <= 8 and TILES < ROWGROUPS * P

    h_dram = nc.dram_tensor("h_rows", (WINDOWS * P, HROW), F32).ap()
    lock_dram = nc.dram_tensor("lock_row", (WINDOWS, P), F32).ap()
    xs_dram = nc.dram_tensor("slot_inputs", (SLOT_ROWS, D), F32).ap()
    ys_dram = nc.dram_tensor("slot_outputs", (FTILES * P, D), F32).ap()

    with ExitStack() as ctx:
        def sb(name, shape, dt=F32):
            return ctx.enter_context(nc.sbuf_tensor(name, shape, dt))

        def sem(name):
            return ctx.enter_context(nc.semaphore(name))

        acc = sb("acc", [P, SLOTS_W, D])
        big = sb("big", [P, 2 * EXPERTS * KC * H])
        scratch = sb("scratch", [P, TCOLS * 4 + SLOTS_W * P + 5 * ROWGROUPS * P])
        ident = sb("ident", [P, P])
        ones = sb("ones", [P, P])
        before = sb("before", [P, P])
        iota_row = sb("iota_row", [P, TAB])
        pid = sb("pid", [P, 1])
        winlo = sb("winlo", [P, 2])
        thr = sb("thr", [P, 1])
        gate = sb("gate", [P, 4])
        eps_col = sb("eps_col", [P, 1])
        ntab = sb("ntab", [P, 8])
        rounds_i = sb("rounds_i", [P, 2], I32)
        ps = ctx.enter_context(nc.psum_tensor("ps", [P, 8, 512], F32))
        psf = ps[:, :, :].rearrange("p a b -> p (a b)")

        xnT = big[:, 0:KC * SLOTS_W * P].rearrange("p (c n) -> p c n", c=KC)
        w1_sb = big[:, 0:EXPERTS * KC * H]
        w2_sb = big[:, EXPERTS * KC * H:]
        rec = scratch[:, 0:TCOLS * 4].rearrange("p (t c) -> p t c", c=4)
        lockrow = scratch[:, TCOLS * 4:TCOLS * 4 + SLOTS_W * P]
        tail_region = scratch[:, TCOLS * 4 + SLOTS_W * P:]

        def by_groups(engine, body, slots):
            with engine.Fori(0, (GROUPS - 1) // slots) as i:
                for s in range(slots):
                    body(i * slots + s, s, i + 1, False)
            for g in range((GROUPS - 1) // slots * slots, GROUPS):
                body(g, g % slots, g // slots + 1, g == GROUPS - 1)

        with ExitStack() as c1:
            def sb1(name, shape, dt=F32):
                return c1.enter_context(nc.sbuf_tensor(name, shape, dt))

            def sem1(name):
                return c1.enter_context(nc.semaphore(name))

            RP = ROWGROUPS * P
            rows_i = tail_region[:, 0:2 * RP].bitcast(I32).rearrange("p (a g e) -> p a g e", a=2, e=P)
            rows_f = tail_region[:, 2 * RP:5 * RP].rearrange("p (a g e) -> p a g e", a=3, e=P)
            lock_i = sb1("lock_i", [8, P], I32)
            lock_f = sb1("lock_f", [8, P])
            spare = big[:, KC * SLOTS_W * P:]
            wrow = lockrow[:, 3 * RP:3 * RP + KC * D].rearrange("p (c d) -> p c d", c=KC)
            WT = sb1("WT", [P, KC, D])
            srcI = lockrow[:, 3 * RP + KC * D:3 * RP + KC * D + TCOLS].bitcast(I32)
            absw = lockrow[:, 3 * RP + KC * D + TCOLS:3 * RP + KC * D + 2 * TCOLS]
            acol = sb1("acol", [P, TCOLS], BF16)
            bcol = sb1("bcol", [P, TCOLS], BF16)
            w_parts = sb1("w_parts", [P, 3, TCOLS], BF16)
            lockcol = sb1("lockcol", [P, 3, 8])
            lockcol_i = sb1("lockcol_i", [P, 8], I32)
            diag = lockrow[:, 0:2 * RP].rearrange("p (m g e) -> p m g e", m=2, g=ROWGROUPS)
            mnmx = sb1("mnmx", [P, 2, ROWGROUPS])
            cand = lockrow[:, 2 * RP:3 * RP]
            oneB = spare[:, 0:BATCH * P].bitcast(BF16).rearrange("p (s b t) -> p s b t", s=2, t=BATCH)
            oneA = sb1("oneA", [P, 2, WINDOWS, BATCH], BF16)
            partA = sb1("partA", [P, 2, 3, WINDOWS, BATCH], BF16)
            iota_t = spare[:, BATCH * P:BATCH * P * 3 // 2].bitcast(BF16).rearrange("p (b t) -> p b t", t=BATCH)
            lockhist = sb1("lockhist", [P, P])
            norms = sb1("norms", [P, WINDOWS])
            small = sb1("small", [P, 4])

            cleared = sem1("cleared")
            consts = sem1("consts")
            src_in, dst_in, w_in = sem1("src_in"), sem1("dst_in"), sem1("w_in")
            lock_in, W_in, x_in = sem1("lock_in"), sem1("W_in"), sem1("x_in")
            rows_float = sem1("rows_float")
            diag_ready = sem1("diag_ready")
            turned = sem1("turned")
            rec_ready = sem1("rec_ready")
            ranges_up = sem1("ranges_up")
            steps_ready = sem1("steps_ready")
            prefix_ready = sem1("prefix_ready")
            filled = sem1("filled")
            column_steps = sem1("column_steps")

            with nc.Block() as block:
                @block.gpsimd
                def _(pool):
                    nc.gpsimd.memset(rows_i[:, 0, ROWGROUPS - 1, :], 0)
                    nc.gpsimd.memset(rows_i[:, 1, ROWGROUPS - 1, :], NOWHERE)
                    nc.gpsimd.memset(rows_f[:, 2, ROWGROUPS - 1, :], 0.0)
                    nc.gpsimd.memset(lock_i[:, :], NOWHERE)
                    nc.gpsimd.memset(lockrow[:, DUMMY * P:], 0.0)
                    nc.gpsimd.memset(xnT[:, :, WINDOWS * P:], 0.0)
                    nc.gpsimd.memset(acc[:, WINDOWS - 1:SLOTS_W, :], 0.0).then_inc(cleared, 1)
                    nc.gpsimd.memset(ident[:, :], 0.0).then_inc(filled, 1)
                    nc.gpsimd.memset(ones[:, :], 1.0).then_inc(filled, 1)
                    nc.gpsimd.memset(eps_col[:, :], EPS)
                    nc.gpsimd.iota(iota_row[:, :], [[1, TAB]], base=0, channel_multiplier=0,
                                   allow_small_or_imprecise_dtypes=True)
                    nc.gpsimd.iota(pid[:, :], [[1, 1]], base=0, channel_multiplier=1,
                                   allow_small_or_imprecise_dtypes=True)
                    nc.gpsimd.iota(winlo[:, :], [[P, 2]], base=0, channel_multiplier=P,
                                   allow_small_or_imprecise_dtypes=True)
                    pool.wait_ge(filled, 2)
                    nc.gpsimd.affine_select(out=ident[:, :], in_=ident[:, :], compare_op=ALU.not_equal, fill=1.0,
                                            base=0, pattern=[[-1, P]], channel_multiplier=1)
                    nc.gpsimd.affine_select(out=before[:, :], in_=ones[:, :], compare_op=ALU.is_gt, fill=0.0,
                                            base=0, pattern=[[1, P]], channel_multiplier=-1).then_inc(consts, 1)

                @block.sync
                def _(sp):
                    full = (ROWGROUPS - 1) * P * P
                    whole = (TILES - 1) * P
                    rest = TILES - 1 - (ROWGROUPS - 1) * P
                    sp.wait_ge(cleared, 1)
                    for a, (dram, rows, landed) in enumerate(((dst, rows_i[:, 1], dst_in), (src, rows_i[:, 0], src_in),
                                                              (edge_weight, rows_f[:, 2], w_in))):
                        sp.dma_start(rows[:, 0:ROWGROUPS - 1, :],
                                     dram[0:full].rearrange("(g t e) -> t g e", t=P, e=P)).then_inc(landed, 16)
                        sp.dma_start(rows[0:rest, ROWGROUPS - 1, :],
                                     dram[full:whole].rearrange("(t e) -> t e", e=P)).then_inc(landed, 16)
                        sp.dma_start(rows[rest:rest + 1, ROWGROUPS - 1, 0:E - whole],
                                     dram[whole:E].rearrange("(a e) -> a e", a=1)).then_inc(landed, 16)
                    lw = (LTILES - 1) * P
                    sp.dma_start(lock_i[0:LTILES - 1, :],
                                 node_lock[0:lw].rearrange("(t e) -> t e", e=P)).then_inc(lock_in, 16)
                    sp.dma_start(lock_i[LTILES - 1:LTILES, 0:NLOCK - lw],
                                 node_lock[lw:NLOCK].rearrange("(a e) -> a e", a=1)).then_inc(lock_in, 16)
                    sp.dma_start(wrow[:, :, :], W.rearrange("(c o) k -> o c k", o=P)).then_inc(W_in, 16)
                    step = (WINDOWS - 1) // 4
                    for q in range(4):
                        sp.dma_start(acc[:, q * step:(q + 1) * step, :],
                                     x[q * step * P:(q + 1) * step * P, :].rearrange("(w p) d -> p w d", p=P)
                                     ).then_inc(x_in, 16)
                    sp.dma_start(acc[0:TAIL, WINDOWS - 1, :], x[(WINDOWS - 1) * P:N, :]).then_inc(x_in, 16)

                @block.tensor
                def _(pe):
                    pe.wait_ge(consts, 1)
                    for a, ready in ((0, 2), (1, 1), (2, 0)):
                        if a < 2:
                            pe.wait_ge(rows_float, ready)
                        else:
                            pe.wait_ge(w_in, 48)
                        for g in range(ROWGROUPS):
                            last = pe.transpose(psf[:, a * 1024 + g * P:a * 1024 + (g + 1) * P],
                                                rows_f[:, a, g, :], ident[:, :])
                        last.then_inc(turned, 1)
                    pe.wait_ge(rows_float, 3)
                    pe.transpose(ps[:, 6, 0:8], lock_f[:, :], ident[0:8, 0:8]).then_inc(turned, 1)
                    pe.wait_ge(W_in, 16)
                    for k in range(KC):
                        for o in range(KC):
                            last = pe.transpose(ps[:, 7, k * D + o * P:k * D + (o + 1) * P],
                                                wrow[:, o, k * P:(k + 1) * P], ident[:, :])
                    last.then_inc(turned, 1)
                    pe.wait_ge(diag_ready, 1)
                    pe.wait_ge(rec_ready, 2)
                    for m in range(2):
                        for g in range(ROWGROUPS):
                            last = pe.matmul(psf[0:SLOTS_W, m * 1024 + g * P:m * 1024 + (g + 1) * P],
                                             ones[:, 0:SLOTS_W], diag[:, m, g, :], start=True, stop=True)
                    last.then_inc(ranges_up, 1)
                    pe.wait_ge(steps_ready, 1)
                    pe.matmul(ps[0:SLOTS_W, 4, 0:1], before[0:SLOTS_W, 0:SLOTS_W], ntab[0:SLOTS_W, 2:3],
                              start=True, stop=True)
                    pe.matmul(ps[:, 4, 2:3], ones[0:SLOTS_W, :], ntab[0:SLOTS_W, 2:3],
                              start=True, stop=True).then_inc(prefix_ready, 1)

                @block.vector
                def _(dve):
                    chain = Chain(dve, column_steps)
                    dve.wait_ge(dst_in, 48)
                    dve.tensor_copy(rows_f[:, 1], rows_i[:, 1]).then_inc(rows_float, 1)
                    dve.wait_ge(src_in, 48)
                    dve.tensor_copy(rows_f[:, 0], rows_i[:, 0]).then_inc(rows_float, 1)
                    dve.wait_ge(lock_in, 32)
                    dve.tensor_copy(lock_f[:, :], lock_i[:, :]).then_inc(rows_float, 1)
                    dve.wait_ge(rows_float, 3)
                    chain(dve.tensor_reduce(mnmx[:, 0, :], rows_f[:, 1], AX.X, ALU.min))
                    chain(dve.tensor_reduce(mnmx[:, 1, :], rows_f[:, 1], AX.X, ALU.max))
                    dve.wait_ge(consts, 1)
                    for m in range(2):
                        for g in range(ROWGROUPS):
                            last = dve.tensor_scalar(diag[:, m, g, :], ident[:, :], mnmx[:, m, g:g + 1], None, ALU.mult)
                    last.then_inc(diag_ready, 1)
                    dve.wait_ge(turned, 1)
                    dve.tensor_copy(rec[:, :, 0], psf[:, 0:TCOLS]).then_inc(rec_ready, 1)
                    dve.wait_ge(turned, 2)
                    dve.tensor_copy(rec[:, :, 1], psf[:, 1024:1024 + TCOLS]).then_inc(rec_ready, 1)
                    dve.wait_ge(turned, 3)
                    dve.tensor_copy(rec[:, :, 2], psf[:, 2048:2048 + TCOLS]).then_inc(rec_ready, 1)
                    dve.wait_ge(turned, 4)
                    dve.tensor_copy(lockcol[:, 0, :], ps[:, 6, 0:8]).then_inc(rec_ready, 1)
                    dve.wait_ge(turned, 5)
                    dve.tensor_copy(WT[:, :, :], ps[:, 7, :].rearrange("p (c o) -> p c o", c=KC)).then_inc(rec_ready, 1)
                    dve.wait_ge(rec_ready, 5)
                    chain(dve.tensor_copy(srcI[:, :], rec[:, :, 0]))
                    chain(dve.tensor_scalar(srcI[:, :], srcI[:, :], 7, None, ALU.arith_shift_right))
                    chain(dve.tensor_copy(acol[:, :], srcI[:, :]))
                    chain(dve.scalar_tensor_tensor(bcol[:, :], acol[:, :], float(-P), rec[:, :, 0], ALU.mult, ALU.add))
                    chain(dve.scalar_tensor_tensor(absw[:, :], rec[:, :, 2], -1.0, rec[:, :, 2], ALU.mult, ALU.max))
                    for part in range(3):
                        chain(dve.tensor_copy(w_parts[:, part, :], absw[:, :]))
                        if part < 2:
                            chain(dve.tensor_tensor(absw[:, :], absw[:, :], w_parts[:, part, :], ALU.subtract))
                    chain(dve.tensor_tensor(rec[:, :, 3], rec[:, :, 0], rec[:, :, 1], ALU.is_equal))
                    chain(dve.tensor_copy(lockcol_i[:, :], lockcol[:, 0, :]))
                    chain(dve.tensor_scalar(lockcol_i[:, :], lockcol_i[:, :], 7, None, ALU.arith_shift_right))
                    chain(dve.tensor_copy(lockcol[:, 1, :], lockcol_i[:, :]))
                    chain(dve.scalar_tensor_tensor(lockcol[:, 2, :], lockcol[:, 1, :], float(-P), lockcol[:, 0, :],
                                                   ALU.mult, ALU.add))
                    dve.wait_ge(ranges_up, 1)
                    wn = slice(0, SLOTS_W)
                    chain(dve.tensor_scalar(cand[wn, 0:TILES], psf[wn, 1024:1024 + TILES], winlo[wn, 0:1], BIG,
                                            ALU.is_lt, ALU.mult))
                    chain(dve.tensor_tensor(cand[wn, 0:TILES], cand[wn, 0:TILES], iota_row[wn, 0:TILES], ALU.add))
                    chain(dve.tensor_reduce(ntab[wn, 0:1], cand[wn, 0:TILES], AX.X, ALU.min))
                    chain(dve.tensor_scalar(ntab[wn, 0:1], ntab[wn, 0:1], float(TILES), None, ALU.min))
                    chain(dve.scalar_tensor_tensor(cand[wn, 0:TILES], psf[wn, 0:TILES], winlo[wn, 1:2],
                                                   iota_row[wn, 1:TILES + 1], ALU.is_lt, ALU.mult))
                    chain(dve.tensor_reduce(ntab[wn, 1:2], cand[wn, 0:TILES], AX.X, ALU.max))
                    chain(dve.tensor_tensor(small[wn, 0:1], ntab[wn, 1:2], ntab[wn, 0:1], ALU.subtract))
                    chain(dve.tensor_scalar(small[wn, 1:2], pid[wn, :], float(WINDOWS), None, ALU.is_lt))
                    chain(dve.tensor_scalar(ntab[wn, 2:3], small[wn, 0:1], 0.0, small[wn, 1:2], ALU.max, ALU.mult))
                    dve.sem_inc(steps_ready, 1)
                    dve.wait_ge(prefix_ready, 1)
                    chain(dve.tensor_copy(ntab[wn, 3:4], ps[wn, 4, 0:1]))
                    chain(dve.tensor_tensor(ntab[wn, 4:5], ntab[wn, 3:4], ntab[wn, 2:3], ALU.add))
                    chain(dve.tensor_tensor(ntab[wn, 5:6], ntab[wn, 0:1], ntab[wn, 3:4], ALU.subtract))
                    chain(dve.tensor_scalar(ntab[wn, 6:7], pid[wn, :], float(-DUMMY), None, ALU.add))
                    chain(dve.tensor_copy(small[:, 2:3], ps[:, 4, 2:3]))
                    chain(dve.tensor_scalar(cand[:, 0:ROUNDS], iota_row[:, 0:ROUNDS], float(STEPS), small[:, 2:3],
                                            ALU.mult, ALU.is_lt))
                    chain(dve.tensor_reduce(small[:, 3:4], cand[:, 0:ROUNDS], AX.X, ALU.add))
                    chain(dve.tensor_scalar(rounds_i[:, 0:1], small[:, 3:4], 1.0, None, ALU.max))

            ACT_NORMS = 5
            xn_ready_dve = sem1("xn_ready_dve")
            xn = tail_region[:, 0:GROUP * D].rearrange("p (w d) -> p w d", w=GROUP)
            std = sb1("std", [P, GROUP])
            var_ready, std_ready = sem1("var_ready"), sem1("std_ready")
            sums_ready, norms_ready = sem1("sums_ready"), sem1("norms_ready")
            stats = sb1("stats", [P, GROUP, 6])
            mv = sb1("mv", [P, GROUP, 2])
            rstd = sb1("rstd", [P, 2, GROUP])
            junk = sb1("junk", [P, D])
            junk_rows = lockrow[:, 0:GROUP * P]
            colsq = sb1("colsq", [P, KC, GROUPS])
            col = sb1("col", [P, 8, KC])
            prune = tail_region[:, 0:2 * KC * D].rearrange("p (m c d) -> p m c d", m=2, c=KC)
            xT = sb1("xT", [P, 3, KC, P])

            def h_slot(j):
                return j % 2 if j < GROUP - 1 else 2

            hrow = tail_region[:, 0:2 * GROUP * HROW].rearrange("p (s w d) -> p s w d", s=2, w=GROUP)
            nsq = sb1("nsq", [P, 2, GROUP])
            xn_ready, xn_turned, xT_saved = sem1("xn_ready"), sem1("xn_turned"), sem1("xT_saved")
            colsum_ready = sem1("colsum_ready")
            norm_steps, lock_steps, prune_steps = sem1("norm_steps"), sem1("lock_steps"), sem1("prune_steps")
            colsq_ready = sem1("colsq_ready")
            total_ready = sem1("total_ready")
            W_ready = sem1("W_ready")
            one_hots_ready, A_eq, hist_done = sem1("one_hots_ready"), sem1("A_eq"), sem1("hist_done")
            iota_ready, scale_ready = sem1("iota_ready"), sem1("scale_ready")
            lock_hot = sem1("lock_hot")
            lock_up, lock_out, lock_back = sem1("lock_up"), sem1("lock_out"), sem1("lock_back")
            xT_slot, h_up, h_down, h_norm, h_out = (sem1("xT_slot"), sem1("h_up"), sem1("h_down"), sem1("h_norm"),
                                                    sem1("h_out"))
            h_free = sem1("h_free")
            sum_up, thr_up = sem1("sum_up"), sem1("thr_up")
            zero_mm = sb1("zero_mm", [P, 3 * WINDOWS], BF16)

            with nc.Block() as block:
                @block.vector
                def _(dve):
                    chain = Chain(dve, lock_steps)
                    chain(dve.memset(zero_mm[:, :], 0.0))
                    chain(dve.tensor_tensor(oneB[:, 0, :, 0:8], iota_row[:, 0:P].unsqueeze(2).to_broadcast([P, P, 8]),
                                            lockcol[:, 2, :].unsqueeze(1).to_broadcast([P, P, 8]), ALU.is_equal))
                    chain(dve.tensor_tensor(oneA[:, 0, :, 0:8],
                                            iota_row[:, 0:WINDOWS].unsqueeze(2).to_broadcast([P, WINDOWS, 8]),
                                            lockcol[:, 1, :].unsqueeze(1).to_broadcast([P, WINDOWS, 8]),
                                            ALU.is_equal))
                    dve.sem_inc(lock_hot, 1)
                    dve.wait_ge(lock_up, 1)
                    chain(dve.tensor_scalar(lockhist[0:WINDOWS, :], ps[0:WINDOWS, 6, 0:P], 1.0, None, ALU.min))
                    dve.sem_inc(lock_up, 1)

                    def one_hots(at, s, n):
                        across = lambda ap, m: ap.unsqueeze(1).to_broadcast([P, m, BATCH])
                        dve.wait_ge(hist_done, n + 1)
                        dve.tensor_tensor(oneA[:, s], iota_t[:, 0:WINDOWS, :],
                                          across(acol[:, bass.ds(at, BATCH)], WINDOWS),
                                          ALU.is_equal).then_inc(A_eq, 1)
                        dve.tensor_tensor(oneB[:, s], iota_t[:, :, :], across(bcol[:, bass.ds(at, BATCH)], P),
                                          ALU.is_equal)
                        dve.wait_ge(A_eq, n + 1)
                        dve.tensor_tensor(partA[:, s], oneA[:, s].unsqueeze(1).to_broadcast([P, 3, WINDOWS, BATCH]),
                                          w_parts[:, :, bass.ds(at, BATCH)].unsqueeze(2)
                                          .to_broadcast([P, 3, WINDOWS, BATCH]), ALU.mult).then_inc(one_hots_ready, 1)

                    dve.wait_ge(iota_ready, 1)
                    dve.wait_ge(x_in, 80)
                    with dve.Fori(0, GROUPS) as g:
                        c = Chain(dve, norm_steps, g * 3)
                        for j in range(GROUP):
                            last = dve.bn_stats(stats[:, j, :], acc[:, bass.ds(g * GROUP + j, 1), :]
                                                .rearrange("p a d -> p (a d)"))
                        c(last)
                        dve.memset(gate[:, 0:1], 0.0)
                        for j in range(GROUP):
                            last = dve.bn_aggr(mv[:, j, :], stats[:, j, :])
                        c(last)
                        dve.sem_inc(var_ready, 1)
                        one_hots(g * (2 * BATCH), 0, g * 2)
                        dve.wait_ge(std_ready, g + 1)
                        c(dve.reciprocal(rstd[:, 0, :], std[:, :]))
                        dve.scalar_tensor_tensor(rstd[:, 1, :], mv[:, :, 0], -1.0, rstd[:, 0, :],
                                                 ALU.mult, ALU.mult).then_inc(scale_ready, 1)
                        dve.wait_ge(xn_turned, (g + 1) * GROUP)
                        for j in range(ACT_NORMS, GROUP):
                            dve.tensor_scalar(xn[:, j, :], acc[:, bass.ds(g * GROUP + j, 1), :]
                                              .rearrange("p a d -> p (a d)"), mv[:, j, 0:1], rstd[:, 0, j:j + 1],
                                              ALU.subtract, ALU.mult).then_inc(xn_ready_dve, 1)
                        one_hots(g * (2 * BATCH) + BATCH, 1, g * 2 + 1)
                    for n in range(2 * GROUPS, 2 * GROUPS + 2):
                        one_hots(n * BATCH, n % 2, n)
                    chain = Chain(dve, prune_steps)
                    dve.wait_ge(colsq_ready, KC * GROUPS)
                    chain(dve.tensor_reduce(col[:, 0, :], colsq[:, :, :], AX.X, ALU.add))
                    dve.sem_inc(colsum_ready, 1)
                    dve.wait_ge(total_ready, 1)
                    chain(dve.tensor_reduce(col[:, 1, 0:1], ps[:, 7, 0:KC], AX.X, ALU.add))
                    dve.sem_inc(sums_ready, 1)
                    dve.wait_ge(norms_ready, 1)
                    chain(dve.reciprocal(col[:, 3, :], col[:, 2, :]))
                    chain(dve.tensor_scalar(col[:, 1, 0:1], col[:, 6, 1:2], 1.0 / D, None, ALU.mult))
                    chain(dve.tensor_scalar(col[:, 4, 0:1], col[:, 1, 0:1], 0.1, None, ALU.mult))
                    chain(dve.tensor_scalar(col[:, 5, :], col[:, 3, :], col[:, 4, 0:1], None, ALU.mult))
                    chain(dve.tensor_scalar(col[:, 6, 0:1], col[:, 1, 0:1], 1e-8, None, ALU.is_gt))
                    chain(dve.scalar_tensor_tensor(prune[:, 0], WT[:, :, :], -1.0, WT[:, :, :], ALU.mult, ALU.max))
                    for k in range(KC):
                        chain(dve.tensor_scalar(prune[:, 1, k, :], prune[:, 0, k, :], col[:, 5, k:k + 1],
                                                col[:, 6, 0:1], ALU.is_lt, ALU.mult))
                    chain(dve.tensor_tensor(prune[:, 0], prune[:, 1], WT[:, :, :], ALU.mult))
                    chain(dve.tensor_tensor(WT[:, :, :], WT[:, :, :], prune[:, 0], ALU.subtract))
                    dve.sem_inc(W_ready, 1)
                    with dve.Fori(0, (BATCHES - 2 * GROUPS) // 2 - 1) as i:
                        for s in range(2):
                            one_hots((i * 2 + (s + 2 * GROUPS + 2)) * BATCH, s, i * 2 + (s + 2 * GROUPS + 2))
                    chain = Chain(dve, rows_float, 3)
                    dve.wait_ge(h_down, GROUPS)
                    dve.wait_ge(hist_done, BATCHES + 3)
                    chain(dve.tensor_tensor(junk[:, 0:3 * WINDOWS].rearrange("p (a w) -> p a w", a=3),
                                             ps[:, 5, 0:3 * WINDOWS].rearrange("p (a w) -> p a w", a=3),
                                             norms[:, :].unsqueeze(1).to_broadcast([P, 3, WINDOWS]), ALU.mult))
                    chain(dve.tensor_reduce(col[:, 7, 0:1], junk[:, 0:3 * WINDOWS], AX.X, ALU.add))
                    dve.sem_inc(sum_up, 1)
                    dve.wait_ge(thr_up, 1)
                    chain(dve.tensor_scalar(thr[:, :], ps[:, 7, 4:5], 1.0 / E, 0.1, ALU.mult, ALU.mult))

                @block.tensor
                def _(pe):
                    pe.sem_inc(xn_turned, GROUP)
                    pe.sem_inc(h_up, 1)
                    pe.sem_inc(hist_done, 2)
                    pe.wait_ge(lock_hot, 1)
                    for t in range(8):
                        last = pe.matmul(ps[0:WINDOWS, 6, 0:P], oneA[:, 0, :, t], oneB[:, 0, :, t],
                                         start=(t == 0), stop=(t == 7))
                    last.then_inc(lock_up, 1)
                    pe.matmul(ps[:, 5, 0:3 * WINDOWS], zero_mm[:, 0:P], zero_mm[:, :], start=True,
                              stop=False, skip_group_check=True)

                    def histogram(n, s):
                        pe.wait_ge(one_hots_ready, n + 1)
                        for t in range(BATCH):
                            last = pe.matmul(ps[:, 5, 0:3 * WINDOWS], oneB[:, s, :, t],
                                             partA[:, s, :, :, t].rearrange("p a w -> p (a w)"),
                                             start=False, stop=False, skip_group_check=True)
                        last.then_inc(hist_done, 1)

                    with pe.Fori(0, GROUPS) as g:
                        histogram(g * 2, 0)
                        for j in range(GROUP):
                            if j < ACT_NORMS:
                                pe.wait_ge(xn_ready, g * ACT_NORMS + j + 1)
                            else:
                                pe.wait_ge(xn_ready_dve, g * (GROUP - ACT_NORMS) + (j - ACT_NORMS) + 1)
                            if j == 0:
                                pe.wait_ge(xT_saved, g * KC + KC)
                            for k in range(KC):
                                last = pe.transpose(psf[:, k * 1024 + j * P:k * 1024 + (j + 1) * P],
                                                    xn[:, j, k * P:(k + 1) * P], ident[:, :])
                            last.then_inc(xn_turned, 1)
                        histogram(g * 2 + 1, 1)
                    for n in range(2 * GROUPS, 2 * GROUPS + 2):
                        histogram(n, n % 2)
                    pe.wait_ge(colsum_ready, 1)
                    pe.matmul(ps[:, 7, 0:KC], ones[:, :], col[:, 0, :], start=True, stop=True).then_inc(total_ready, 1)
                    pe.wait_ge(W_ready, 1)
                    with pe.Fori(0, GROUPS) as g:
                        for j in range(GROUP):
                            pe.wait_ge(xT_slot, g * GROUP + j + 1)
                            pe.wait_ge(h_norm, g * GROUP + j + 1)
                            for k in range(KC):
                                last = pe.matmul(ps[:, 2 + h_slot(j), 0:D], xT[:, h_slot(j), k, :], WT[:, k, :],
                                                 start=(k == 0), stop=(k == KC - 1))
                            last.then_inc(h_up, 1)
                            if j in (1, 3, 5, 6):
                                at = (1, 3, 5, 6).index(j)
                                histogram(g * 4 + (2 * GROUPS + 2 + at), at % 2)
                    with pe.Fori(0, (BATCHES - 6 * GROUPS) // 2 - 1) as i:
                        for s in range(2):
                            histogram(i * 2 + (6 * GROUPS + 2 + s), s)
                    pe.matmul(ps[:, 5, 0:3 * WINDOWS], zero_mm[:, 0:P], zero_mm[:, :], start=False,
                              stop=True, skip_group_check=True).then_inc(hist_done, 1)
                    pe.wait_ge(sum_up, 1)
                    pe.matmul(ps[:, 7, 4:5], ones[:, :], col[:, 7, 0:1], start=True, stop=True).then_inc(thr_up, 1)

                @block.scalar
                def _(act):
                    act.copy(iota_t[:, :, :], iota_row[:, 0:P].unsqueeze(2).to_broadcast([P, P, BATCH])
                             ).then_inc(iota_ready, 1)
                    act.sem_inc(xT_saved, KC)
                    act.sem_inc(h_norm, 2)
                    with act.Fori(0, GROUPS) as g:
                        act.wait_ge(var_ready, g + 1)
                        act.activation(std[:, :], mv[:, :, 1], ACT.Sqrt, bias=eps_col[:, :]).then_inc(std_ready, 1)
                        act.wait_ge(scale_ready, g + 1)
                        act.wait_ge(xn_turned, (g + 1) * GROUP)
                        for j in range(ACT_NORMS):
                            act.activation(xn[:, j, :], acc[:, bass.ds(g * GROUP + j, 1), :]
                                           .rearrange("p a d -> p (a d)"), ACT.Identity, scale=rstd[:, 0, j:j + 1],
                                           bias=rstd[:, 1, j:j + 1]).then_inc(xn_ready, 1)
                        act.wait_ge(xn_turned, (g + 2) * GROUP)
                        for k in range(KC):
                            act.copy(xnT[:, k, bass.ds(g * GROUP * P, GROUP * P)],
                                     psf[:, k * 1024:k * 1024 + GROUP * P])
                            act.activation(junk_rows[:, :], psf[:, k * 1024:k * 1024 + GROUP * P], ACT.Square,
                                           accum_out=colsq[:, k, bass.ds(g, 1)]).then_inc(xT_saved, 1)
                            act.wait_ge(xT_saved, g * KC + k + 1 + KC)
                    act.sem_inc(colsq_ready, KC * GROUPS)
                    act.wait_ge(sums_ready, 1)
                    act.activation(col[:, 2, :], col[:, 0, :], ACT.Sqrt)
                    act.activation(col[:, 6, 1:2], col[:, 1, 0:1], ACT.Sqrt).then_inc(norms_ready, 1)
                    act.copy(xT[:, 0], xnT[:, :, 0:P]).then_inc(xT_slot, 1)

                    def keep_h(g, s, use, last):
                        for j in range(GROUP):
                            act.copy(xT[:, h_slot((j + 1) % GROUP)], xnT[:, :, bass.ds((g * GROUP + j + 1) * P, P)]
                                     ).then_inc(xT_slot, 1)
                            act.wait_ge(h_up, g * GROUP + j + 2)
                            if j == 0:
                                act.wait_ge(h_free, g + 1)
                            act.copy(hrow[:, s, j, 0:D], ps[:, 2 + h_slot(j), 0:D])
                            act.wait_ge(h_norm, g * GROUP + j + 2)
                            act.activation(junk[:, 0:D], ps[:, 2 + h_slot(j), 0:D], ACT.Square,
                                           accum_out=nsq[:, s, j:j + 1]).then_inc(h_norm, 1)
                        act.wait_ge(h_norm, g * GROUP + GROUP + 2)
                        act.activation(norms[:, bass.ds(g * GROUP, GROUP)], nsq[:, s, :], ACT.Sqrt)
                        act.activation(hrow[:, s, :, D], nsq[:, s, :], ACT.Sqrt).then_inc(h_down, 1)

                    by_groups(act, keep_h, 2)

                @block.sync
                def _(sp):
                    sp.wait_ge(lock_up, 2)
                    sp.dma_start(lock_dram, lockhist[0:WINDOWS, :]).then_inc(lock_out, 16)
                    sp.wait_ge(lock_out, 16)
                    sp.wait_ge(W_ready, 1)
                    sp.dma_start(lockrow[:, 0:WINDOWS * P],
                                 lock_dram.rearrange("(a w) e -> a (w e)", a=1).to_broadcast([P, WINDOWS * P])
                                 ).then_inc(lock_back, 16)
                    sp.sem_inc(h_free, 2)

                    def store_h(g, s, use, last):
                        sp.wait_ge(h_down, g + 1)
                        sp.dma_start(h_dram[bass.ds(g * (GROUP * P), GROUP * P), :]
                                     .rearrange("(w p) d -> p w d", p=P), hrow[:, s]).then_inc(h_out, 16)
                        sp.wait_ge(h_out, (g + 1) * 16)
                        sp.sem_inc(h_free, 1)

                    by_groups(sp, store_h, 2)
                    sp.wait_ge(h_out, GROUPS * 16)
                    sp.wait_ge(lock_back, 16)

        RPAR = EXPERTS * HC + 2 * KC
        param_rows = sb("param_rows", [RPAR, P])
        Wr_sb = sb("Wr_sb", [P, KC, EXPERTS])
        br_b = sb("br_b", [P, EXPERTS])
        bias_b = sb("bias_b", [P, D])

        with ExitStack() as c2:
            def sb2(name, shape, dt=F32):
                return c2.enter_context(nc.sbuf_tensor(name, shape, dt))

            def sem2(name):
                return c2.enter_context(nc.semaphore(name))

            tile_tab = sb2("tile_tab", [P, TAB], I32)
            win_tab = sb2("win_tab", [P, TAB], I32)
            win_base = sb2("win_base", [P, TAB])
            in_window = sb2("in_window", [P, TAB], BF16)
            tile_sum = sb2("tile_sum", [P, TAB])
            bounds = sb2("bounds", [P, 8])
            table_rows = sb2("table_rows", [P, 3, P], BF16)
            recs = sb2("recs", [P, PACKS, PACK, 4])
            src_idx = sb2("src_idx", [P, PACKS, PACK], I32)
            coef = sb2("coef", [P, PACKS, 8, PACK])
            keepw2 = sb2("keepw2", [P, 2, PACK, P])
            GSIZE = PACK * HROW
            places = [tail_region[:, q * GSIZE:(q + 1) * GSIZE] for q in range(2)]
            places += [w2_sb[:, q * GSIZE:(q + 1) * GSIZE] for q in range(PACKS - 2)]
            G = [place.rearrange("p (u d) -> p u d", u=PACK) for place in places]
            at = (PACKS - 2) * GSIZE
            keepw3 = w2_sb[:, at:at + PACK * P].rearrange("p (u n) -> p u n", u=PACK)
            keepw = [keepw3 if s == PACKS - 1 else keepw2[:, s % 2] for s in range(PACKS)]
            at += PACK * P
            S = w2_sb[:, at:at + 4 * P].rearrange("p (q n) -> p q n", q=4)
            zeros = w2_sb[:, at + 4 * P:at + 4 * P + D]
            TH = TAB // 2

            steps_placed, tab_up, tab_ready = sem2("steps_placed"), sem2("tab_up"), sem2("tab_ready")
            tiles_known = sem2("tiles_known")
            table_steps = sem2("table_steps")
            recs_ready, idx_ready = sem2("recs_ready"), sem2("idx_ready")
            gathered = [[sem2(f"gathered{s}{q}") for q in range(PACK // 2)] for s in range(PACKS)]
            assert ROUNDS * ITERS * 32 < 1 << 16 and ROUNDS * STEPS + PACKS * PACK < 1 << 16
            coef_steps, coef_ready, keep_ready = sem2("coef_steps"), sem2("coef_ready"), sem2("keep_ready")
            S_ready, messages_up, acc_done = sem2("S_ready"), sem2("messages_up"), sem2("acc_done")
            params_in = sem2("params_in")
            gated, pack_in = sem2("gated"), sem2("pack_in")
            zeros_set, zeroed, weights_in = sem2("zeros_set"), sem2("zeroed"), sem2("weights_in")

            def value(engine, ap, top):
                _, values = nc.values_load_multi_w_load_instructions(
                    ap, engines=[engine.engine], min_val=0, max_val=top,
                    skip_runtime_bounds_check_because="the tables hold tile and window numbers only")
                return values

            with nc.Block() as block:
                @block.sync
                def _(sp):
                    sp.dma_start(w1_sb.rearrange("p (a h) -> p a h", h=H),
                                 W1.rearrange("e (c k) h -> k (e c) h", k=P)).then_inc(weights_in, 16)
                    chunks = EXPERTS * HC
                    sp.dma_start(param_rows[0:chunks, :], b1.rearrange("e (c h) -> (e c) h", h=P)).then_inc(params_in, 16)
                    sp.dma_start(param_rows[chunks:chunks + KC, :], gamma.rearrange("(c k) -> c k", k=P)
                                 ).then_inc(params_in, 16)
                    sp.dma_start(param_rows[chunks + KC:RPAR, :], beta.rearrange("(c k) -> c k", k=P)
                                 ).then_inc(params_in, 16)
                    sp.dma_start(br_b[:, :], br.rearrange("(a d) -> a d", a=1).to_broadcast([P, EXPERTS])
                                 ).then_inc(params_in, 16)
                    sp.dma_start(Wr_sb[:, :, :], Wr.rearrange("(c k) e -> k c e", k=P)).then_inc(params_in, 16)
                    sp.dma_start(bias_b[:, :], b.rearrange("(a d) -> a d", a=1).to_broadcast([P, D])
                                 ).then_inc(params_in, 16)
                    sp.wait_ge(zeros_set, 1)
                    for t in range(EXPERTS):
                        sp.dma_start(xs_dram[IDLE + t * P:IDLE + (t + 1) * P, :], zeros[:, :]).then_inc(zeroed, 16)
                    rounds = sp.value_load(rounds_i[0:1, 0:1], min_val=1, max_val=ROUNDS)
                    with sp.Fori(0, rounds) as r:
                        with sp.Fori(0, ITERS) as i:
                            for s in range(PACKS):
                                for q in range(PACK // 2):
                                    sp.wait_ge(gathered[s][q], (r * ITERS + i + 1) * 32)
                                sp.sem_inc(pack_in, 1)
                    sp.wait_ge(zeroed, 16 * EXPERTS)
                    sp.wait_ge(weights_in, 16)
                    sp.wait_ge(params_in, 6 * 16)

                @block.gpsimd
                def _(pool):
                    pool.sem_inc(gated, 1)
                    nc.gpsimd.memset(zeros[:, :], 0.0).then_inc(zeros_set, 1)
                    pool.wait_ge(zeros_set, 1)
                    rounds = pool.value_load(rounds_i[0:1, 0:1], min_val=1, max_val=ROUNDS)
                    with pool.Fori(0, rounds) as r:
                        with pool.Fori(0, ITERS) as i:
                            for s in range(PACKS):
                                pack = r * (PACKS * ITERS) + i * PACKS + s
                                pool.wait_ge(idx_ready, pack + 1)
                                pool.wait_ge(messages_up, pack * PACK + PACK)
                                pool.wait_ge(gated, pack + 1)
                                nc.gpsimd.tensor_tensor(gate[:, 0:1], zeros[:, 0:1], zeros[:, 1:2],
                                                        ALU.add).then_inc(gated, 1)
                                for u in range(PACK):
                                    nc.gpsimd.indirect_dma_start(
                                        G[s][:, u, :], None, h_dram,
                                        bass.IndirectOffsetOnAxis(ap=src_idx[:, s, u:u + 1], axis=0)
                                    ).then_inc(gathered[s][u // 2], 16)

                @block.scalar
                def _(act):
                    def fetch(s, tiles, pack):
                        for u in range(PACK):
                            last = act.copy(recs[:, s, u, :], rec[:, bass.ds(tiles[u], 1), :]
                                            .rearrange("p a c -> p (a c)"))
                        last.then_inc(recs_ready, 1)
                        act.wait_ge(recs_ready, pack + 1)
                        act.copy(src_idx[:, s, :], recs[:, s, :, 0]).then_inc(idx_ready, 1)

                    def tiles_at(at):
                        return value(act, tile_tab[0:1, bass.ds(at, PACK)], TILES - 1)

                    act.wait_ge(tiles_known, 1)
                    for s in range(AHEAD):
                        fetch(s, tiles_at(s * PACK), s)
                    rounds = act.value_load(rounds_i[0:1, 0:1], min_val=1, max_val=ROUNDS)
                    with act.Fori(0, rounds) as r:
                        act.wait_ge(tab_ready, r + 1)
                        with act.Fori(0, ITERS) as i:
                            for s in range(PACKS):
                                pack = r * (PACKS * ITERS) + i * PACKS + s
                                fetch((s + AHEAD) % PACKS, tiles_at((i * PACKS + (s + AHEAD)) * PACK), pack + AHEAD)
                                wins = value(act, win_tab[0:1, bass.ds((i * PACKS + s) * PACK, PACK)], DUMMY)
                                act.wait_ge(coef_ready, pack + 1)
                                act.wait_ge(S_ready, pack * PACK + PACK)
                                for u in range(PACK):
                                    act.activation(keepw[s][:, u, :], lockrow[:, bass.ds(wins[u] * P, P)],
                                                   ACT.Identity, scale=coef[:, s, 5, u:u + 1],
                                                   bias=coef[:, s, 4, u:u + 1]).then_inc(keep_ready, 1)

                @block.tensor
                def _(pe):
                    pe.sem_inc(messages_up, PACKS * PACK)
                    rounds = pe.value_load(rounds_i[0:1, 0:1], min_val=1, max_val=ROUNDS)

                    def tables_up(r):
                        pe.wait_ge(steps_placed, r + 1)
                        for q in range(2):
                            steps = in_window[0:SLOTS_W, q * TH:(q + 1) * TH]
                            for part in range(2):
                                pe.matmul(ps[:, q, 0:TH], table_rows[0:SLOTS_W, part, :], steps,
                                          start=(part == 0), stop=(part == 1))
                            last = pe.matmul(ps[:, 2 + q, 0:TH], table_rows[0:SLOTS_W, 2, :], steps,
                                             start=True, stop=True)
                        last.then_inc(tab_up, 1)

                    with pe.Fori(0, rounds) as r:
                        tables_up(r)
                        with pe.Fori(0, ITERS) as i:
                            for s in range(PACKS):
                                for u in range(PACK):
                                    step = (r * (PACKS * ITERS) + i * PACKS + s) * PACK + u
                                    pe.wait_ge(S_ready, step + 17)
                                    pe.wait_ge(acc_done, step + 1)
                                    pe.matmul(ps[:, 4 + u % 4, 0:D], S[:, u % 4, :], G[s][:, u, 0:D],
                                              start=True, stop=True).then_inc(messages_up, 1)

                @block.vector
                def _(dve):
                    dve.sem_inc(S_ready, 16)
                    dve.sem_inc(acc_done, 4)
                    wn = slice(0, SLOTS_W)

                    def coefs(s, at, pack):
                        dve.wait_ge(pack_in, pack + 1)
                        c = Chain(dve, coef_steps, pack * 4)
                        norm, w, loops = G[s][:, :, D], recs[:, s, :, 2], recs[:, s, :, 3]
                        dve.tensor_tensor(coef[:, s, 6, :], recs[:, s, :, 1], win_base[:, bass.ds(at, PACK)],
                                          ALU.subtract)
                        c(dve.tensor_tensor(coef[:, s, 0, :], norm, w, ALU.mult))
                        c(dve.scalar_tensor_tensor(coef[:, s, 1, :], coef[:, s, 0, :], -1.0, coef[:, s, 0, :],
                                                   ALU.mult, ALU.max))
                        c(dve.scalar_tensor_tensor(coef[:, s, 2, :], coef[:, s, 1, :], thr[:, 0:1], loops,
                                                   ALU.is_ge, ALU.max))
                        c(dve.tensor_tensor(coef[:, s, 4, :], coef[:, s, 2, :], w, ALU.mult))
                        dve.tensor_tensor(coef[:, s, 5, :], w, coef[:, s, 4, :], ALU.subtract).then_inc(coef_ready, 1)

                    def make_tables(r):
                        c = Chain(dve, table_steps, r * 12 + 1)
                        c(dve.tensor_scalar(in_window[wn, :], iota_row[wn, :], bounds[wn, 1:2], None, ALU.is_lt))
                        c(dve.scalar_tensor_tensor(in_window[wn, :], iota_row[wn, :], bounds[wn, 0:1],
                                                   in_window[wn, :], ALU.is_ge, ALU.mult))
                        c(dve.tensor_scalar(table_rows[wn, 0, :], ones[wn, :], bounds[wn, 2:3], None, ALU.mult))
                        c(dve.scalar_tensor_tensor(table_rows[wn, 1, :], ones[wn, :], bounds[wn, 2:3],
                                                   table_rows[wn, 0, :], ALU.mult, ALU.subtract))
                        c(dve.tensor_scalar(table_rows[wn, 2, :], ones[wn, :], ntab[wn, 6:7], None, ALU.mult))
                        dve.sem_inc(steps_placed, 1)
                        c(dve.tensor_scalar(bounds[wn, 0:2], bounds[wn, 0:2], float(-STEPS), None, ALU.add))
                        c(dve.tensor_scalar(bounds[wn, 2:3], bounds[wn, 2:3], float(STEPS), None, ALU.add))
                        dve.wait_ge(tab_up, r + 1)
                        two = lambda t: t.rearrange("p (q n) -> p q n", q=2)
                        c(dve.tensor_tensor(two(tile_sum[:, :]), ps[:, 0:2, 0:TH], two(iota_row[:, :]), ALU.add))
                        c(dve.tensor_scalar(tile_tab[:, :], tile_sum[:, :], float(TILES - 1), None, ALU.min))
                        dve.sem_inc(tiles_known, 1)
                        c(dve.tensor_scalar(two(win_tab[:, :]), ps[:, 2:4, 0:TH], float(DUMMY), None, ALU.add))
                        c(dve.tensor_scalar(two(win_base[:, :]), ps[:, 2:4, 0:TH], float(DUMMY), float(P),
                                            ALU.add, ALU.mult))
                        c(dve.memset(gate[:, 1:2], 0.0))
                        dve.sem_inc(tab_ready, 1)
                    c = Chain(dve, table_steps)
                    c(dve.tensor_copy(bounds[wn, 0:3], ntab[wn, 3:6]))
                    rounds = dve.value_load(rounds_i[0:1, 0:1], min_val=1, max_val=ROUNDS)
                    def add_messages(r, i, s, last):
                        pack = r * (PACKS * ITERS) + i * PACKS + s
                        wins = value(dve, win_tab[0:1, bass.ds((i * PACKS + s) * PACK, PACK)], DUMMY)

                        def add(u):
                            step = pack * PACK + u
                            dve.wait_ge(messages_up, step + (PACKS * PACK + 1))
                            dve.wait_ge(acc_done, step + 4)
                            at = acc[:, bass.ds(wins[u], 1), :].rearrange("p a d -> p (a d)")
                            dve.tensor_tensor(at, at, ps[:, 4 + u % 4, 0:D], ALU.add).then_inc(acc_done, 1)

                        for u in range(PACK):
                            step = pack * PACK + u
                            dve.wait_ge(keep_ready, step + 1)
                            dve.wait_ge(messages_up, step + (PACKS * PACK - 3))
                            dve.scalar_tensor_tensor(S[:, u % 4, :], iota_row[:, 0:P], coef[:, s, 6, u:u + 1],
                                                     keepw[s][:, u, :], ALU.is_equal,
                                                     ALU.mult).then_inc(S_ready, 1)
                            if u >= 2:
                                add(u - 2)
                        if not last:
                            coefs((s + 1) % PACKS, (i * PACKS + (s + 1)) * PACK, pack + 1)
                        add(PACK - 2)
                        add(PACK - 1)

                    with dve.Fori(0, rounds) as r:
                        make_tables(r)
                        coefs(0, 0, r * (PACKS * ITERS))
                        with dve.Fori(0, ITERS - 1) as i:
                            for s in range(PACKS):
                                add_messages(r, i, s, False)
                        for s in range(PACKS):
                            add_messages(r, ITERS - 1, s, s == PACKS - 1)

        weight_k = sb("weight_k", [P, 2, WINDOWS])
        pos_k = sb("pos_k", [P, 2, WINDOWS], I32)
        tile_expert = sb("tile_expert", [P, FTILES], I32)
        tile_row = sb("tile_row", [P, FTILES], I32)
        b1T = sb("b1T", [P, EXPERTS * HC])
        b2_b = sb("b2_b", [P, EXPERTS, D])

        XG = 3
        with ExitStack() as c3:
            def sb3(name, shape, dt=F32):
                return c3.enter_context(nc.sbuf_tensor(name, shape, dt))

            def sem3(name):
                return c3.enter_context(nc.semaphore(name))

            param_cols = sb3("param_cols", [P, RPAR])
            gamma_col = param_cols[:, EXPERTS * HC:EXPERTS * HC + KC]
            beta_col = param_cols[:, EXPERTS * HC + KC:RPAR]
            beta_wide = sb3("beta_wide", [P, KC, P])
            Wr_scaled = sb3("Wr_scaled", [P, KC, EXPERTS])
            xg = scratch[:, 0:XG * GROUP * D].rearrange("p (s w d) -> p s w d", s=XG, w=GROUP)
            xTg = scratch[:, XG * GROUP * D:(XG + 1) * GROUP * D].rearrange("p (c n) -> p c n", c=KC)
            stat = sb3("stat", [P, GROUP, 6])
            mv3 = sb3("mv3", [P, XG, GROUP, 2])
            sd = sb3("sd", [P, XG, GROUP])
            sc = sb3("sc", [P, XG, 2, GROUP])
            eps2 = sb3("eps2", [P, 1])
            iota_e = sb3("iota_e", [P, GROUP, EXPERTS])
            iota_low = sb3("iota_low", [P, GROUP, EXPERTS])
            logits = sb3("logits", [P, GROUP, EXPERTS])
            masked = sb3("masked", [P, GROUP, EXPERTS])
            hot = sb3("hot", [P, 2, GROUP, EXPERTS])
            work = sb3("work", [P, 2, GROUP, EXPERTS])
            both = sb3("both", [P, GROUP + 1, EXPERTS])
            pos = sb3("pos", [P, GROUP, EXPERTS])
            least = sb3("least", [P, 2, GROUP])
            tops = sb3("tops", [P, 2, WINDOWS])
            soft = sb3("soft", [P, 3, WINDOWS])
            ratio = sb3("ratio", [P, WINDOWS])
            exists = sb3("exists", [P, WINDOWS])
            spare_row = sb3("spare_row", [P, 2, WINDOWS])
            row_base = sb3("row_base", [P, EXPERTS])
            row_base_i = sb3("row_base_i", [P, EXPERTS], I32)
            region = sb3("region", [P, EXPERTS])
            pos_slot = sb3("pos_slot", [P, XG, 2, GROUP], I32)
            e_tab = sb3("e_tab", [P, 3, EXPERTS + 1])
            e_int = sb3("e_int", [P, EXPERTS], I32)
            te = scratch[:, (XG + 1) * GROUP * D:(XG + 1) * GROUP * D + FTILES * EXPERTS].rearrange("p (t e) -> p t e", e=EXPERTS)
            te_f = sb3("te_f", [P, FTILES])
            pos_all = sb3("pos_all", [P, 2, WINDOWS])
            past = scratch[:, (XG + 1) * GROUP * D:(XG + 1) * GROUP * D + 2 * WINDOWS * EXPERTS].rearrange(
                "p (k w e) -> p k w e", k=2, w=WINDOWS)
            zeros3 = sb3("zeros3", [P, D])

            out_weights_in = sem3("out_weights_in")
            weights_turned, param_steps = sem3("weights_turned"), sem3("param_steps")
            param_kept, beta_up = sem3("param_kept"), sem3("beta_up")
            b1_up = sem3("b1_up")
            stat_steps, var3, std3, scale3, normed = sem3("stat_steps"), sem3("var3"), sem3("std3"), sem3("scale3"), sem3("normed")
            turned3, xT3, routed3, logits3 = sem3("turned3"), sem3("xT3"), sem3("routed3"), sem3("logits3")
            route_steps, both_ready, counts_up = sem3("route_steps"), sem3("both_ready"), sem3("counts_up")
            rows_ready, rows_free, gated3 = sem3("rows_ready"), sem3("rows_free"), sem3("gated3")
            sent = [sem3(f"sent{s}") for s in range(XG)]
            soft_in, exp_out, ends_ready, ends_out = sem3("soft_in"), sem3("exp_out"), sem3("ends_ready"), sem3("ends_out")
            end_steps = sem3("end_steps")

            with nc.Block() as block:
                @block.sync
                def _(sp):
                    sp.dma_start(b2_b[:, :, :].rearrange("p e d -> p (e d)"),
                                 b2.rearrange("(a e) d -> a (e d)", a=1).to_broadcast([P, EXPERTS * D])
                                 ).then_inc(out_weights_in, 16)
                    sp.dma_start(w2_sb.rearrange("p (a d) -> p a d", d=D),
                                 W2.rearrange("e (c k) d -> k (e c) d", k=P)).then_inc(out_weights_in, 16)
                    sp.sem_inc(rows_free, XG)

                    def tell_sent(g, s, use, last):
                        sp.wait_ge(sent[s], use * (2 * GROUP * 16))
                        sp.sem_inc(rows_free, 1)

                    by_groups(sp, tell_sent, XG)
                    sp.wait_ge(ends_ready, 1)
                    ends = value(sp, row_base_i[0:1, 0:EXPERTS], IDLE)
                    for e in range(EXPERTS):
                        sp.dma_start(xs_dram[bass.ds(ends[e], P), :], zeros3[:, :]).then_inc(ends_out, 16)
                    sp.wait_ge(ends_out, EXPERTS * 16)
                    sp.wait_ge(out_weights_in, 32)

                @block.vector
                def _(dve):
                    c = Chain(dve, param_steps)
                    across = lambda ap: ap.unsqueeze(1).to_broadcast([P, GROUP, EXPERTS])
                    dve.memset(eps2[:, :], EPS * EPS)
                    dve.memset(zeros3[:, :], 0.0)
                    dve.memset(both[:, :, :], 0.0)
                    dve.tensor_copy(iota_e[:, :, :], across(iota_row[:, 0:EXPERTS]))
                    dve.tensor_scalar(iota_low[:, :, :], across(iota_row[:, 0:EXPERTS]), -BIG, None, ALU.add)
                    dve.tensor_scalar(region[:, :], iota_row[:, 0:EXPERTS], float(REGION), None, ALU.mult)
                    dve.tensor_scalar(row_base[:, :], iota_row[:, 0:EXPERTS], float(REGION), None, ALU.mult)
                    c(dve.tensor_scalar(exists[:, :], iota_row[:, 0:WINDOWS], float(P), pid[:, :], ALU.mult, ALU.add))
                    c(dve.tensor_scalar(exists[:, :], exists[:, :], float(N), None, ALU.is_lt))
                    c(dve.tensor_scalar(soft[:, 0, :], exists[:, :], -1.0, 1.0, ALU.mult, ALU.add))
                    c(dve.tensor_scalar(soft[:, 1, 0:1], pid[:, :], float(SPARE), None, ALU.add))
                    c(dve.tensor_scalar(soft[:, 2, 0:1], pid[:, :], float(SPARE + P), None, ALU.add))
                    for k in range(2):
                        c(dve.tensor_scalar(spare_row[:, k, :], soft[:, 0, :], soft[:, 1 + k, 0:1], None, ALU.mult))
                    def stats(g, s):
                        c = Chain(dve, stat_steps, g * 4)
                        at = acc[:, bass.ds(g * GROUP, GROUP), :]
                        c(dve.tensor_tensor(at, at, bias_b[:, :].unsqueeze(1).to_broadcast([P, GROUP, D]), ALU.add))
                        dve.memset(gate[:, 2:3], 0.0)
                        for j in range(GROUP):
                            last = dve.bn_stats(stat[:, j, :], acc[:, bass.ds(g * GROUP + j, 1), :]
                                                .rearrange("p a d -> p (a d)"))
                        c(last)
                        dve.memset(gate[:, 2:3], 0.0)
                        for j in range(GROUP):
                            last = dve.bn_aggr(mv3[:, s, j, :], stat[:, j, :])
                        last.then_inc(var3, 1)
                        dve.wait_ge(std3, g + 1)
                        c(dve.reciprocal(sc[:, s, 0, :], sd[:, s, :]))
                        c(dve.scalar_tensor_tensor(sc[:, s, 1, :], mv3[:, s, :, 0], -1.0, sc[:, s, 0, :],
                                                   ALU.mult, ALU.mult))
                        dve.sem_inc(scale3, 1)

                    def route(g, s, use, last):
                        if not last:
                            stats(g + 1, (s + 1) % XG)
                        c = Chain(dve, route_steps, g * 19)
                        over = lambda column: column.unsqueeze(2).to_broadcast([P, GROUP, EXPERTS])
                        windows = bass.ds(g * GROUP, GROUP)
                        dve.wait_ge(routed3, g + 2)
                        c(dve.tensor_tensor(logits[:, :, :],
                                            ps[:, 4, 0:GROUP * EXPERTS].rearrange("p (w e) -> p w e", w=GROUP),
                                            across(br_b[:, :]), ALU.add))
                        dve.sem_inc(logits3, 1)
                        for k, scores in enumerate((logits, masked)):
                            top = tops[:, k, windows]
                            c(dve.tensor_reduce(top, scores[:, :, :], AX.X, ALU.max))
                            c(dve.tensor_tensor(work[:, 0], scores[:, :, :], over(top), ALU.is_ge))
                            c(dve.scalar_tensor_tensor(work[:, 1], work[:, 0], -BIG, iota_e[:, :, :], ALU.mult, ALU.add))
                            c(dve.tensor_reduce(least[:, k, :], work[:, 1], AX.X, ALU.min))
                            c(dve.tensor_tensor(hot[:, k], iota_low[:, :, :], over(least[:, k, :]), ALU.is_equal))
                            if k == 0:
                                c(dve.scalar_tensor_tensor(masked[:, :, :], hot[:, 0], -3e38, logits[:, :, :],
                                                           ALU.mult, ALU.add))
                        c(dve.tensor_tensor(both[:, 0:GROUP, :], hot[:, 0], hot[:, 1], ALU.add))
                        c(dve.tensor_tensor(both[:, 0:GROUP, :], both[:, 0:GROUP, :], over(exists[:, windows]), ALU.mult))
                        dve.sem_inc(both_ready, 1)
                        dve.wait_ge(counts_up, g + 1)
                        counts = ps[:, 5, 0:(GROUP + 1) * EXPERTS].rearrange("p (w e) -> p w e", e=EXPERTS)
                        c(dve.tensor_tensor(pos[:, :, :], counts[:, 0:GROUP, :], across(row_base[:, :]), ALU.add))
                        dve.tensor_tensor(row_base[:, :], row_base[:, :], counts[:, GROUP, :], ALU.add)
                        c(dve.tensor_tensor(work[:, :], hot[:, :],
                                            pos[:, :, :].unsqueeze(1).to_broadcast([P, 2, GROUP, EXPERTS]), ALU.mult))
                        c(dve.tensor_reduce(least[:, :, :], work[:, :], AX.X, ALU.add))
                        c(dve.tensor_tensor(least[:, :, :], least[:, :, :],
                                            exists[:, windows].unsqueeze(1).to_broadcast([P, 2, GROUP]), ALU.mult))
                        dve.wait_ge(rows_free, g + 1)
                        dve.tensor_tensor(pos_slot[:, s], least[:, :, :], spare_row[:, :, windows],
                                          ALU.add).then_inc(rows_ready, 1)
                        c(dve.tensor_copy(pos_all[:, :, windows], least[:, :, :]))

                    stats(0, 0)
                    dve.wait_ge(weights_turned, 1)
                    c = Chain(dve, param_steps, 7)
                    c(dve.tensor_copy(param_cols[:, :], ps[:, 7, 0:RPAR]))
                    for k in range(KC):
                        dve.tensor_scalar(beta_wide[:, k, :], ones[:, :], beta_col[:, k:k + 1], None, ALU.mult)
                        c(dve.tensor_scalar(Wr_scaled[:, k, :], Wr_sb[:, k, :], gamma_col[:, k:k + 1], None, ALU.mult))
                    dve.sem_inc(param_kept, 1)
                    dve.wait_ge(beta_up, 1)
                    c(dve.tensor_tensor(br_b[:, :], br_b[:, :], ps[:, 6, 0:EXPERTS], ALU.add))
                    dve.sem_inc(logits3, 1)
                    by_groups(dve, route, XG)
                    c = Chain(dve, end_steps)
                    c(dve.tensor_copy(row_base_i[:, :], row_base[:, :]))
                    dve.sem_inc(ends_ready, 1)
                    c(dve.tensor_tensor(soft[:, 0, :], tops[:, 1, :], tops[:, 0, :], ALU.subtract))
                    dve.sem_inc(soft_in, 1)
                    c(dve.tensor_tensor(e_tab[:, 0, 0:EXPERTS], row_base[:, :], region[:, :], ALU.subtract))
                    c(dve.tensor_scalar(e_int[:, :], e_tab[:, 0, 0:EXPERTS], float(P - 1), None, ALU.add))
                    c(dve.tensor_scalar(e_int[:, :], e_int[:, :], 7, None, ALU.arith_shift_right))
                    c(dve.tensor_copy(e_tab[:, 0, 0:EXPERTS], e_int[:, :]))
                    c(dve.tensor_copy(e_tab[:, 1, 0:1], e_tab[:, 0, 0:1]))
                    for e in range(1, EXPERTS):
                        c(dve.tensor_tensor(e_tab[:, 1, e:e + 1], e_tab[:, 1, e - 1:e], e_tab[:, 0, e:e + 1], ALU.add))
                    c(dve.tensor_scalar(e_tab[:, 2, 0:EXPERTS], e_tab[:, 0, 0:EXPERTS], float(-P), float(REGION),
                                        ALU.mult, ALU.add))
                    tiles_by = lambda ap: ap.unsqueeze(1).to_broadcast([P, FTILES, EXPERTS])
                    c(dve.tensor_tensor(te[:, :, :], iota_row[:, 0:FTILES].unsqueeze(2)
                                        .to_broadcast([P, FTILES, EXPERTS]), tiles_by(e_tab[:, 1, 0:EXPERTS]), ALU.is_ge))
                    c(dve.tensor_reduce(te_f[:, :], te[:, :, 0:EXPERTS - 1], AX.X, ALU.add))
                    c(dve.tensor_copy(tile_expert[:, :], te_f[:, :]))
                    c(dve.tensor_tensor(te[:, :, :], te[:, :, :], tiles_by(e_tab[:, 2, 0:EXPERTS]), ALU.mult))
                    c(dve.tensor_reduce(te_f[:, :], te[:, :, :], AX.X, ALU.add))
                    c(dve.scalar_tensor_tensor(tile_row[:, :], iota_row[:, 0:FTILES], float(P), te_f[:, :],
                                               ALU.mult, ALU.add))
                    by_pair = lambda ap: ap.unsqueeze(1).unsqueeze(1).to_broadcast([P, 2, WINDOWS, EXPERTS])
                    c(dve.tensor_scalar(region[:, :], region[:, :], float(REGION), None, ALU.add))
                    c(dve.tensor_tensor(past, pos_all[:, :, :].unsqueeze(3).to_broadcast([P, 2, WINDOWS, EXPERTS]),
                                        by_pair(region[:, :]), ALU.is_ge))
                    c(dve.tensor_tensor(past, past, by_pair(e_tab[:, 2, 0:EXPERTS]), ALU.mult))
                    c(dve.tensor_reduce(soft[:, 1:3, :], past, AX.X, ALU.add))
                    c(dve.tensor_tensor(pos_k[:, :, :], pos_all[:, :, :], soft[:, 1:3, :], ALU.subtract))
                    dve.wait_ge(exp_out, 1)
                    c(dve.tensor_scalar(soft[:, 2, :], ratio[:, :], 1.0, None, ALU.add))
                    c(dve.reciprocal(weight_k[:, 0, :], soft[:, 2, :]))
                    c(dve.tensor_tensor(weight_k[:, 1, :], ratio[:, :], weight_k[:, 0, :], ALU.mult))
                    dve.wait_ge(b1_up, EXPERTS)
                    c(dve.tensor_tensor(b1T[:, :], ps[:, 7, 0:EXPERTS * HC], param_cols[:, 0:EXPERTS * HC], ALU.add))

                @block.scalar
                def _(act):
                    act.sem_inc(xT3, 1)

                    def norm(g, s, use, last):
                        act.wait_ge(var3, g + 1)
                        act.activation(sd[:, s, :], mv3[:, s, :, 1], ACT.Sqrt, bias=eps2[:, :],
                                       scale=1.0 + EPS).then_inc(std3, 1)
                        act.wait_ge(scale3, g + 1)
                        act.wait_ge(rows_free, g + 1)
                        for j in range(GROUP):
                            rows = acc[:, bass.ds(g * GROUP + j, 1), :].rearrange("p a d -> p (a d)")
                            act.activation(xg[:, s, j, :], rows, ACT.Identity, scale=sc[:, s, 0, j:j + 1],
                                           bias=sc[:, s, 1, j:j + 1]).then_inc(normed, 1)
                        act.wait_ge(turned3, g + 1)
                        act.wait_ge(routed3, g + 1)
                        for k in range(KC):
                            last_one = act.copy(xTg[:, k, :], psf[:, k * 1024:k * 1024 + GROUP * P])
                        last_one.then_inc(xT3, 1)

                    by_groups(act, norm, XG)
                    act.wait_ge(soft_in, 1)
                    act.activation(ratio[:, :], soft[:, 0, :], ACT.Exp).then_inc(exp_out, 1)
                    for e in range(EXPERTS):
                        act.wait_ge(b1_up, e + 1)
                        for k in range(KC):
                            at = w1_sb[:, (e * KC + k) * H:(e * KC + k + 1) * H]
                            act.activation(at, at, ACT.Copy, scale=gamma_col[:, k:k + 1])

                @block.tensor
                def _(pe):
                    pe.sem_inc(routed3, 1)
                    pe.transpose(ps[:, 7, 0:RPAR], param_rows[:, :], ident[0:RPAR, 0:RPAR]).then_inc(weights_turned, 1)
                    pe.wait_ge(param_kept, 1)
                    for k in range(KC):
                        last_one = pe.matmul(ps[:, 6, 0:EXPERTS], beta_wide[:, k, :], Wr_sb[:, k, :],
                                             start=(k == 0), stop=(k == KC - 1))
                    last_one.then_inc(beta_up, 1)

                    def turn(g, s):
                        pe.wait_ge(xT3, g + 1)
                        for j in range(GROUP):
                            pe.wait_ge(normed, g * GROUP + j + 1)
                            for k in range(KC):
                                last_one = pe.transpose(psf[:, k * 1024 + j * P:k * 1024 + (j + 1) * P],
                                                        xg[:, s, j, k * P:(k + 1) * P], ident[:, :])
                        last_one.then_inc(turned3, 1)

                    def count(g, s, use, last):
                        pe.wait_ge(xT3, g + 2)
                        pe.wait_ge(logits3, g + 1)
                        for j in range(GROUP):
                            for k in range(KC):
                                last_one = pe.matmul(ps[:, 4, j * EXPERTS:(j + 1) * EXPERTS],
                                                     xTg[:, k, j * P:(j + 1) * P], Wr_scaled[:, k, :],
                                                     start=(k == 0), stop=(k == KC - 1))
                        last_one.then_inc(routed3, 1)
                        if not last:
                            turn(g + 1, (s + 1) % XG)
                        pe.wait_ge(both_ready, g + 1)
                        pe.matmul(ps[:, 5, 0:(GROUP + 1) * EXPERTS], before[:, :],
                                  both[:, :, :].rearrange("p w e -> p (w e)"), start=True, stop=False,
                                  skip_group_check=True)
                        for j in range(GROUP):
                            later = GROUP - j
                            last_one = pe.matmul(ps[:, 5, (j + 1) * EXPERTS:(GROUP + 1) * EXPERTS], ones[:, :],
                                                 both[:, j:j + 1, :].to_broadcast([P, later, EXPERTS]),
                                                 start=False, stop=(j == GROUP - 1), skip_group_check=True)
                        last_one.then_inc(counts_up, 1)

                    turn(0, 0)
                    by_groups(pe, count, XG)
                    for e in range(EXPERTS):
                        for h in range(HC):
                            for k in range(KC):
                                at = (e * KC + k) * H + h * P
                                last_one = pe.matmul(ps[:, 7, e * HC + h:e * HC + h + 1], w1_sb[:, at:at + P],
                                                     beta_col[:, k:k + 1], start=(k == 0), stop=(k == KC - 1))
                        last_one.then_inc(b1_up, 1)

                @block.gpsimd
                def _(pool):
                    pool.sem_inc(gated3, 1)

                    def send(g, s, use, last):
                        pool.wait_ge(rows_ready, g + 1)
                        pool.wait_ge(gated3, g + 1)
                        nc.gpsimd.tensor_tensor(gate[:, 3:4], ones[:, 0:1], ones[:, 1:2], ALU.add).then_inc(gated3, 1)
                        for j in range(GROUP):
                            for k in range(2):
                                nc.gpsimd.indirect_dma_start(
                                    xs_dram, bass.IndirectOffsetOnAxis(ap=pos_slot[:, s, k, j:j + 1], axis=0),
                                    xg[:, s, j, :], None).then_inc(sent[s], 16)

                    by_groups(pool, send, XG)

        with ExitStack() as c4:
            def sb4(name, shape, dt=F32):
                return c4.enter_context(nc.sbuf_tensor(name, shape, dt))

            def sem4(name):
                return c4.enter_context(nc.semaphore(name))

            XS = 3
            UNROLL = 6
            assert (FTILES - 4) % UNROLL == 0 and UNROLL % XS == 0 and UNROLL % 2 == 0
            xrow = sb4("xrow", [P, XS, D])
            xTt = sb4("xTt", [P, 2, KC, P])
            w1_now = sb4("w1_now", [P, 2, KC, H])
            hidT = sb4("hidT", [P, 2, HC, P])
            yrow = sb4("yrow", [P, 2, D])
            x_in4, x_turned4, xT4 = [sem4(f"x_in4_{s}") for s in range(XS)], sem4("x_turned4"), sem4("xT4")
            w1_ready, hid_up, act_done = sem4("w1_ready"), sem4("hid_up"), sem4("act_done")
            y_up, y_down, y_out = sem4("y_up"), sem4("y_down"), [sem4(f"y_out{s}") for s in range(2)]
            y_free = sem4("y_free")

            def tiles(engine, stages, of_experts=True, of_rows=False):
                behind_most = 2
                per_slot = UNROLL // XS

                def load_tables(first, count):
                    experts = (value(engine, tile_expert[0:1, bass.ds(first, count)], EXPERTS - 1) if of_experts
                               else [None] * count)
                    rows = (value(engine, tile_row[0:1, bass.ds(first, count)], SLOT_ROWS - P) if of_rows
                            else [None] * count)
                    return [(experts[v], rows[v]) for v in range(count)]

                entries = load_tables(0, 2)
                for front in range(behind_most):
                    for behind, stage in stages:
                        n = front - behind
                        if n >= 0:
                            stage(n, n % UNROLL, n // XS + 1, *entries[n])
                with engine.Fori(0, (FTILES - 4) // UNROLL) as i:
                    entries = load_tables(i * UNROLL, UNROLL + 2)
                    for u in range(UNROLL):
                        for behind, stage in stages:
                            v = u + behind_most - behind
                            stage(i * UNROLL + v, v % UNROLL, i * per_slot + v // XS + 1, *entries[v])
                entries = load_tables(FTILES - 4, 4)
                for front in range(FTILES - 2, FTILES + behind_most):
                    for behind, stage in stages:
                        n = front - behind
                        if n < FTILES:
                            stage(n, n % UNROLL, n // XS + 1, *entries[n - (FTILES - 4)])

            with nc.Block() as block:
                @block.sync
                def _(sp):
                    def load(n, u, use, _, row):
                        sp.wait_ge(x_turned4, n + 1)
                        sp.dma_start(xrow[:, u % XS, :], xs_dram[bass.ds(row, P), :]).then_inc(x_in4[u % XS], 16)

                    tiles(sp, [(0, load)], of_experts=False, of_rows=True)

                @block.gpsimd
                def _(pool):
                    pool.sem_inc(y_free, 2)
                    with pool.Fori(0, FTILES // 2) as i:
                        for s in range(2):
                            pool.wait_ge(y_out[s], (i + 1) * 16)
                            pool.sem_inc(y_free, 1)

                @block.scalar
                def _(act):
                    act.sem_inc(act_done, 2)

                    def gelu(n, u, use, expert, _):
                        s = u % 2
                        act.wait_ge(hid_up, n + 3)
                        act.wait_ge(y_up, n + 1)
                        for k in range(HC):
                            last = act.activation(hidT[:, s, k, :], ps[:, 2 + s, k * P:(k + 1) * P], ACT.Gelu,
                                                  bias=b1T[:, bass.ds(expert * HC + k, 1)])
                        last.then_inc(act_done, 1)

                    def store(n, u, use, _, row):
                        act.wait_ge(y_down, n + 3)
                        act.dma_start(ys_dram[bass.ds(n * P, P), :], yrow[:, u % 2, :]).then_inc(y_out[u % 2], 16)

                    tiles(act, [(1, gelu), (2, store)])

                @block.vector
                def _(dve):
                    dve.sem_inc(xT4, 2)
                    dve.sem_inc(y_down, 2)

                    def keep_rows(n, u, use, _, row):
                        dve.wait_ge(x_turned4, n + XS + 1)
                        dve.wait_ge(hid_up, n + 1)
                        dve.tensor_copy(xTt[:, u % 2].rearrange("p c n -> p (c n)"),
                                        ps[:, u % 2, 0:KC * P]).then_inc(xT4, 1)

                    def place_w1(n, u, use, expert, _):
                        at = w1_sb[:, bass.ds(expert * (KC * H), KC * H)]
                        dve.tensor_copy(w1_now[:, u % 2].rearrange("p c h -> p (c h)"), at).then_inc(w1_ready, 1)

                    def finish(n, u, use, expert, _):
                        dve.wait_ge(y_up, n + 3)
                        dve.wait_ge(y_free, n + 1)
                        dve.tensor_tensor(yrow[:, u % 2, :], ps[:, 6 + u % 2, 0:D],
                                          b2_b[:, bass.ds(expert, 1), :].rearrange("p a d -> p (a d)"),
                                          ALU.add).then_inc(y_down, 1)

                    tiles(dve, [(0, keep_rows), (0, place_w1), (2, finish)])

                @block.tensor
                def _(pe):
                    pe.sem_inc(x_turned4, XS)
                    pe.sem_inc(hid_up, 2)
                    pe.sem_inc(y_up, 2)

                    def turn_rows(n, u, use, _, row):
                        pe.wait_ge(x_in4[u % XS], use * 16)
                        pe.wait_ge(xT4, n + 1)
                        for k in range(KC):
                            last = pe.transpose(ps[:, u % 2, k * P:(k + 1) * P], xrow[:, u % XS, k * P:(k + 1) * P],
                                                ident[:, :])
                        last.then_inc(x_turned4, 1)

                    def into_hidden(n, u, use, expert, _):
                        pe.wait_ge(xT4, n + 3)
                        pe.wait_ge(w1_ready, n + 1)
                        pe.wait_ge(act_done, n + 1)
                        for h in range(HC):
                            for k in range(KC):
                                last = pe.matmul(ps[:, 2 + u % 2, h * P:(h + 1) * P],
                                                 w1_now[:, u % 2, k, h * P:(h + 1) * P], xTt[:, u % 2, k, :],
                                                 start=(k == 0), stop=(k == KC - 1))
                        last.then_inc(hid_up, 1)

                    def out_of_hidden(n, u, use, expert, _):
                        pe.wait_ge(act_done, n + 3)
                        pe.wait_ge(y_down, n + 1)
                        for k in range(HC):
                            last = pe.matmul(ps[:, 6 + u % 2, 0:D], hidT[:, u % 2, k, :],
                                             w2_sb[:, bass.ds(expert * (HC * D) + k * D, D)],
                                             start=(k == 0), stop=(k == HC - 1))
                        last.then_inc(y_up, 1)

                    tiles(pe, [(0, turn_rows), (1, into_hidden), (2, out_of_hidden)])

        with ExitStack() as c5:
            def sb5(name, shape, dt=F32):
                return c5.enter_context(nc.sbuf_tensor(name, shape, dt))

            def sem5(name):
                return c5.enter_context(nc.semaphore(name))

            y_got = big[:, 0:4 * GROUP * D].rearrange("p (s k j d) -> p s k j d", s=2, k=2, j=GROUP)
            pos_now = sb5("pos_now", [P, 2, 2, GROUP], I32)
            slots5, gated5, added = sem5("slots5"), sem5("gated5"), sem5("added")
            got = [[sem5(f"got{s}{k}") for k in range(2)] for s in range(2)]
            stored, added_free = sem5("stored"), sem5("added_free")
            with nc.Block() as block:
                @block.vector
                def _(dve):
                    dve.tensor_copy(pos_now[:, 0], pos_k[:, :, 0:GROUP]).then_inc(slots5, 1)

                    def combine(g, s, use, last):
                        if not last:
                            dve.tensor_copy(pos_now[:, 1 - s], pos_k[:, :, bass.ds(g * GROUP + GROUP, GROUP)]
                                            ).then_inc(slots5, 1)
                        for k in range(2):
                            dve.wait_ge(got[s][k], use * (GROUP * 16))
                            for j in range(GROUP):
                                at = acc[:, bass.ds(g * GROUP + j, 1), :].rearrange("p a d -> p (a d)")
                                if k == 1:
                                    dve.wait_ge(added, g * (2 * GROUP) + j + 1)
                                dve.scalar_tensor_tensor(at, y_got[:, s, k, j, :],
                                                         weight_k[:, k, bass.ds(g * GROUP + j, 1)], at,
                                                         ALU.mult, ALU.add).then_inc(added, 1)
                        dve.wait_ge(added, (g + 1) * (2 * GROUP))
                        dve.sem_inc(added_free, 1)

                    by_groups(dve, combine, 2)

                @block.gpsimd
                def _(pool):
                    pool.sem_inc(gated5, 1)
                    pool.sem_inc(added_free, 2)

                    def gather(g, s, use, last):
                        pool.wait_ge(slots5, g + 1)
                        pool.wait_ge(added_free, g + 1)
                        pool.wait_ge(gated5, g + 1)
                        nc.gpsimd.tensor_tensor(gate[:, 3:4], ones[:, 0:1], ones[:, 1:2], ALU.add).then_inc(gated5, 1)
                        for k in range(2):
                            for j in range(GROUP):
                                nc.gpsimd.indirect_dma_start(
                                    y_got[:, s, k, j, :], None, ys_dram,
                                    bass.IndirectOffsetOnAxis(ap=pos_now[:, s, k, j:j + 1], axis=0)
                                ).then_inc(got[s][k], 16)

                    by_groups(pool, gather, 2)

                @block.sync
                def _(sp):
                    with sp.Fori(0, GROUPS - 1) as g:
                        sp.wait_ge(added, (g + 1) * (2 * GROUP))
                        sp.dma_start(out[bass.ds(g * (GROUP * P), GROUP * P), :].rearrange("(w p) d -> p w d", p=P),
                                     acc[:, bass.ds(g * GROUP, GROUP), :]).then_inc(stored, 16)
                    for w in range((GROUPS - 1) * GROUP, WINDOWS):
                        rows = P if w < WINDOWS - 1 else TAIL
                        sp.wait_ge(added, w + (GROUPS * GROUP) + 1)
                        sp.dma_start(out[w * P:w * P + rows, :], acc[0:rows, w, :]).then_inc(stored, 16)
                    sp.wait_ge(stored, (GROUPS - 1 + GROUP) * 16)


_INS = ['x', 'src', 'dst', 'edge_weight', 'L0_gnn_node_lock', 'L0_gnn_W', 'L0_gnn_b', 'L0_ffn_gamma', 'L0_ffn_beta',
        'L0_ffn_Wr', 'L0_ffn_br', 'L0_ffn_W1', 'L0_ffn_b1', 'L0_ffn_W2', 'L0_ffn_b2']


def kernel(**inputs):
    import numpy as _np
    import concourse.bacc as _bacc
    from concourse import mybir as _mybir
    from concourse.bass_utils import run_bass_kernel_spmd as _run

    nc = _bacc.Bacc("TRN2", target_bir_lowering=False, num_devices=1)
    arrays, args = {}, []
    for name in _INS:
        a = _np.ascontiguousarray(inputs[name])
        arrays[f"in_{name}_dram"] = a
        args.append(nc.dram_tensor(f"in_{name}_dram", a.shape, _mybir.dt.from_np(a.dtype), kind="ExternalInput").ap())
    args.append(nc.dram_tensor("out_0_dram", inputs['x'].shape, _mybir.dt.float32, kind="ExternalOutput").ap())
    gnn_moe_kernel(nc, *args)
    r = _run(nc, [arrays], core_ids=[0])
    return r.results[0]["out_0_dram"]
```
